# Optimizing a Trainium2 kernel written in Bass

```python
import numpy as np
import jax
import jax.numpy as jnp

def _softmax(x, axis=-1):
    return jax.nn.softmax(x, axis=axis)

def _gelu(x):
    return jax.nn.gelu(x, approximate=True)

def _silu(x):
    return jax.nn.silu(x)

def _sigmoid(x):
    return jax.nn.sigmoid(x)

def _layernorm(x, axis=-1, eps=1e-05):
    m = jnp.mean(x, axis=axis, keepdims=True)
    v = jnp.var(x, axis=axis, keepdims=True)
    return (x - m) / jnp.sqrt(v + eps)

def _scatter_add(tgt, idx, src, axis=0):
    return tgt.at[idx].add(src)

def _segment_sum(src, seg, n):
    return jax.ops.segment_sum(src, seg, n)
kernel_name = 'mk_vit_tower_cls_d4_tok_img768_r4_e8e918'

def setup_inputs(seed: int=0):
    np.random.seed(seed)
    _w = jnp.asarray

    def _rec_inputs():
        import jax
        import jax.numpy as jnp
        _rk = jax.random.key(seed)
        x = -0.000222058 + 0.999998 * jax.random.normal(jax.random.fold_in(_rk, 1), (16, 128, 192, 1), jnp.float32)
        cls_tok = 0.02 * jax.random.normal(jax.random.fold_in(_rk, 5), (1, 1, 192), jnp.float32)
        return (x, cls_tok)
    x, cls_tok = _rec_inputs()

    def _L0_tok_setup():
        import jax, jax.numpy as jnp
        from jax import lax
        import numpy as np
        DIM = 192
        K = 7
        PAD = K // 2
        EPS = 1e-06
        key = jax.random.key(seed)
        ks = jax.random.split(key, 6)
        B, L = (64, 128)
        x = jax.random.normal(ks[0], (B, L, DIM, 1), dtype=jnp.float32)
        fan_dw = 1 * K * 1
        dw_w = jax.random.uniform(ks[1], (DIM, 1, K, 1), jnp.float32, -1.0 / np.sqrt(fan_dw), 1.0 / np.sqrt(fan_dw))
        fan_pw = DIM
        pw_w = jax.random.uniform(ks[2], (DIM, DIM), jnp.float32, -1.0 / np.sqrt(fan_pw), 1.0 / np.sqrt(fan_pw))
        pw_b = jax.random.uniform(ks[3], (DIM,), jnp.float32, -1.0 / np.sqrt(fan_pw), 1.0 / np.sqrt(fan_pw))
        ln_g = jnp.ones((DIM,), jnp.float32)
        ln_b = jnp.zeros((DIM,), jnp.float32)
        return {'x': x, 'dw_w': dw_w, 'pw_w': pw_w, 'pw_b': pw_b, 'ln_g': ln_g, 'ln_b': ln_b}
    _L0_tok_all = _L0_tok_setup()
    _L0_tok_in = {k: v for k, v in _L0_tok_all.items() if k in ('dw_w', 'pw_w', 'pw_b', 'ln_g', 'ln_b')}
    del _L0_tok_all

    def _L0_attn_setup():
        import jax, jax.numpy as jnp
        import numpy as np
        B, N, C = (32, 256, 192)
        H = 12
        E = C // H
        SCALE = E ** (-0.5)
        EPS = 1e-06
        key = jax.random.key(seed)
        k1, k2, k3 = jax.random.split(key, 3)
        x = jax.random.normal(k1, (B, N, C), dtype=jnp.float32)
        qkv_w = jax.random.normal(k2, (3 * C, C), dtype=jnp.float32) * C ** (-0.5)
        proj_w = jax.random.normal(k3, (C, C), dtype=jnp.float32) * C ** (-0.5)
        proj_b = jnp.zeros((C,), dtype=jnp.float32)
        return {'x': x, 'qkv_w': qkv_w, 'proj_w': proj_w, 'proj_b': proj_b}
    _L0_attn_all = _L0_attn_setup()
    _L0_attn_in = {k: v for k, v in _L0_attn_all.items() if k in ('qkv_w', 'proj_w', 'proj_b')}
    del _L0_attn_all

    def _L0_ffn_setup():
        import jax, jax.numpy as jnp
        import numpy as np
        DIM = 192
        HID = 128
        E = 16
        G = 8
        TOPK_G = 4
        TOPK_E = 4
        SCALE = 2.5
        B, S = (2, 512)
        key = jax.random.key(seed)
        ks = jax.random.split(key, 9)
        init = lambda k, shape: jax.random.normal(k, shape, dtype=jnp.float32) * 0.02
        z = lambda shape: jnp.zeros(shape, jnp.float32)
        return {'x': jax.random.normal(ks[0], (B, S, DIM), dtype=jnp.float32), 'gate_w': init(ks[1], (DIM, E)), 'gate_b': z((E,)), 'bias': z((E,)), 'Wu': init(ks[2], (E, DIM, HID)), 'bu': z((E, HID)), 'Wg': init(ks[3], (E, DIM, HID)), 'bg': z((E, HID)), 'Wd': init(ks[4], (E, HID, DIM)), 'bd': z((E, DIM)), 'sWu': init(ks[5], (DIM, HID)), 'sbu': z((HID,)), 'sWg': init(ks[6], (DIM, HID)), 'sbg': z((HID,)), 'sWd': init(ks[7], (HID, DIM)), 'sbd': z((DIM,))}
    _L0_ffn_all = _L0_ffn_setup()
    _L0_ffn_in = {k: v for k, v in _L0_ffn_all.items() if k in ('gate_w', 'gate_b', 'bias', 'Wu', 'bu', 'Wg', 'bg', 'Wd', 'bd', 'sWu', 'sbu', 'sWg', 'sbg', 'sWd', 'sbd')}
    del _L0_ffn_all

    def _L1_attn_setup():
        import jax, jax.numpy as jnp
        import numpy as np
        D_MODEL = 192
        EXPAND = 2
        D_INNER = EXPAND * D_MODEL
        D_STATE = 16
        D_CONV = 4
        DT_RANK = (D_MODEL + 15) // 16
        BATCH, SEQ = (8, 512)
        EPS = 1e-12

        def _silu(x):
            return x * jax.nn.sigmoid(x)

        def _mamba(x, in_w, conv_w, conv_b, xproj_w, dt_w, dt_b, A_log, D_skip, out_w):
            B, L, _ = x.shape
            xz = x @ in_w.T
            u, z = jnp.split(xz, 2, axis=-1)
            pad = jnp.pad(u, ((0, 0), (D_CONV - 1, 0), (0, 0)))
            uc = conv_b + sum((pad[:, k:k + L, :] * conv_w[:, k] for k in range(D_CONV)))
            uc = _silu(uc)
            x_dbl = uc @ xproj_w.T
            dt, Bm, Cm = jnp.split(x_dbl, [DT_RANK, DT_RANK + D_STATE], axis=-1)
            dt = jax.nn.softplus(dt @ dt_w.T + dt_b)
            A = -jnp.exp(A_log)

            def step(h, t):
                dt_t, B_t, C_t, u_t = t
                dA = jnp.exp(dt_t[:, :, None] * A)
                h = dA * h + (dt_t * u_t)[:, :, None] * B_t[:, None, :]
                y = jnp.einsum('bdn,bn->bd', h, C_t)
                return (h, y)
            xs = (dt.swapaxes(0, 1), Bm.swapaxes(0, 1), Cm.swapaxes(0, 1), uc.swapaxes(0, 1))
            h0 = jnp.zeros((B, D_INNER, D_STATE), x.dtype)
            _, ys = jax.lax.scan(step, h0, xs)
            y = ys.swapaxes(0, 1) + uc * D_skip
            return y * _silu(z) @ out_w.T

        def _mamba_params(key):
            ks = jax.random.split(key, 8)
            return dict(in_w=jax.random.normal(ks[0], (2 * D_INNER, D_MODEL), jnp.float32) * 0.02, conv_w=jax.random.normal(ks[1], (D_INNER, D_CONV), jnp.float32) * 0.2, conv_b=jnp.zeros((D_INNER,), jnp.float32), xproj_w=jax.random.normal(ks[2], (DT_RANK + 2 * D_STATE, D_INNER), jnp.float32) * 0.02, dt_w=jax.random.normal(ks[3], (D_INNER, DT_RANK), jnp.float32) * 0.02, dt_b=jax.random.normal(ks[4], (D_INNER,), jnp.float32) * 0.02, A_log=jnp.log(jnp.tile(jnp.arange(1, D_STATE + 1, dtype=jnp.float32), (D_INNER, 1))), D_skip=jnp.ones((D_INNER,), jnp.float32), out_w=jax.random.normal(ks[5], (D_MODEL, D_INNER), jnp.float32) * 0.02)
        key = jax.random.key(seed)
        k0, k1, k2 = jax.random.split(key, 3)
        inp = {'hidden_states': jax.random.normal(k0, (BATCH, SEQ, D_MODEL), jnp.float32)}
        for pref, k in (('f_', k1), ('b_', k2)):
            for name, v in _mamba_params(k).items():
                inp[pref + name] = v
        inp['ln_g'] = jnp.ones((D_MODEL,), jnp.float32)
        inp['ln_b'] = jnp.zeros((D_MODEL,), jnp.float32)
        return inp
    _L1_attn_all = _L1_attn_setup()
    _L1_attn_in = {k: v for k, v in _L1_attn_all.items() if k in ('f_in_w', 'f_conv_w', 'f_conv_b', 'f_xproj_w', 'f_dt_w', 'f_dt_b', 'f_A_log', 'f_D_skip', 'f_out_w', 'b_in_w', 'b_conv_w', 'b_conv_b', 'b_xproj_w', 'b_dt_w', 'b_dt_b', 'b_A_log', 'b_D_skip', 'b_out_w', 'ln_g', 'ln_b')}
    del _L1_attn_all

    def _L1_ffn_setup():
        import jax, jax.numpy as jnp
        import numpy as np
        QN, QP = (-8, 7)

        def round_pass(x):
            return x + jax.lax.stop_gradient(jnp.round(x) - x)

        def _quant_act(x, alpha_a):
            a = alpha_a.mean()
            return round_pass(jnp.clip(x / a, QN, QP))

        def _quant_w(w, alpha_w):
            return round_pass(jnp.clip(w / alpha_w[:, None], QN, QP))
        key = jax.random.key(seed)
        ks = jax.random.split(key, 9)
        B, S, D, H = (16, 256, 192, 768)

        def unif(k, shape):
            return jax.random.uniform(k, shape, jnp.float32, 0.02, 0.1)
        return {'x0': jax.random.normal(ks[0], (B, S, D), jnp.float32), 'w1': jax.random.normal(ks[1], (H, D), jnp.float32) * 0.02, 'b1': jax.random.normal(ks[2], (H,), jnp.float32) * 0.02, 'alpha_w1': unif(ks[3], (H,)), 'alpha_a1': unif(ks[4], (D,)), 'w2': jax.random.normal(ks[5], (D, H), jnp.float32) * 0.02, 'b2': jax.random.normal(ks[6], (D,), jnp.float32) * 0.02, 'alpha_w2': unif(ks[7], (D,)), 'alpha_a2': unif(ks[8], (H,))}
    _L1_ffn_all = _L1_ffn_setup()
    _L1_ffn_in = {k: v for k, v in _L1_ffn_all.items() if k in ('w1', 'b1', 'alpha_w1', 'alpha_a1', 'w2', 'b2', 'alpha_w2', 'alpha_a2')}
    del _L1_ffn_all

    def _L2_attn_setup():
        import jax, jax.numpy as jnp
        import numpy as np
        DIM = 192
        GP_NUM = 49
        key = jax.random.key(seed)
        ks = jax.random.split(key, 7)
        b, n, d = (16, 256, DIM)
        s = d ** (-0.5)
        x = jax.random.normal(ks[0], (b, n, d), dtype=jnp.float32)
        W_qkv = jax.random.normal(ks[1], (d, 3 * d), dtype=jnp.float32) * s
        b_qkv = jnp.zeros((3 * d,), dtype=jnp.float32)
        W_proj = jax.random.normal(ks[2], (d, d), dtype=jnp.float32) * s
        b_proj = jnp.zeros((d,), dtype=jnp.float32)
        W_gp = jax.random.normal(ks[3], (d, GP_NUM), dtype=jnp.float32) * s
        alpha = jnp.zeros((1,), dtype=jnp.float32)
        return {'x': x, 'W_qkv': W_qkv, 'b_qkv': b_qkv, 'W_proj': W_proj, 'b_proj': b_proj, 'W_gp': W_gp, 'alpha': alpha}
    _L2_attn_all = _L2_attn_setup()
    _L2_attn_in = {k: v for k, v in _L2_attn_all.items() if k in ('W_qkv', 'b_qkv', 'W_proj', 'b_proj', 'W_gp', 'alpha')}
    del _L2_attn_all

    def _L2_ffn_setup():
        import jax, jax.numpy as jnp
        import numpy as np
        B, S, D = (4, 256, 192)
        E = 8
        H = 192
        HS = 768
        TOPK_ROUTED = 2
        key = jax.random.key(seed)
        ks = jax.random.split(key, 10)
        w = lambda k, shape: jax.random.normal(k, shape, dtype=jnp.float32) * 0.02
        return {'x': jax.random.normal(ks[0], (B, S, D), dtype=jnp.float32), 'router_w': w(ks[1], (D, E)), 'w_gate': w(ks[2], (E, D, H)), 'w_up': w(ks[3], (E, D, H)), 'w_down': w(ks[4], (E, H, D)), 'ws_gate': w(ks[5], (D, HS)), 'ws_up': w(ks[6], (D, HS)), 'ws_down': w(ks[7], (HS, D)), 'sg_w': w(ks[8], (D, 1)), 'sg_b': jnp.zeros((1,), jnp.float32)}
    _L2_ffn_all = _L2_ffn_setup()
    _L2_ffn_in = {k: v for k, v in _L2_ffn_all.items() if k in ('router_w', 'w_gate', 'w_up', 'w_down', 'ws_gate', 'ws_up', 'ws_down', 'sg_w', 'sg_b')}
    del _L2_ffn_all

    def _L3_attn_setup():
        import jax, jax.numpy as jnp
        import numpy as np
        DIM = 192
        ALL_KEY_DIM = 192
        NUM_HEADS = 12
        HEAD_DIM = DIM // NUM_HEADS
        SCALE = HEAD_DIM ** (-0.5)
        key = jax.random.key(seed)
        ks = jax.random.split(key, 8)
        B, N = (8, 256)
        s = 0.02
        return {'x': jax.random.normal(ks[0], (B, N, DIM), dtype=jnp.float32), 'Wq': jax.random.normal(ks[1], (ALL_KEY_DIM, DIM), dtype=jnp.float32) * s, 'Wk': jax.random.normal(ks[2], (ALL_KEY_DIM, DIM), dtype=jnp.float32) * s, 'Wv': jax.random.normal(ks[3], (DIM, DIM), dtype=jnp.float32) * s, 'bv': jnp.zeros((DIM,), dtype=jnp.float32), 'Wmix': jax.random.normal(ks[4], (NUM_HEADS, ALL_KEY_DIM), dtype=jnp.float32) * s, 'Wcb': jax.random.normal(ks[5], (NUM_HEADS, DIM), dtype=jnp.float32) * s, 'Wproj': jax.random.normal(ks[6], (DIM, DIM), dtype=jnp.float32) * s, 'bproj': jnp.zeros((DIM,), dtype=jnp.float32)}
    _L3_attn_all = _L3_attn_setup()
    _L3_attn_in = {k: v for k, v in _L3_attn_all.items() if k in ('Wq', 'Wk', 'Wv', 'bv', 'Wmix', 'Wcb', 'Wproj', 'bproj')}
    del _L3_attn_all

    def _L3_ffn_setup():
        import jax, jax.numpy as jnp
        import numpy as np
        NUM_EXPERTS = 8
        TOP_K = 2
        CAP_FACTOR = 1.0
        D_MODEL = 192
        D_FF = 768
        key = jax.random.key(seed)
        k0, k1, k2, k3 = jax.random.split(key, 4)
        B, S, D = (1, 512, D_MODEL)
        inputs = jax.random.normal(k0, (B, S, D), dtype=jnp.float32)
        router_w = jax.random.normal(k1, (NUM_EXPERTS, D), dtype=jnp.float32) * D ** (-0.5)
        w1 = jax.random.normal(k2, (NUM_EXPERTS, D, D_FF), dtype=jnp.float32) * D ** (-0.5)
        w2 = jax.random.normal(k3, (NUM_EXPERTS, D_FF, D), dtype=jnp.float32) * D_FF ** (-0.5)
        return {'inputs': inputs, 'router_w': router_w, 'w1': w1, 'w2': w2}
    _L3_ffn_all = _L3_ffn_setup()
    _L3_ffn_in = {k: v for k, v in _L3_ffn_all.items() if k in ('router_w', 'w1', 'w2')}
    del _L3_ffn_all
    return {'x': x, 'cls_tok': cls_tok, 'L0_tok_dw_w': _L0_tok_in['dw_w'], 'L0_tok_pw_w': _L0_tok_in['pw_w'], 'L0_tok_pw_b': _L0_tok_in['pw_b'], 'L0_tok_ln_g': _L0_tok_in['ln_g'], 'L0_tok_ln_b': _L0_tok_in['ln_b'], 'L0_attn_qkv_w': _L0_attn_in['qkv_w'], 'L0_attn_proj_w': _L0_attn_in['proj_w'], 'L0_attn_proj_b': _L0_attn_in['proj_b'], 'L0_ffn_gate_w': _L0_ffn_in['gate_w'], 'L0_ffn_gate_b': _L0_ffn_in['gate_b'], 'L0_ffn_bias': _L0_ffn_in['bias'], 'L0_ffn_Wu': _L0_ffn_in['Wu'], 'L0_ffn_bu': _L0_ffn_in['bu'], 'L0_ffn_Wg': _L0_ffn_in['Wg'], 'L0_ffn_bg': _L0_ffn_in['bg'], 'L0_ffn_Wd': _L0_ffn_in['Wd'], 'L0_ffn_bd': _L0_ffn_in['bd'], 'L0_ffn_sWu': _L0_ffn_in['sWu'], 'L0_ffn_sbu': _L0_ffn_in['sbu'], 'L0_ffn_sWg': _L0_ffn_in['sWg'], 'L0_ffn_sbg': _L0_ffn_in['sbg'], 'L0_ffn_sWd': _L0_ffn_in['sWd'], 'L0_ffn_sbd': _L0_ffn_in['sbd'], 'L1_attn_f_in_w': _L1_attn_in['f_in_w'], 'L1_attn_f_conv_w': _L1_attn_in['f_conv_w'], 'L1_attn_f_conv_b': _L1_attn_in['f_conv_b'], 'L1_attn_f_xproj_w': _L1_attn_in['f_xproj_w'], 'L1_attn_f_dt_w': _L1_attn_in['f_dt_w'], 'L1_attn_f_dt_b': _L1_attn_in['f_dt_b'], 'L1_attn_f_A_log': _L1_attn_in['f_A_log'], 'L1_attn_f_D_skip': _L1_attn_in['f_D_skip'], 'L1_attn_f_out_w': _L1_attn_in['f_out_w'], 'L1_attn_b_in_w': _L1_attn_in['b_in_w'], 'L1_attn_b_conv_w': _L1_attn_in['b_conv_w'], 'L1_attn_b_conv_b': _L1_attn_in['b_conv_b'], 'L1_attn_b_xproj_w': _L1_attn_in['b_xproj_w'], 'L1_attn_b_dt_w': _L1_attn_in['b_dt_w'], 'L1_attn_b_dt_b': _L1_attn_in['b_dt_b'], 'L1_attn_b_A_log': _L1_attn_in['b_A_log'], 'L1_attn_b_D_skip': _L1_attn_in['b_D_skip'], 'L1_attn_b_out_w': _L1_attn_in['b_out_w'], 'L1_attn_ln_g': _L1_attn_in['ln_g'], 'L1_attn_ln_b': _L1_attn_in['ln_b'], 'L1_ffn_w1': _L1_ffn_in['w1'], 'L1_ffn_b1': _L1_ffn_in['b1'], 'L1_ffn_alpha_w1': _L1_ffn_in['alpha_w1'], 'L1_ffn_alpha_a1': _L1_ffn_in['alpha_a1'], 'L1_ffn_w2': _L1_ffn_in['w2'], 'L1_ffn_b2': _L1_ffn_in['b2'], 'L1_ffn_alpha_w2': _L1_ffn_in['alpha_w2'], 'L1_ffn_alpha_a2': _L1_ffn_in['alpha_a2'], 'L2_attn_W_qkv': _L2_attn_in['W_qkv'], 'L2_attn_b_qkv': _L2_attn_in['b_qkv'], 'L2_attn_W_proj': _L2_attn_in['W_proj'], 'L2_attn_b_proj': _L2_attn_in['b_proj'], 'L2_attn_W_gp': _L2_attn_in['W_gp'], 'L2_attn_alpha': _L2_attn_in['alpha'], 'L2_ffn_router_w': _L2_ffn_in['router_w'], 'L2_ffn_w_gate': _L2_ffn_in['w_gate'], 'L2_ffn_w_up': _L2_ffn_in['w_up'], 'L2_ffn_w_down': _L2_ffn_in['w_down'], 'L2_ffn_ws_gate': _L2_ffn_in['ws_gate'], 'L2_ffn_ws_up': _L2_ffn_in['ws_up'], 'L2_ffn_ws_down': _L2_ffn_in['ws_down'], 'L2_ffn_sg_w': _L2_ffn_in['sg_w'], 'L2_ffn_sg_b': _L2_ffn_in['sg_b'], 'L3_attn_Wq': _L3_attn_in['Wq'], 'L3_attn_Wk': _L3_attn_in['Wk'], 'L3_attn_Wv': _L3_attn_in['Wv'], 'L3_attn_bv': _L3_attn_in['bv'], 'L3_attn_Wmix': _L3_attn_in['Wmix'], 'L3_attn_Wcb': _L3_attn_in['Wcb'], 'L3_attn_Wproj': _L3_attn_in['Wproj'], 'L3_attn_bproj': _L3_attn_in['bproj'], 'L3_ffn_router_w': _L3_ffn_in['router_w'], 'L3_ffn_w1': _L3_ffn_in['w1'], 'L3_ffn_w2': _L3_ffn_in['w2']}

def reference(x, cls_tok, L0_tok_dw_w, L0_tok_pw_w, L0_tok_pw_b, L0_tok_ln_g, L0_tok_ln_b, L0_attn_qkv_w, L0_attn_proj_w, L0_attn_proj_b, L0_ffn_gate_w, L0_ffn_gate_b, L0_ffn_bias, L0_ffn_Wu, L0_ffn_bu, L0_ffn_Wg, L0_ffn_bg, L0_ffn_Wd, L0_ffn_bd, L0_ffn_sWu, L0_ffn_sbu, L0_ffn_sWg, L0_ffn_sbg, L0_ffn_sWd, L0_ffn_sbd, L1_attn_f_in_w, L1_attn_f_conv_w, L1_attn_f_conv_b, L1_attn_f_xproj_w, L1_attn_f_dt_w, L1_attn_f_dt_b, L1_attn_f_A_log, L1_attn_f_D_skip, L1_attn_f_out_w, L1_attn_b_in_w, L1_attn_b_conv_w, L1_attn_b_conv_b, L1_attn_b_xproj_w, L1_attn_b_dt_w, L1_attn_b_dt_b, L1_attn_b_A_log, L1_attn_b_D_skip, L1_attn_b_out_w, L1_attn_ln_g, L1_attn_ln_b, L1_ffn_w1, L1_ffn_b1, L1_ffn_alpha_w1, L1_ffn_alpha_a1, L1_ffn_w2, L1_ffn_b2, L1_ffn_alpha_w2, L1_ffn_alpha_a2, L2_attn_W_qkv, L2_attn_b_qkv, L2_attn_W_proj, L2_attn_b_proj, L2_attn_W_gp, L2_attn_alpha, L2_ffn_router_w, L2_ffn_w_gate, L2_ffn_w_up, L2_ffn_w_down, L2_ffn_ws_gate, L2_ffn_ws_up, L2_ffn_ws_down, L2_ffn_sg_w, L2_ffn_sg_b, L3_attn_Wq, L3_attn_Wk, L3_attn_Wv, L3_attn_bv, L3_attn_Wmix, L3_attn_Wcb, L3_attn_Wproj, L3_attn_bproj, L3_ffn_router_w, L3_ffn_w1, L3_ffn_w2):
    import jax
    import jax.numpy as jnp

    def _L0_tok_ref(x, dw_w, pw_w, pw_b, ln_g, ln_b):
        import jax, jax.numpy as jnp
        from jax import lax
        import numpy as np
        DIM = 192
        K = 7
        PAD = K // 2
        EPS = 1e-06
        h = jnp.transpose(x, (0, 2, 1, 3))
        h = lax.conv_general_dilated(h, dw_w, window_strides=(1, 1), padding=((PAD, PAD), (0, 0)), dimension_numbers=('NCHW', 'OIHW', 'NCHW'), feature_group_count=DIM)
        h = h[..., 0]
        y = jnp.einsum('bdl,ed->ble', h, pw_w) + pw_b
        mu = jnp.mean(y, axis=-1, keepdims=True)
        var = jnp.mean(jnp.square(y - mu), axis=-1, keepdims=True)
        y = (y - mu) * lax.rsqrt(var + EPS) * ln_g + ln_b
        return jax.nn.relu(y)

    def _L0_attn_ref(x, qkv_w, proj_w, proj_b):
        import jax, jax.numpy as jnp
        import numpy as np
        B, N, C = (32, 256, 192)
        H = 12
        E = C // H
        SCALE = E ** (-0.5)
        EPS = 1e-06
        b, n, c = x.shape
        qkv = jnp.einsum('bnc,dc->bnd', x, qkv_w).reshape(b, n, 3, H, E)
        q = qkv[:, :, 0]
        k = qkv[:, :, 1]
        v = qkv[:, :, 2]
        q_ = jax.nn.relu(q) + SCALE
        k_ = jax.nn.relu(k) + SCALE
        kv = jnp.einsum('bnhe,bnhd->bhed', k_, v)
        k_sum = jnp.sum(k_, axis=1)
        z = 1.0 / (jnp.einsum('bnhe,bhe->bnh', q_, k_sum) + EPS)
        out = jnp.einsum('bnhe,bhed->bnhd', q_, kv) * z[..., None]
        out = out.reshape(b, n, c)
        return jnp.einsum('bnc,dc->bnd', out, proj_w) + proj_b

    def _L0_ffn_ref(x, gate_w, gate_b, bias, Wu, bu, Wg, bg, Wd, bd, sWu, sbu, sWg, sbg, sWd, sbd):
        import jax, jax.numpy as jnp
        import numpy as np
        DIM = 192
        HID = 128
        E = 16
        G = 8
        TOPK_G = 4
        TOPK_E = 4
        SCALE = 2.5
        B, S = (2, 512)
        orig_shape = x.shape
        xt = x.reshape(-1, DIM)
        T = xt.shape[0]
        scores = jax.nn.softmax(xt @ gate_w + gate_b, axis=-1)
        orig_scores = jax.lax.stop_gradient(scores)
        s = scores + bias[None, :]
        s3 = s.reshape(T, G, E // G)
        group_scores = jax.lax.top_k(s3, 2)[0].sum(-1)
        gidx = jax.lax.top_k(group_scores, TOPK_G)[1]
        gmask = jnp.any(jnp.arange(G)[None, None, :] == gidx[:, :, None], axis=1)
        s_masked = jnp.where(gmask[:, :, None], s3, -jnp.inf).reshape(T, E)
        _, idx = jax.lax.top_k(s_masked, TOPK_E)
        w = jnp.take_along_axis(orig_scores, idx, axis=1) * SCALE
        w_full = jnp.zeros((T, E), xt.dtype).at[jnp.arange(T)[:, None], idx].add(w)
        up = jax.nn.silu(jnp.einsum('td,edh->teh', xt, Wu) + bu)
        gt = jnp.einsum('td,edh->teh', xt, Wg) + bg
        act = up * gt * w_full[:, :, None]
        y = jnp.einsum('teh,ehd->td', act, Wd) + w_full @ bd
        sh = jax.nn.silu(xt @ sWu + sbu) * (xt @ sWg + sbg)
        y = y + sh @ sWd + sbd
        return y.reshape(orig_shape)

    def _L1_attn_ref(hidden_states, f_in_w, f_conv_w, f_conv_b, f_xproj_w, f_dt_w, f_dt_b, f_A_log, f_D_skip, f_out_w, b_in_w, b_conv_w, b_conv_b, b_xproj_w, b_dt_w, b_dt_b, b_A_log, b_D_skip, b_out_w, ln_g, ln_b):
        import jax, jax.numpy as jnp
        import numpy as np
        D_MODEL = 192
        EXPAND = 2
        D_INNER = EXPAND * D_MODEL
        D_STATE = 16
        D_CONV = 4
        DT_RANK = (D_MODEL + 15) // 16
        BATCH, SEQ = (8, 512)
        EPS = 1e-12

        def _silu(x):
            return x * jax.nn.sigmoid(x)

        def _mamba(x, in_w, conv_w, conv_b, xproj_w, dt_w, dt_b, A_log, D_skip, out_w):
            B, L, _ = x.shape
            xz = x @ in_w.T
            u, z = jnp.split(xz, 2, axis=-1)
            pad = jnp.pad(u, ((0, 0), (D_CONV - 1, 0), (0, 0)))
            uc = conv_b + sum((pad[:, k:k + L, :] * conv_w[:, k] for k in range(D_CONV)))
            uc = _silu(uc)
            x_dbl = uc @ xproj_w.T
            dt, Bm, Cm = jnp.split(x_dbl, [DT_RANK, DT_RANK + D_STATE], axis=-1)
            dt = jax.nn.softplus(dt @ dt_w.T + dt_b)
            A = -jnp.exp(A_log)

            def step(h, t):
                dt_t, B_t, C_t, u_t = t
                dA = jnp.exp(dt_t[:, :, None] * A)
                h = dA * h + (dt_t * u_t)[:, :, None] * B_t[:, None, :]
                y = jnp.einsum('bdn,bn->bd', h, C_t)
                return (h, y)
            xs = (dt.swapaxes(0, 1), Bm.swapaxes(0, 1), Cm.swapaxes(0, 1), uc.swapaxes(0, 1))
            h0 = jnp.zeros((B, D_INNER, D_STATE), x.dtype)
            _, ys = jax.lax.scan(step, h0, xs)
            y = ys.swapaxes(0, 1) + uc * D_skip
            return y * _silu(z) @ out_w.T

        def _mamba_params(key):
            ks = jax.random.split(key, 8)
            return dict(in_w=jax.random.normal(ks[0], (2 * D_INNER, D_MODEL), jnp.float32) * 0.02, conv_w=jax.random.normal(ks[1], (D_INNER, D_CONV), jnp.float32) * 0.2, conv_b=jnp.zeros((D_INNER,), jnp.float32), xproj_w=jax.random.normal(ks[2], (DT_RANK + 2 * D_STATE, D_INNER), jnp.float32) * 0.02, dt_w=jax.random.normal(ks[3], (D_INNER, DT_RANK), jnp.float32) * 0.02, dt_b=jax.random.normal(ks[4], (D_INNER,), jnp.float32) * 0.02, A_log=jnp.log(jnp.tile(jnp.arange(1, D_STATE + 1, dtype=jnp.float32), (D_INNER, 1))), D_skip=jnp.ones((D_INNER,), jnp.float32), out_w=jax.random.normal(ks[5], (D_MODEL, D_INNER), jnp.float32) * 0.02)
        hf = _mamba(hidden_states, f_in_w, f_conv_w, f_conv_b, f_xproj_w, f_dt_w, f_dt_b, f_A_log, f_D_skip, f_out_w)
        hb = jnp.flip(_mamba(jnp.flip(hidden_states, 1), b_in_w, b_conv_w, b_conv_b, b_xproj_w, b_dt_w, b_dt_b, b_A_log, b_D_skip, b_out_w), 1)
        h = hf + hb + hidden_states
        mu = h.mean(-1, keepdims=True)
        var = ((h - mu) ** 2).mean(-1, keepdims=True)
        return (h - mu) / jnp.sqrt(var + EPS) * ln_g + ln_b

    def _L1_ffn_ref(x0, w1, b1, alpha_w1, alpha_a1, w2, b2, alpha_w2, alpha_a2):
        import jax, jax.numpy as jnp
        import numpy as np
        QN, QP = (-8, 7)

        def round_pass(x):
            return x + jax.lax.stop_gradient(jnp.round(x) - x)

        def _quant_act(x, alpha_a):
            a = alpha_a.mean()
            return round_pass(jnp.clip(x / a, QN, QP))

        def _quant_w(w, alpha_w):
            return round_pass(jnp.clip(w / alpha_w[:, None], QN, QP))
        xq = _quant_act(x0, alpha_a1)
        wq1 = _quant_w(w1, alpha_w1)
        x1 = jnp.einsum('bsd,hd->bsh', xq, wq1)
        x1 = x1 * alpha_w1 * alpha_a1.mean() + b1
        x1 = jax.nn.gelu(x1, approximate=False)
        x1 = jnp.clip(x1, -10.0, 10.0)
        hq = _quant_act(x1, alpha_a2)
        wq2 = _quant_w(w2, alpha_w2)
        x2 = jnp.einsum('bsh,dh->bsd', hq, wq2)
        x2 = x2 * alpha_w2 * alpha_a2.mean() + b2
        return x2

    def _L2_attn_ref(x, W_qkv, b_qkv, W_proj, b_proj, W_gp, alpha):
        import jax, jax.numpy as jnp
        import numpy as np
        DIM = 192
        GP_NUM = 49
        d = x.shape[-1]
        scale = d ** (-0.5)
        qkv = x @ W_qkv + b_qkv
        q, k, v = jnp.split(qkv, 3, axis=-1)
        scores = jnp.einsum('bnd,bmd->bnm', q, k) * scale
        attn = jax.nn.softmax(scores, axis=-1)
        gw = jax.nn.softmax(q @ W_gp, axis=-1)
        group = jnp.einsum('bng,bmg->bnm', gw, gw)
        a = jax.nn.sigmoid(alpha)
        weights = attn * (a + (1.0 - a) * group)
        out = jnp.einsum('bnm,bmd->bnd', weights, v)
        return out @ W_proj + b_proj

    def _L2_ffn_ref(x, router_w, w_gate, w_up, w_down, ws_gate, ws_up, ws_down, sg_w, sg_b):
        import jax, jax.numpy as jnp
        import numpy as np
        B, S, D = (4, 256, 192)
        E = 8
        H = 192
        HS = 768
        TOPK_ROUTED = 2
        probs = jax.nn.softmax(x @ router_w, axis=-1)
        gates, idx = jax.lax.top_k(probs, TOPK_ROUTED)
        gates = gates / jnp.sum(gates, axis=-1, keepdims=True)
        n_exp = router_w.shape[1]
        dense_g = jnp.sum(jax.nn.one_hot(idx, n_exp, dtype=x.dtype) * gates[..., None], axis=-2)
        g = jax.nn.silu(jnp.einsum('bsd,edh->bseh', x, w_gate))
        u = jnp.einsum('bsd,edh->bseh', x, w_up)
        expert_out = jnp.einsum('bseh,ehd->bsed', g * u, w_down)
        routed = jnp.einsum('bse,bsed->bsd', dense_g, expert_out)
        shared = jax.nn.silu(x @ ws_gate) * (x @ ws_up) @ ws_down
        alpha = jax.nn.sigmoid(x @ sg_w + sg_b)
        return alpha * shared + (1.0 - alpha) * routed

    def _L3_attn_ref(x, Wq, Wk, Wv, bv, Wmix, Wcb, Wproj, bproj):
        import jax, jax.numpy as jnp
        import numpy as np
        DIM = 192
        ALL_KEY_DIM = 192
        NUM_HEADS = 12
        HEAD_DIM = DIM // NUM_HEADS
        SCALE = HEAD_DIM ** (-0.5)
        B, N, C = x.shape
        H, Dh = (NUM_HEADS, C // NUM_HEADS)
        q_shared = x @ Wq.T
        k = x @ Wk.T
        v = (x @ Wv.T + bv).reshape(B, N, H, Dh).transpose(0, 2, 1, 3)
        q = jnp.einsum('bnd,hd->bhnd', q_shared, Wmix)
        scores = jnp.einsum('bhnd,bmd->bhnm', q, k)
        content_bias = jnp.einsum('bmd,hd->bhm', x, Wcb)
        attn = jax.nn.softmax((scores + content_bias[:, :, None, :]) * SCALE, axis=-1)
        out = jnp.einsum('bhnm,bhmd->bhnd', attn, v)
        out = out.transpose(0, 2, 1, 3).reshape(B, N, C)
        return out @ Wproj.T + bproj

    def _L3_ffn_ref(inputs, router_w, w1, w2):
        import jax, jax.numpy as jnp
        import numpy as np
        NUM_EXPERTS = 8
        TOP_K = 2
        CAP_FACTOR = 1.0
        D_MODEL = 192
        D_FF = 768
        B, S, D = inputs.shape
        x = inputs.reshape(-1, D)
        N = x.shape[0]
        logits = x @ router_w.T
        probs = jax.nn.softmax(logits.astype(jnp.float32), axis=-1)
        weights, sel = jax.lax.top_k(probs, TOP_K)
        cap = int(CAP_FACTOR * N * TOP_K) + 1
        n_real = N * TOP_K
        expert_flat = sel.reshape(-1)
        weight_flat = weights.reshape(-1)
        token_idx = jnp.repeat(jnp.arange(N), TOP_K)
        pad = cap - n_real
        expert_flat = jnp.pad(expert_flat, (0, pad))
        weight_flat = jnp.pad(weight_flat, (0, pad))
        token_idx = jnp.pad(token_idx, (0, pad))
        valid = jnp.arange(cap) < n_real
        toks = x[token_idx]

        def mlp(w1e, w2e):
            return jax.nn.gelu(toks @ w1e) @ w2e
        ys = jax.vmap(mlp)(w1, w2)
        gate = (weight_flat * valid.astype(weight_flat.dtype)).astype(toks.dtype)
        res = ys[expert_flat, jnp.arange(cap)] * gate[:, None]
        out = jnp.zeros((N, D), dtype=inputs.dtype).at[token_idx].add(res)
        return out.reshape(B, S, D)
    h = _L0_tok_ref(x, L0_tok_dw_w, L0_tok_pw_w, L0_tok_pw_b, L0_tok_ln_g, L0_tok_ln_b)
    h = jnp.concatenate([jnp.broadcast_to(cls_tok, (h.shape[0], 1, h.shape[2])), h], axis=1)
    h = h + _L0_attn_ref(_layernorm(h, axis=-1), L0_attn_qkv_w, L0_attn_proj_w, L0_attn_proj_b)
    h = h + _L0_ffn_ref(_layernorm(h, axis=-1), L0_ffn_gate_w, L0_ffn_gate_b, L0_ffn_bias, L0_ffn_Wu, L0_ffn_bu, L0_ffn_Wg, L0_ffn_bg, L0_ffn_Wd, L0_ffn_bd, L0_ffn_sWu, L0_ffn_sbu, L0_ffn_sWg, L0_ffn_sbg, L0_ffn_sWd, L0_ffn_sbd)
    h = h + _L1_attn_ref(_layernorm(h, axis=-1), L1_attn_f_in_w, L1_attn_f_conv_w, L1_attn_f_conv_b, L1_attn_f_xproj_w, L1_attn_f_dt_w, L1_attn_f_dt_b, L1_attn_f_A_log, L1_attn_f_D_skip, L1_attn_f_out_w, L1_attn_b_in_w, L1_attn_b_conv_w, L1_attn_b_conv_b, L1_attn_b_xproj_w, L1_attn_b_dt_w, L1_attn_b_dt_b, L1_attn_b_A_log, L1_attn_b_D_skip, L1_attn_b_out_w, L1_attn_ln_g, L1_attn_ln_b)
    h = h + _L1_ffn_ref(_layernorm(h, axis=-1), L1_ffn_w1, L1_ffn_b1, L1_ffn_alpha_w1, L1_ffn_alpha_a1, L1_ffn_w2, L1_ffn_b2, L1_ffn_alpha_w2, L1_ffn_alpha_a2)
    h = h + _L2_attn_ref(_layernorm(h, axis=-1), L2_attn_W_qkv, L2_attn_b_qkv, L2_attn_W_proj, L2_attn_b_proj, L2_attn_W_gp, L2_attn_alpha)
    h = h + _L2_ffn_ref(_layernorm(h, axis=-1), L2_ffn_router_w, L2_ffn_w_gate, L2_ffn_w_up, L2_ffn_w_down, L2_ffn_ws_gate, L2_ffn_ws_up, L2_ffn_ws_down, L2_ffn_sg_w, L2_ffn_sg_b)
    h = h + _L3_attn_ref(_layernorm(h, axis=-1), L3_attn_Wq, L3_attn_Wk, L3_attn_Wv, L3_attn_bv, L3_attn_Wmix, L3_attn_Wcb, L3_attn_Wproj, L3_attn_bproj)
    h = h + _L3_ffn_ref(_layernorm(h, axis=-1), L3_ffn_router_w, L3_ffn_w1, L3_ffn_w2)
    return h

_drawn_inputs = setup_inputs


def setup_inputs(seed=0):
    import zlib

    import numpy as np

    out = dict(_drawn_inputs(seed))
    spreads = {'L0_tok_ln_g': (1.0, 0.2),
     'L0_tok_ln_b': (0.0, 0.1),
     'L0_attn_proj_b': (0.0, 0.1),
     'L0_ffn_gate_b': (0.0, 0.338),
     'L0_ffn_bias': (0.0, 0.1),
     'L0_ffn_bu': (0.0, 0.8),
     'L0_ffn_bg': (0.0, 0.8),
     'L0_ffn_bd': (0.0, 0.1),
     'L0_ffn_sbu': (0.0, 0.8),
     'L0_ffn_sbg': (0.0, 0.728),
     'L0_ffn_sbd': (0.0, 0.1),
     'L1_attn_f_conv_b': (0.0, 0.8),
     'L1_attn_f_D_skip': (1.0, 0.6),
     'L1_attn_b_conv_b': (0.0, 0.8),
     'L1_attn_b_D_skip': (1.0, 0.6),
     'L1_attn_ln_g': (1.0, 0.2),
     'L1_attn_ln_b': (0.0, 0.1),
     'L2_attn_b_qkv': (0.0, 0.1),
     'L2_attn_b_proj': (0.0, 0.1),
     'L3_attn_bv': (0.0, 1.722),
     'L3_attn_bproj': (0.0, 0.434)}
    factors = {'cls_tok': 3.37,
     'L0_ffn_Wu': 7.405,
     'L0_ffn_Wg': 7.186,
     'L0_ffn_Wd': 6.779,
     'L0_ffn_sWu': 3.314,
     'L0_ffn_sWg': 3.39,
     'L0_ffn_sWd': 3.322,
     'L1_attn_f_in_w': 8.0,
     'L1_attn_f_conv_w': 8.0,
     'L1_attn_f_xproj_w': 8.0,
     'L1_attn_f_dt_w': 8.0,
     'L1_attn_f_dt_b': 25.642,
     'L1_attn_f_A_log': 8.0,
     'L1_attn_f_out_w': 8.0,
     'L1_attn_b_in_w': 8.0,
     'L1_attn_b_conv_w': 8.0,
     'L1_attn_b_xproj_w': 8.0,
     'L1_attn_b_dt_w': 8.0,
     'L1_attn_b_dt_b': 8.0,
     'L1_attn_b_A_log': 8.0,
     'L1_attn_b_out_w': 8.0,
     'L1_ffn_b1': 28.823,
     'L1_ffn_alpha_w1': 29.872,
     'L1_ffn_b2': 3.807,
     'L1_ffn_alpha_w2': 14.887,
     'L1_ffn_alpha_a2': 200.0,
     'L2_attn_W_gp': 29.776,
     'L2_ffn_router_w': 8.0,
     'L2_ffn_w_gate': 8.0,
     'L2_ffn_w_up': 8.0,
     'L2_ffn_w_down': 8.0,
     'L2_ffn_ws_gate': 6.372,
     'L2_ffn_ws_up': 6.089,
     'L2_ffn_ws_down': 6.238,
     'L2_ffn_sg_w': 8.0,
     'L3_attn_Wq': 64.0,
     'L3_attn_Wk': 64.0,
     'L3_attn_Wmix': 64.0,
     'L3_attn_Wcb': 184.881,
     'L1_ffn_w1': 8.0,
     'L1_ffn_w2': 5.993,
     'L3_attn_Wv': 8.0,
     'L3_attn_Wproj': 2.998}
    for name, (base, spread) in spreads.items():
        noise = np.random.default_rng([zlib.crc32(name.encode()), seed]).standard_normal(out[name].shape)
        drawn = base * np.exp(spread * noise) if base else spread * noise
        out[name] = jnp.asarray(drawn.astype(out[name].dtype))
    for name, factor in factors.items():
        out[name] = (out[name] * factor).astype(out[name].dtype)
    return out
```

```python
from contextlib import ExitStack

import concourse.bass as bass
from concourse import mybir

ALU = mybir.AluOpType
ACT = mybir.ActivationFunctionType
AX = mybir.AxisListType
F32 = mybir.dt.float32
BF16 = mybir.dt.bfloat16
ds = bass.ds

ITEMS = 16
PATCHES = 128
N = PATCHES + 1
D = 192
HALF = D // 2
T = ITEMS * N
TILE = 344
TILES = T // TILE
assert TILES * TILE == T


class Stage:

    def __init__(self, nc, name):
        self.nc, self.name, self.ctx, self.sems = nc, name, ExitStack(), []

    def __enter__(self):
        self.ctx.__enter__()
        return self

    def sb(self, name, shape, dt=F32):
        return self.ctx.enter_context(self.nc.sbuf_tensor(f"{self.name}_{name}", shape, dt))

    def ps(self, name, shape, dt=F32):
        return self.ctx.enter_context(self.nc.psum_tensor(f"{self.name}_{name}", shape, dt))

    def sem(self, name):
        s = self.ctx.enter_context(self.nc.semaphore(f"{self.name}_{name}"))
        self.sems.append(s)
        return s

    def __exit__(self, *exc):
        if exc[0] is None:
            with self.nc.Block() as block:
                @block.gpsimd
                def _(pool):
                    for s in self.sems:
                        pool.sem_clear(s)
        return self.ctx.__exit__(*exc)


def layer_norm(nc, h, xn, name):
    with Stage(nc, name) as st:
        averager = st.sb("averager", [HALF, HALF])
        eps = st.sb("eps", [HALF, 1])
        centred = st.sb("centred", [HALF, 2, 2, TILE])
        squared = st.sb("squared", [HALF, 2, 2, TILE])
        std = st.sb("std", [HALF, 2, TILE])
        rstd = st.sb("rstd", [HALF, 2, TILE])
        mean_ps = st.ps("mean", [HALF, 2, 512])
        var_ps = st.ps("var", [HALF, 2, 512])
        consts = st.sem("consts")
        mean_ready = st.sem("mean_ready")
        centred_ready = st.sem("centred_ready")
        squared_ready = st.sem("squared_ready")
        var_ready = st.sem("var_ready")
        std_ready = st.sem("std_ready")
        rstd_ready = st.sem("rstd_ready")
        xn_ready = st.sem("xn_ready")

        def cols(t):
            return slice(t * TILE, (t + 1) * TILE)

        with nc.Block() as block:
            @block.gpsimd
            def _(pool):
                pool.memset(averager[:], 1.0 / D).then_inc(consts, 1)
                pool.memset(eps[:], 1e-5).then_inc(consts, 1)

            @block.tensor
            def _(pe):
                def mean(t):
                    if t >= 2:
                        pe.wait_ge(centred_ready, t - 1)
                    for j in range(2):
                        mm = pe.matmul(mean_ps[:, t % 2, 0:TILE], averager[:], h[:, j, cols(t)],
                                       start=(j == 0), stop=(j == 1))
                    mm.then_inc(mean_ready, 1)

                pe.wait_ge(consts, 2)
                mean(0)
                for t in range(TILES):
                    if t + 1 < TILES:
                        mean(t + 1)
                    pe.wait_ge(squared_ready, t + 1)
                    if t >= 2:
                        pe.wait_ge(std_ready, t - 1)
                    for j in range(2):
                        mm = pe.matmul(var_ps[:, t % 2, 0:TILE], averager[:], squared[:, t % 2, j, :],
                                       start=(j == 0), stop=(j == 1))
                    mm.then_inc(var_ready, 1)

            @block.scalar
            def _(act):
                def square(t):
                    act.wait_ge(centred_ready, t + 1)
                    if t >= 2:
                        act.wait_ge(var_ready, t - 1)
                    act.activation(squared[:, t % 2], centred[:, t % 2], ACT.Square).then_inc(squared_ready, 1)

                act.wait_ge(consts, 2)
                square(0)
                for t in range(TILES):
                    if t + 1 < TILES:
                        square(t + 1)
                    act.wait_ge(var_ready, t + 1)
                    if t >= 2:
                        act.wait_ge(rstd_ready, t - 1)
                    act.activation(std[:, t % 2], var_ps[:, t % 2, 0:TILE], ACT.Sqrt,
                                   bias=eps[:]).then_inc(std_ready, 1)

            @block.vector
            def _(dve):
                def centre(t):
                    dve.wait_ge(mean_ready, t + 1)
                    if t >= 2:
                        dve.wait_ge(squared_ready, t - 1)
                        dve.wait_ge(xn_ready, t - 1)
                    dve.tensor_tensor(centred[:, t % 2], h[:, :, cols(t)],
                                      mean_ps[:, t % 2, 0:TILE].unsqueeze(1).broadcast_to([HALF, 2, TILE]),
                                      ALU.subtract).then_inc(centred_ready, 1)

                centre(0)
                for t in range(TILES):
                    if t + 1 < TILES:
                        centre(t + 1)
                    dve.wait_ge(std_ready, t + 1)
                    if t >= 2:
                        dve.wait_ge(xn_ready, t - 1)
                    dve.reciprocal(rstd[:, t % 2], std[:, t % 2]).then_inc(rstd_ready, 1)
                    dve.wait_ge(rstd_ready, t + 1)
                    dve.tensor_tensor(xn[:, :, cols(t)], centred[:, t % 2],
                                      rstd[:, t % 2].unsqueeze(1).broadcast_to([HALF, 2, TILE]),
                                      ALU.mult).then_inc(xn_ready, 1)


def steps(engine, count, body):
    body(0, True)
    with engine.Fori(1, count) as s:
        body(s, False)


def embed_tokens(nc, dram, h, xn):
    TAPS = 7
    PAD = TAPS // 2
    G = 2
    COLS = G * PATCHES
    STEPS = ITEMS // G
    with Stage(nc, "embed") as st:
        x = st.sb("x", [HALF, 2, ITEMS, PATCHES + 2 * PAD])
        taps = st.sb("taps", [HALF, 2, TAPS])
        diag = st.sb("diag", [HALF, 2, TAPS, HALF])
        ones = st.sb("ones", [HALF, HALF])
        averager = st.sb("averager", [HALF, HALF])
        point_w = st.sb("point_w", [HALF, 2, D])
        cols = st.sb("cols", [HALF, 4, 2])
        eps = st.sb("eps", [HALF, 1])
        conv = st.sb("conv", [HALF, 2, COLS])
        y = st.sb("y", [HALF, 2, COLS])
        centred = st.sb("centred", [HALF, 2, COLS])
        squared = st.sb("squared", [HALF, 2, COLS])
        std = st.sb("std", [HALF, COLS])
        rstd = st.sb("rstd", [HALF, COLS])
        normed = st.sb("normed", [HALF, 2, COLS])
        conv_ps = st.ps("conv_ps", [HALF, 2, COLS])
        y_ps = st.ps("y_ps", [HALF, 2, COLS])
        mean_ps = st.ps("mean_ps", [HALF, COLS])
        var_ps = st.ps("var_ps", [HALF, COLS])
        x_loaded = st.sem("x_loaded")
        weights_loaded = st.sem("weights_loaded")
        padded = st.sem("padded")
        consts = st.sem("consts")
        diag_ready = st.sem("diag_ready")
        conv_done = st.sem("conv_done")
        conv_ready = st.sem("conv_ready")
        y_done = st.sem("y_done")
        y_ready = st.sem("y_ready")
        mean_ready = st.sem("mean_ready")
        centred_ready = st.sem("centred_ready")
        squared_ready = st.sem("squared_ready")
        var_ready = st.sem("var_ready")
        std_ready = st.sem("std_ready")
        rstd_ready = st.sem("rstd_ready")
        normed_ready = st.sem("normed_ready")
        h_ready = st.sem("h_ready")
        h_items = h[:].rearrange("p j (b n) -> p j b n", n=N)
        with nc.Block() as block:
            @block.sync
            def _(sp):
                for j in range(2):
                    sp.dma_start(x[:, j, :, PAD:PAD + PATCHES], dram["x"][:, j]).then_inc(x_loaded, 16)
                sp.dma_start(taps[:], dram["embed_taps"]).then_inc(weights_loaded, 16)
                sp.dma_start(point_w[:], dram["embed_point_w"]).then_inc(weights_loaded, 16)
                sp.dma_start(cols[:], dram["embed_cols"]).then_inc(weights_loaded, 16)

            @block.gpsimd
            def _(pool):
                pool.memset(x[:, :, :, 0:PAD], 0.0).then_inc(padded, 1)
                pool.memset(x[:, :, :, PAD + PATCHES:], 0.0).then_inc(padded, 1)
                pool.memset(ones[:], 1.0).then_inc(consts, 1)
                pool.memset(averager[:], 1.0 / D).then_inc(consts, 1)
                pool.memset(eps[:], 1e-6).then_inc(consts, 1)
                pool.wait_ge(weights_loaded, 48)
                pool.wait_ge(consts, 3)
                for j in range(2):
                    for k in range(TAPS):
                        pool.tensor_scalar(diag[:, j, k, :], ones[:], taps[:, j, k:k + 1], None,
                                           ALU.mult).then_inc(diag_ready, 1)
                pool.wait_ge(diag_ready, 2 * TAPS)
                for j in range(2):
                    pool.affine_select(out=diag[:, j], in_=diag[:, j], compare_op=ALU.is_equal, fill=0.0,
                                       base=0, pattern=[[0, TAPS], [-1, HALF]],
                                       channel_multiplier=1).then_inc(diag_ready, 1)

            @block.tensor
            def _(pe):
                pe.wait_ge(diag_ready, 2 * TAPS + 2)
                pe.wait_ge(padded, 2)
                pe.wait_ge(x_loaded, 32)
                pe.wait_ge(weights_loaded, 48)

                def step(s, first):
                    for j in range(2):
                        for k in range(TAPS):
                            mm = pe.matmul(conv_ps[:, j, :].rearrange("p (b n) -> p b n", b=G), diag[:, j, k, :],
                                           x[:, j, ds(s * G, G), k:k + PATCHES],
                                           start=(k == 0), stop=(k == TAPS - 1))
                    mm.then_inc(conv_done, 1)
                    pe.wait_ge(conv_ready, s + 1)
                    for m in range(2):
                        for j in range(2):
                            mm = pe.matmul(y_ps[:, m, :], point_w[:, j, m * HALF:(m + 1) * HALF], conv[:, j, :],
                                           start=(j == 0), stop=(j == 1))
                    mm.then_inc(y_done, 1)
                    pe.wait_ge(y_ready, 2 * s + 2)
                    for j in range(2):
                        mm = pe.matmul(mean_ps[:], averager[:], y[:, j, :], start=(j == 0), stop=(j == 1))
                    mm.then_inc(mean_ready, 1)
                    pe.wait_ge(squared_ready, s + 1)
                    if not first:
                        pe.wait_ge(std_ready, s)
                    for j in range(2):
                        mm = pe.matmul(var_ps[:], averager[:], squared[:, j, :], start=(j == 0), stop=(j == 1))
                    mm.then_inc(var_ready, 1)

                steps(pe, STEPS, step)

            @block.scalar
            def _(act):
                act.wait_ge(weights_loaded, 48)
                act.wait_ge(consts, 3)

                def step(s, first):
                    act.wait_ge(conv_done, s + 1)
                    act.activation(conv[:], conv_ps[:], ACT.Copy).then_inc(conv_ready, 1)
                    act.wait_ge(y_done, s + 1)
                    for m in range(2):
                        act.activation(y[:, m, :], y_ps[:, m, :], ACT.Identity,
                                       bias=cols[:, 0, m:m + 1]).then_inc(y_ready, 1)
                    act.wait_ge(centred_ready, s + 1)
                    act.activation(squared[:], centred[:], ACT.Square).then_inc(squared_ready, 1)
                    act.wait_ge(var_ready, s + 1)
                    if not first:
                        act.wait_ge(rstd_ready, s)
                    act.activation(std[:], var_ps[:], ACT.Sqrt, bias=eps[:]).then_inc(std_ready, 1)
                    act.wait_ge(normed_ready, s + 1)
                    for m in range(2):
                        act.activation(h_items[:, m, ds(s * G, G), 1:N],
                                       normed[:, m, :].rearrange("p (b n) -> p b n", b=G), ACT.Relu,
                                       bias=cols[:, 2, m:m + 1], scale=cols[:, 1, m:m + 1]).then_inc(h_ready, 1)

                steps(act, STEPS, step)

            @block.vector
            def _(dve):
                dve.wait_ge(weights_loaded, 48)
                for m in range(2):
                    dve.tensor_copy(h_items[:, m, :, 0], cols[:, 3, m:m + 1].broadcast_to([HALF, ITEMS]))

                def step(s, first):
                    dve.wait_ge(mean_ready, s + 1)
                    if not first:
                        dve.wait_ge(normed_ready, s)
                    dve.tensor_tensor(centred[:], y[:], mean_ps[:].unsqueeze(1).broadcast_to([HALF, 2, COLS]),
                                      ALU.subtract).then_inc(centred_ready, 1)
                    dve.wait_ge(std_ready, s + 1)
                    dve.reciprocal(rstd[:], std[:]).then_inc(rstd_ready, 1)
                    dve.wait_ge(rstd_ready, s + 1)
                    if not first:
                        dve.wait_ge(h_ready, 2 * s)
                    dve.tensor_tensor(normed[:], centred[:], rstd[:].unsqueeze(1).broadcast_to([HALF, 2, COLS]),
                                      ALU.mult).then_inc(normed_ready, 1)

                steps(dve, STEPS, step)


def linear_attention(nc, dram, h, xn):
    HEAD = 16
    SCALE = HEAD ** -0.5
    CHUNKS = ((0, 65), (65, 64))
    with Stage(nc, "linattn") as st:
        w_qkv = st.sb("w_qkv", [HALF, 2, 3 * D])
        w_proj = st.sb("w_proj", [HALF, 2, D])
        b_proj = st.sb("b_proj", [HALF, 1, 2])
        mask = st.sb("mask", [HALF, 2, HALF])
        x = st.sb("x", [HALF, 2, N])
        q = st.sb("q", [HALF, 2, N])
        k = st.sb("k", [65, 2, D])
        v1 = st.sb("v1", [65, 2, 2, 2, HALF])
        kv = st.sb("kv", [HALF, 2, 2, HALF])
        den = st.sb("den", [HALF, 2, N])
        rden = st.sb("rden", [HALF, 2, N])
        heads = st.sb("heads", [HALF, 2, N])
        q_ps = st.ps("q_ps", [HALF, 2, N])
        k_v_ps = st.ps("k_v_ps", [65, 2, 512])
        kv_ps = st.ps("kv_ps", [HALF, 2, 2, HALF])
        num_ps = st.ps("num_ps", [HALF, 2, N])
        den_ps = st.ps("den_ps", [HALF, 2, N])
        o_ps = st.ps("o_ps", [HALF, 2, N])
        loaded = st.sem("loaded")
        ones_ready = st.sem("ones_ready")
        x_ready = st.sem("x_ready")
        qkv_done = st.sem("qkv_done")
        v_ready = st.sem("v_ready")
        k_ready = st.sem("k_ready")
        q_ready = st.sem("q_ready")
        kv_done = st.sem("kv_done")
        kv_ready = st.sem("kv_ready")
        num_done = st.sem("num_done")
        den_ready = st.sem("den_ready")
        rden_ready = st.sem("rden_ready")
        heads_ready = st.sem("heads_ready")
        proj_done = st.sem("proj_done")
        h_ready = st.sem("h_ready")
        with nc.Block() as block:
            @block.sync
            def _(sp):
                sp.dma_start(w_qkv[:], dram["linattn_qkv"]).then_inc(loaded, 16)
                sp.dma_start(w_proj[:], dram["linattn_proj"]).then_inc(loaded, 16)
                sp.dma_start(b_proj[:], dram["linattn_cols"]).then_inc(loaded, 16)
                sp.dma_start(mask[:], dram["head_mask"]).then_inc(loaded, 16)

            @block.gpsimd
            def _(pool):
                pool.memset(v1[:, :, :, 1, :], 1.0).then_inc(ones_ready, 1)

                def step(b, first):
                    if not first:
                        pool.wait_ge(qkv_done, b)
                    pool.tensor_copy(x[:], xn[:, :, ds(b * N, N)]).then_inc(x_ready, 1)

                steps(pool, ITEMS, step)

            @block.tensor
            def _(pe):
                pe.wait_ge(loaded, 64)
                pe.wait_ge(ones_ready, 1)

                def step(b, first):
                    pe.wait_ge(x_ready, b + 1)
                    for c, (c0, n) in enumerate(CHUNKS):
                        for j in range(2):
                            pe.matmul(k_v_ps[0:n, c, 0:2 * D], x[:, j, c0:c0 + n], w_qkv[:, j, D:3 * D],
                                      start=(j == 0), stop=(j == 1))
                    for m in range(2):
                        for j in range(2):
                            mm = pe.matmul(q_ps[:, m, :], w_qkv[:, j, m * HALF:(m + 1) * HALF], x[:, j, :],
                                           start=(j == 0), stop=(j == 1))
                    mm.then_inc(qkv_done, 1)
                    pe.wait_ge(v_ready, 2 * b + 2)
                    pe.wait_ge(k_ready, 2 * b + 2)
                    for j in range(2):
                        for c, (c0, n) in enumerate(CHUNKS):
                            mm = pe.matmul(kv_ps[:, j], k[0:n, c, j * HALF:(j + 1) * HALF], v1[0:n, c, j],
                                           start=(c == 0), stop=(c == 1))
                    mm.then_inc(kv_done, 1)
                    pe.wait_ge(kv_ready, b + 1)
                    pe.wait_ge(q_ready, b + 1)
                    for j in range(2):
                        pe.matmul(num_ps[:, j, :], kv[:, j, 0, :], q[:, j, :], start=True, stop=True)
                        mm = pe.matmul(den_ps[:, j, :], kv[:, j, 1, :], q[:, j, :], start=True, stop=True)
                    mm.then_inc(num_done, 1)
                    pe.wait_ge(heads_ready, b + 1)
                    if not first:
                        pe.wait_ge(h_ready, 2 * b)
                    for m in range(2):
                        for j in range(2):
                            mm = pe.matmul(o_ps[:, m, :], w_proj[:, j, m * HALF:(m + 1) * HALF], heads[:, j, :],
                                           start=(j == 0), stop=(j == 1))
                    mm.then_inc(proj_done, 1)

                steps(pe, ITEMS, step)

            @block.scalar
            def _(act):
                def step(b, first):
                    act.wait_ge(qkv_done, b + 1)
                    if not first:
                        act.wait_ge(kv_done, b)
                    for c, (c0, n) in enumerate(CHUNKS):
                        act.activation(v1[0:n, c, :, 0, :],
                                       k_v_ps[0:n, c, D:2 * D].rearrange("p (j f) -> p j f", j=2),
                                       ACT.Copy).then_inc(v_ready, 1)

                steps(act, ITEMS, step)

            @block.vector
            def _(dve):
                dve.wait_ge(loaded, 64)

                def step(b, first):
                    dve.wait_ge(qkv_done, b + 1)
                    if not first:
                        dve.wait_ge(kv_done, b)
                    dve.tensor_scalar(q[:], q_ps[:], 0.0, SCALE, ALU.max, ALU.add).then_inc(q_ready, 1)
                    dve.wait_ge(v_ready, 2 * b + 2)
                    for c, (c0, n) in enumerate(CHUNKS):
                        dve.tensor_scalar(k[0:n, c, :], k_v_ps[0:n, c, 0:D], 0.0, SCALE, ALU.max,
                                          ALU.add).then_inc(k_ready, 1)
                    dve.wait_ge(kv_done, b + 1)
                    dve.tensor_tensor(kv[:], kv_ps[:], mask[:].unsqueeze(1).broadcast_to([HALF, 2, 2, HALF]),
                                      ALU.mult).then_inc(kv_ready, 1)
                    dve.wait_ge(num_done, b + 1)
                    dve.tensor_scalar(den[:], den_ps[:], 1e-6, None, ALU.add).then_inc(den_ready, 1)
                    dve.wait_ge(den_ready, b + 1)
                    dve.reciprocal(rden[:], den[:]).then_inc(rden_ready, 1)
                    dve.wait_ge(rden_ready, b + 1)
                    if not first:
                        dve.wait_ge(proj_done, b)
                    dve.tensor_tensor(heads[:], num_ps[:], rden[:], ALU.mult).then_inc(heads_ready, 1)
                    dve.wait_ge(proj_done, b + 1)
                    for m in range(2):
                        dve.scalar_tensor_tensor(out=h[:, m, ds(b * N, N)], in0=o_ps[:, m, :],
                                                 scalar=b_proj[:, 0, m:m + 1], in1=h[:, m, ds(b * N, N)],
                                                 op0=ALU.add, op1=ALU.add).then_inc(h_ready, 1)

                steps(dve, ITEMS, step)


RT = 86
CHUNKS = T // RT
SPLIT = 96
assert CHUNKS * RT == T and TILE % RT == 0


def router(nc, dram, xn, gates, name, experts, choose, extra=0):
    E = experts + extra
    with Stage(nc, name + "_router") as st:
        w = st.sb("w", [HALF, 2, E])
        ident = st.sb("ident", [RT, RT])
        b = {k: st.sb(k, [RT, E]) for k in ("logit_bias", "score_bias", "scratch_bias")}
        lower = st.sb("lower", [RT, E, E])
        big = {k: st.sb(k, [RT, CHUNKS, experts, experts], BF16) for k in ("greater", "equal")}
        f = {k: st.sb(k, [RT, CHUNKS, E]) for k in ("logits", "exps", "probs", "scores", "rank", "mask", "weight")}
        g = {k: st.sb(k, [RT, CHUNKS, 8]) for k in ("group", "group_rank", "group_mask")}
        c = {k: st.sb(k, [RT, CHUNKS]) for k in ("top", "total", "recip", "u", "v")}
        wide = st.sb("wide", [RT, CHUNKS, SPLIT])
        full = st.sb("full", [SPLIT, T])
        rest = st.sb("rest", [SPLIT, T])
        part = st.sb("part", [SPLIT, T], BF16)
        logits_ps = st.ps("logits_ps", [RT, CHUNKS, E])
        turned_ps = st.ps("turned_ps", [SPLIT, TILES, 512])
        loaded = st.sem("loaded")
        logits_done = st.sem("logits_done")
        exp_in_ready = st.sem("exp_in_ready")
        exp_ready = st.sem("exp_ready")
        wide_ready = st.sem("wide_ready")
        turned_done = st.sem("turned_done")
        full_ready = st.sem("full_ready")
        chain = st.sem("chain")
        with nc.Block() as block:
            @block.sync
            def _(sp):
                sp.dma_start(w[:], dram[name + "_router_w"]).then_inc(loaded, 16)
                sp.dma_start(b["logit_bias"][:], dram[name + "_router_b"][0:1].broadcast_to([RT, E])).then_inc(loaded, 16)
                sp.dma_start(b["score_bias"][:], dram[name + "_router_b"][1:2].broadcast_to([RT, E])).then_inc(loaded, 16)
                sp.dma_start(ident[:], dram["ident"][0:RT, 0:RT]).then_inc(loaded, 16)
                sp.dma_start(lower[:, 0:experts, 0:experts], dram[f"lower{experts}"]).then_inc(loaded, 16)

            @block.tensor
            def _(pe):
                pe.wait_ge(loaded, 80)
                for t in range(CHUNKS):
                    for j in range(2):
                        mm = pe.matmul(logits_ps[:, t, :], xn[:, j, t * RT:(t + 1) * RT], w[:, j, :],
                                       start=(j == 0), stop=(j == 1))
                mm.then_inc(logits_done, 1)
                pe.wait_ge(wide_ready, 1)
                per = TILE // RT
                for t in range(CHUNKS):
                    mm = pe.transpose(turned_ps[:, t // per, (t % per) * RT:(t % per + 1) * RT],
                                      wide[:, t, :], ident[:])
                mm.then_inc(turned_done, 1)

            @block.scalar
            def _(act):
                act.wait_ge(exp_in_ready, 1)
                act.activation(f["exps"][:], f["logits"][:], ACT.Exp).then_inc(exp_ready, 1)
                act.wait_ge(turned_done, 1)
                act.activation(full[:].rearrange("p (t n) -> p t n", n=TILE), turned_ps[:, :, 0:TILE],
                               ACT.Copy).then_inc(full_ready, 1)

            @block.vector
            def _(dve):
                count = [0]

                def link(ins):
                    count[0] += 1
                    ins.then_inc(chain, 1)
                    dve.wait_ge(chain, count[0])

                def over(ap, n):
                    return ap.unsqueeze(1).broadcast_to([RT, CHUNKS, n])

                def last(ap, n):
                    return ap.unsqueeze(2).broadcast_to([RT, CHUNKS, n])

                def rank(out, score, n, kind):
                    this = score.unsqueeze(3).broadcast_to([RT, CHUNKS, n, n])
                    other = score.unsqueeze(2).broadcast_to([RT, CHUNKS, n, n])
                    gt = big["greater"][:].rearrange("p c a b -> p c (a b)")[:, :, 0:n * n].rearrange("p c (a b) -> p c a b", a=n)
                    eq = big["equal"][:].rearrange("p c a b -> p c (a b)")[:, :, 0:n * n].rearrange("p c (a b) -> p c a b", a=n)
                    link(dve.tensor_tensor(gt, other, this, ALU.is_gt))
                    link(dve.tensor_tensor(eq, other, this, ALU.is_equal))
                    link(dve.tensor_tensor(eq, eq, lower[:, 0:n, 0:n].unsqueeze(1).broadcast_to([RT, CHUNKS, n, n]),
                                           ALU.mult))
                    link(dve.tensor_tensor(gt, gt, eq, ALU.add))
                    link(dve.tensor_reduce(out, gt, AX.X, ALU.add))

                link(dve.memset(wide[:], 0.0))
                dve.wait_ge(loaded, 80)
                dve.wait_ge(logits_done, 1)
                L = f["logits"]
                n = experts
                link(dve.tensor_tensor(L[:], logits_ps[:], over(b["logit_bias"][:], E), ALU.add))
                link(dve.tensor_reduce(c["top"][:], L[:, :, 0:n], AX.X, ALU.max))
                link(dve.tensor_tensor(L[:, :, 0:n], L[:, :, 0:n], last(c["top"][:], n), ALU.subtract))
                if extra:
                    link(dve.tensor_scalar(L[:, :, n:E], L[:, :, n:E], -1.0, None, ALU.mult))
                dve.nop().then_inc(exp_in_ready, 1)
                dve.wait_ge(exp_ready, 1)
                link(dve.tensor_reduce(c["total"][:], f["exps"][:, :, 0:n], AX.X, ALU.add))
                link(dve.reciprocal(c["recip"][:], c["total"][:]))
                link(dve.tensor_tensor(f["probs"][:, :, 0:n], f["exps"][:, :, 0:n], last(c["recip"][:], n), ALU.mult))
                choose(dve, link, rank, over, last, b, f, g, c)
                for r in range(3):
                    ins = dve.tensor_copy(wide[:, :, 32 * r:32 * r + E], f["weight"][:])
                ins.then_inc(wide_ready, 1)
                dve.wait_ge(full_ready, 1)
                link(dve.tensor_copy(part[:], full[:]))
                link(dve.tensor_copy(gates[0:32, :], part[0:32, :]))
                link(dve.tensor_tensor(rest[:], full[:], part[:], ALU.subtract))
                link(dve.tensor_copy(part[:], rest[:]))
                link(dve.tensor_copy(gates[32:64, :], part[32:64, :]))
                link(dve.tensor_tensor(rest[:], rest[:], part[:], ALU.subtract))
                link(dve.tensor_copy(gates[64:96, :], rest[64:96, :]))


def expert_mlps(nc, h, xn, gates, sel, name, units, act_fn, bias, y_bias, extra_down):
    U = len(units)
    with Stage(nc, name + "_mlp") as st:
        s = st.sb("s", [128, 2, TILE])
        prod = st.sb("prod", [128, 2, TILE])
        hid = st.sb("hid", [128, 2, TILE])
        up_ps = st.ps("up_ps", [128, 2, 512])
        gate_ps = st.ps("gate_ps", [128, 2, 512])
        wide_ps = st.ps("wide_ps", [128, 2, 512])
        y_ps = st.ps("y_ps", [HALF, 2, 512])
        up_done = st.sem("up_done")
        side_done = st.sem("side_done")
        s_ready = st.sem("s_ready")
        prod_ready = st.sem("prod_ready")
        hid_ready = st.sem("hid_ready")
        down_done = st.sem("down_done")
        h_ready = st.sem("h_ready")
        gated = [k for k, u in enumerate(units) if u["row"] is not None and u["gate"] is not None]
        prods = len(gated)
        with nc.Block() as block:
            @block.tensor
            def _(pe):
                def down(t, first, k):
                    u = units[k]
                    pe.wait_ge(hid_ready, t * U + k + 1)
                    if k == 0 and not first:
                        pe.wait_ge(h_ready, 2 * t)
                    if k == 0:
                        for i, w in enumerate(extra_down):
                            for m in range(2):
                                pe.matmul(y_ps[:, m, 0:TILE], w[:, m * HALF:(m + 1) * HALF],
                                          gates[:, ds(t * TILE, TILE)], start=(i == 0), stop=False)
                    for m in range(2):
                        mm = pe.matmul(y_ps[:, m, 0:TILE], u["down"][:, m * HALF:(m + 1) * HALF],
                                       hid[0:u["n"], k % 2, :], start=(k == 0 and not extra_down),
                                       stop=(k == U - 1))
                    mm.then_inc(down_done, 1)

                def step(t, first):
                    x = [xn[:, j, ds(t * TILE, TILE)] for j in range(2)]
                    for k, u in enumerate(units):
                        n = u["n"]
                        for j in range(2):
                            mm = pe.matmul(up_ps[0:n, k % 2, 0:TILE], u["up"][:, j, :], x[j],
                                           start=(j == 0), stop=(j == 1))
                        mm.then_inc(up_done, 1)
                        if u["gate"] is not None:
                            for j in range(2):
                                mm = pe.matmul(gate_ps[0:n, k % 2, 0:TILE], u["gate"][:, j, :], x[j],
                                               start=(j == 0), stop=(j == 1))
                        if u["row"] is not None:
                            mm = pe.matmul(wide_ps[0:n, k % 2, 0:TILE], sel[:, u["row"], 0:n],
                                           gates[:, ds(t * TILE, TILE)], start=True, stop=True)
                        mm.then_inc(side_done, 1)
                        if k:
                            down(t, first, k - 1)
                    down(t, first, U - 1)

                steps(pe, TILES, step)

            @block.scalar
            def _(act):
                def step(t, first):
                    for k, u in enumerate(units):
                        n = u["n"]
                        act.wait_ge(up_done, t * U + k + 1)
                        if not first or k >= 2:
                            act.wait_ge(hid_ready, t * U + k - 1)
                        act.activation(s[0:n, k % 2, :], up_ps[0:n, k % 2, 0:TILE], act_fn,
                                       bias=0.0 if bias is None else bias[0:n, 0, k:k + 1]).then_inc(s_ready, 1)

                steps(act, TILES, step)

            @block.vector
            def _(dve):
                def step(t, first):
                    done = 0
                    for k, u in enumerate(units):
                        n = u["n"]
                        g_bias = 0.0 if bias is None else bias[0:n, 1, k:k + 1]
                        dve.wait_ge(s_ready, t * U + k + 1)
                        dve.wait_ge(side_done, t * U + k + 1)
                        if not first or k >= 2:
                            dve.wait_ge(down_done, t * U + k - 1)
                        if u["gate"] is not None and u["row"] is not None:
                            done += 1
                            dve.scalar_tensor_tensor(out=prod[0:n, k % 2, :], in0=gate_ps[0:n, k % 2, 0:TILE],
                                                     scalar=g_bias, in1=s[0:n, k % 2, :], op0=ALU.add,
                                                     op1=ALU.mult).then_inc(prod_ready, 1)
                            dve.wait_ge(prod_ready, t * prods + done)
                            dve.tensor_tensor(hid[0:n, k % 2, :], prod[0:n, k % 2, :], wide_ps[0:n, k % 2, 0:TILE],
                                              ALU.mult).then_inc(hid_ready, 1)
                        elif u["gate"] is not None:
                            dve.scalar_tensor_tensor(out=hid[0:n, k % 2, :], in0=gate_ps[0:n, k % 2, 0:TILE],
                                                     scalar=g_bias, in1=s[0:n, k % 2, :], op0=ALU.add,
                                                     op1=ALU.mult).then_inc(hid_ready, 1)
                        else:
                            dve.tensor_tensor(hid[0:n, k % 2, :], s[0:n, k % 2, :], wide_ps[0:n, k % 2, 0:TILE],
                                              ALU.mult).then_inc(hid_ready, 1)
                    dve.wait_ge(down_done, (t + 1) * U)
                    for m in range(2):
                        tile = h[:, m, ds(t * TILE, TILE)]
                        dve.scalar_tensor_tensor(out=tile, in0=y_ps[:, m, 0:TILE],
                                                 scalar=0.0 if y_bias is None else y_bias[:, 0, m:m + 1],
                                                 in1=tile, op0=ALU.add, op1=ALU.add).then_inc(h_ready, 1)

                steps(dve, TILES, step)


def load(nc, name, pairs):
    with Stage(nc, name) as st:
        loaded = st.sem("loaded")
        with nc.Block() as block:
            @block.sync
            def _(sp):
                for dst, src in pairs:
                    sp.dma_start(dst, src).then_inc(loaded, 16)
                sp.wait_ge(loaded, 16 * len(pairs))


def split_weights(nc, name, w, rest, parts):
    with Stage(nc, name) as st:
        chain = st.sem("chain")
        with nc.Block() as block:
            @block.vector
            def _(dve):
                source = w
                for i in range(3):
                    dve.tensor_copy(parts[:, i], source[:]).then_inc(chain, 1)
                    dve.wait_ge(chain, 2 * i + 1)
                    if i < 2:
                        dve.tensor_tensor(rest[:], source[:], parts[:, i], ALU.subtract).then_inc(chain, 1)
                        dve.wait_ge(chain, 2 * i + 2)
                        source = rest


def grouped_experts(nc, dram, h, xn):
    E, HID, BIG = 16, 128, 1e30

    def choose(dve, link, rank, over, last, b, f, g, c):
        link(dve.tensor_tensor(f["scores"][:], f["probs"][:], over(b["score_bias"][:], E), ALU.add))
        pairs = f["scores"][:].rearrange("p c (g i) -> p c g i", i=2)
        link(dve.tensor_tensor(g["group"][:], pairs[:, :, :, 0], pairs[:, :, :, 1], ALU.add))
        rank(g["group_rank"][:], g["group"][:], 8, "group")
        link(dve.tensor_scalar(g["group_mask"][:], g["group_rank"][:], 3.5, None, ALU.is_lt))
        gm = g["group_mask"][:].unsqueeze(3).broadcast_to([RT, CHUNKS, 8, 2])
        link(dve.tensor_tensor(pairs, pairs, gm, ALU.mult))
        link(dve.tensor_scalar(g["group_mask"][:], g["group_mask"][:], BIG, -BIG, ALU.mult, ALU.add))
        link(dve.tensor_tensor(pairs, pairs, gm, ALU.add))
        rank(f["rank"][:], f["scores"][:], E, "expert")
        link(dve.tensor_scalar(f["mask"][:], f["rank"][:], 3.5, 2.5, ALU.is_lt, ALU.mult))
        link(dve.tensor_tensor(f["weight"][:], f["probs"][:], f["mask"][:], ALU.mult))

    with Stage(nc, "grouped") as st:
        gates = st.sb("gates", [SPLIT, T], BF16)
        sel = st.sb("sel", [SPLIT, E, 128], BF16)
        router(nc, dram, xn, gates, "grouped", E, choose)
        up = st.sb("up", [HALF, 2, E + 1, HID])
        gate = st.sb("gate", [HALF, 2, E + 1, HID])
        down = st.sb("down", [HID, E + 1, D])
        bias = st.sb("bias", [HID, 2, E + 1])
        bd = st.sb("bd", [SPLIT, D])
        bd_rest = st.sb("bd_rest", [SPLIT, D])
        bd_parts = st.sb("bd_parts", [SPLIT, 3, D], BF16)
        y_bias = st.sb("y_bias", [HALF, 1, 2])
        load(nc, "grouped_load", [(up[:], dram["grouped_up"]), (gate[:], dram["grouped_gate"]),
                                  (down[:], dram["grouped_down"]), (bias[:], dram["grouped_bias"]),
                                  (bd[:], dram["grouped_bd"]), (y_bias[:], dram["grouped_cols"]),
                                  (sel[:], dram["sel"][:, 0:E])])
        split_weights(nc, "grouped_bd_split", bd, bd_rest, bd_parts)
        units = [dict(up=up[:, :, e], gate=gate[:, :, e], down=down[:, e], n=HID, row=e if e < E else None)
                 for e in range(E + 1)]
        expert_mlps(nc, h, xn, gates, sel, "grouped", units, ACT.Silu, bias, y_bias,
                    [bd_parts[:, i] for i in range(3)])


def top2(n):
    def choose(dve, link, rank, over, last, b, f, g, c):
        rank(f["rank"][:, :, 0:n], f["probs"][:, :, 0:n], n, "expert")
        link(dve.tensor_scalar(f["mask"][:, :, 0:n], f["rank"][:, :, 0:n], 1.5, None, ALU.is_lt))
        link(dve.tensor_tensor(f["weight"][:, :, 0:n], f["probs"][:, :, 0:n], f["mask"][:, :, 0:n], ALU.mult))
    return choose


def shared_experts(nc, dram, h, xn):
    E, HID, SHARED = 8, 192, 768

    def choose(dve, link, rank, over, last, b, f, g, c):
        top2(E)(dve, link, rank, over, last, b, f, g, c)
        w, alpha = f["weight"][:, :, 0:E], f["weight"][:, :, E]
        link(dve.tensor_reduce(c["total"][:], w, AX.X, ALU.add))
        link(dve.reciprocal(c["recip"][:], c["total"][:]))
        link(dve.tensor_tensor(w, w, last(c["recip"][:], E), ALU.mult))
        link(dve.tensor_scalar(c["u"][:], f["exps"][:, :, E], 1.0, None, ALU.add))
        link(dve.reciprocal(c["v"][:], c["u"][:]))
        link(dve.tensor_copy(alpha, c["v"][:]))
        link(dve.tensor_scalar(c["u"][:], c["v"][:], -1.0, 1.0, ALU.mult, ALU.add))
        link(dve.tensor_tensor(w, w, last(c["u"][:], E), ALU.mult))

    with Stage(nc, "shared") as st:
        gates = st.sb("gates", [SPLIT, T], BF16)
        sel = st.sb("sel", [SPLIT, E + 1, 128], BF16)
        router(nc, dram, xn, gates, "shared", E, choose, extra=1)
        W = E * HID + SHARED
        up = st.sb("up", [HALF, 2, W])
        gate = st.sb("gate", [HALF, 2, W])
        down_r = st.sb("down_r", [HALF, E * 2, D])
        down_s = st.sb("down_s", [128, SHARED // 128, D])
        load(nc, "shared_load", [(up[:], dram["shared_up"]), (gate[:], dram["shared_gate"]),
                                 (down_r[:], dram["shared_down_r"]), (down_s[:], dram["shared_down_s"]),
                                 (sel[:], dram["sel"][:, 0:E + 1])])
        units = [dict(up=up[:, :, k * HALF:(k + 1) * HALF], gate=gate[:, :, k * HALF:(k + 1) * HALF],
                      down=down_r[:, k], n=HALF, row=k // 2) for k in range(2 * E)]
        for k in range(SHARED // 128):
            cols = slice(E * HID + k * 128, E * HID + (k + 1) * 128)
            units.append(dict(up=up[:, :, cols], gate=gate[:, :, cols], down=down_s[:, k], n=128, row=E))
        expert_mlps(nc, h, xn, gates, sel, "shared", units, ACT.Silu, None, None, [])


def gelu_experts(nc, dram, h, xn):
    E, HID = 8, 768
    with Stage(nc, "geluexp") as st:
        gates = st.sb("gates", [SPLIT, T], BF16)
        sel = st.sb("sel", [SPLIT, E, 128], BF16)
        router(nc, dram, xn, gates, "geluexp", E, top2(E))
        up = st.sb("up", [HALF, 2, E * HID])
        down = st.sb("down", [128, E * HID // 128, D])
        load(nc, "geluexp_load", [(up[:], dram["geluexp_up"]), (down[:], dram["geluexp_down"]),
                                  (sel[:], dram["sel"][:, 0:E])])
        units = [dict(up=up[:, :, k * 128:(k + 1) * 128], gate=None, down=down[:, k], n=128,
                      row=k // (HID // 128)) for k in range(E * HID // 128)]
        expert_mlps(nc, h, xn, gates, sel, "geluexp", units, ACT.Gelu_apprx_tanh, None, None, [])


INNER = 2 * D
IC = INNER // 128
STATES = 16
DCONV = 4
RANK = 12
MG = 2
MT = MG * N
MTILES = ITEMS // MG
SMALL = 1 / 32


def mamba(nc, dram, xn, mout, which):
    back = which == "b"
    FIRST = N - 1 if back else 0
    SILU_PIECES = 3 * IC
    PIECES = SILU_PIECES + 1 + IC + 2
    with Stage(nc, "mamba_" + which) as st:
        in_w = st.sb("in_w", [HALF, 2, 2 * INNER])
        x_w = st.sb("x_w", [128, IC, 128])
        dt_w = st.sb("dt_w", [RANK, INNER])
        out_w = st.sb("out_w", [128, IC, D])
        cols = st.sb("cols", [128, IC, DCONV + 3])
        A = st.sb("A", [128, IC, STATES])
        A_log = st.sb("A_log", [128, IC, STATES])
        ident = st.sb("ident", [128, 128])
        diag = st.sb("diag", [128, IC, DCONV, 128])
        sel = st.sb("sel", [128, 2 * STATES, 128], BF16)
        upad = st.sb("upad", [128, IC, MG, N + 2 * (DCONV - 1)])
        uc = st.sb("uc", [128, IC, MT])
        sz = st.sb("sz", [128, IC, MT])
        xd = st.sb("xd", [128, MT])
        xd_rest = st.sb("xd_rest", [128, MT])
        xd_part = st.sb("xd_part", [128, MT], BF16)
        parts = st.sb("parts", [128, MT], BF16)
        pre = st.sb("pre", [128, IC, MT])
        soft = st.sb("soft", [128, IC, MT])
        log = st.sb("log", [128, IC, MT])
        series = st.sb("series", [128, IC, MT])
        dt = st.sb("dt", [128, IC, MT])
        dtu = st.sb("dtu", [128, IC, MT])
        decay = st.sb("decay", [128, 2, IC, MG, N])
        inject = st.sb("inject", [128, 2, IC, MT])
        state = st.sb("state", [128, 2, IC, MT])
        seen = st.sb("seen", [128, 2, IC, MT])
        yd = st.sb("yd", [128, IC, MT])
        gated = st.sb("gated", [128, IC, MT])
        o = st.sb("o", [HALF, 2, MT])
        work_ps = st.ps("work_ps", [128, 512])
        y_ps = st.ps("y_ps", [128, IC, 512])
        b_ps = st.ps("b_ps", [128, 2, 512])
        c_ps = st.ps("c_ps", [128, 2, 512])
        names = ("loaded zeroed consts a_ready work_done work_read xd_split soft_step dt_step dt_ready dtu_ready bc_done "
                 "decay_ready inject_ready scanned seen_ready summed yd_ready gated_ready mout_ready").split()
        sem = {n: st.sem(n) for n in names}

        def tile(t):
            return ds(t * MT, MT)

        with nc.Block() as block:
            @block.sync
            def _(sp):
                for dst, src in ((in_w, which + "_in"), (x_w, which + "_x"), (dt_w, which + "_dt"),
                                 (out_w, which + "_out"), (cols, which + "_cols"), (A_log, which + "_A_log")):
                    sp.dma_start(dst[:], dram["mamba_" + src]).then_inc(sem["loaded"], 16)
                sp.dma_start(ident[:], dram["ident"]).then_inc(sem["loaded"], 16)
                sp.dma_start(sel[:], dram["state_sel"]).then_inc(sem["loaded"], 16)

            @block.gpsimd
            def _(pool):
                pool.memset(upad[:], 0.0).then_inc(sem["zeroed"], 1)
                pool.memset(decay[:], 0.0).then_inc(sem["zeroed"], 1)
                pool.wait_ge(sem["loaded"], 128)
                for c in range(IC):
                    for k in range(DCONV):
                        pool.tensor_scalar(diag[:, c, k, :], ident[:], cols[:, c, k:k + 1], None,
                                           ALU.mult).then_inc(sem["consts"], 1)

            @block.tensor
            def _(pe):
                pe.wait_ge(sem["loaded"], 128)
                pe.wait_ge(sem["consts"], IC * DCONV)

                def step(t, first):
                    w0 = t * PIECES

                    def piece(i):
                        if not first or i:
                            pe.wait_ge(sem["work_read"], w0 + i)

                    def broadcast(n):
                        pe.matmul(b_ps[:, n % 2, 0:MT], sel[:, n, :], parts[:], start=True, stop=True)
                        pe.matmul(c_ps[:, n % 2, 0:MT], sel[:, STATES + n, :], parts[:], start=True,
                                  stop=True).then_inc(sem["bc_done"], 1)

                    for i in range(2 * IC):
                        piece(i)
                        for j in range(2):
                            mm = pe.matmul(work_ps[:, 0:MT], in_w[:, j, i * 128:(i + 1) * 128], xn[:, j, tile(t)],
                                           start=(j == 0), stop=(j == 1))
                        mm.then_inc(sem["work_done"], 1)
                    for c in range(IC):
                        piece(2 * IC + c)
                        for k in range(DCONV):
                            shift = 2 * (DCONV - 1) - k if back else k
                            mm = pe.matmul(work_ps[:, 0:MT].rearrange("p (b n) -> p b n", b=MG), diag[:, c, k, :],
                                           upad[:, c, :, shift:shift + N], start=(k == 0), stop=(k == DCONV - 1))
                        mm.then_inc(sem["work_done"], 1)
                    piece(SILU_PIECES)
                    for c in range(IC):
                        mm = pe.matmul(work_ps[:, 0:MT], x_w[:, c, :], uc[:, c, :], start=(c == 0), stop=(c == IC - 1))
                    mm.then_inc(sem["work_done"], 1)
                    for c in range(IC):
                        piece(SILU_PIECES + 1 + c)
                        pe.matmul(work_ps[:, 0:MT], dt_w[:, c * 128:(c + 1) * 128], xd[0:RANK, :], start=True,
                                  stop=True).then_inc(sem["work_done"], 1)
                    pe.wait_ge(sem["xd_split"], 7 * t + 7)
                    broadcast(0)
                    for n in range(STATES):
                        if n + 1 < STATES:
                            broadcast(n + 1)
                        pe.wait_ge(sem["seen_ready"], t * STATES + n + 1)
                        for c in range(IC):
                            mm = pe.matmul(y_ps[:, c, 0:MT], ident[:], seen[:, n % 2, c, :], start=(n == 0),
                                           stop=(n == STATES - 1))
                        mm.then_inc(sem["summed"], 1)
                    pe.wait_ge(sem["gated_ready"], t + 1)
                    for m in range(2):
                        piece(PIECES - 2 + m)
                        for c in range(IC):
                            mm = pe.matmul(work_ps[0:HALF, 0:MT], out_w[:, c, m * HALF:(m + 1) * HALF], gated[:, c, :],
                                           start=(c == 0), stop=(c == IC - 1))
                        mm.then_inc(sem["work_done"], 1)

                steps(pe, MTILES, step)

            @block.scalar
            def _(act):
                act.wait_ge(sem["loaded"], 128)
                act.wait_ge(sem["zeroed"], 2)
                act.activation(A[:], A_log[:], ACT.Exp).then_inc(sem["a_ready"], 1)
                act.wait_ge(sem["a_ready"], 2)

                def step(t, first):
                    w0 = t * PIECES

                    def piece(i, out, func, src=None, **kw):
                        act.wait_ge(sem["work_done"], w0 + i + 1)
                        act.activation(out, work_ps[:, 0:MT] if src is None else src, func,
                                       **kw).then_inc(sem["work_read"], 1)

                    for c in range(IC):
                        piece(c, upad[:, c, :, DCONV - 1:DCONV - 1 + N], ACT.Copy,
                              src=work_ps[:, 0:MT].rearrange("p (b n) -> p b n", b=MG))
                    for c in range(IC):
                        piece(IC + c, sz[:, c, :], ACT.Silu)
                    if not first:
                        act.wait_ge(sem["dtu_ready"], t)
                    for c in range(IC):
                        piece(2 * IC + c, uc[:, c, :], ACT.Silu, bias=cols[:, c, DCONV:DCONV + 1])
                    if not first:
                        act.wait_ge(sem["xd_split"], 7 * t)
                    piece(SILU_PIECES, xd[:], ACT.Copy)
                    for c in range(IC):
                        piece(SILU_PIECES + 1 + c, pre[:, c, :], ACT.Identity, bias=cols[:, c, DCONV + 1:DCONV + 2])
                    act.wait_ge(sem["work_read"], w0 + SILU_PIECES + 1 + IC)
                    act.activation(soft[:], pre[:], ACT.Abs).then_inc(sem["soft_step"], 1)
                    act.wait_ge(sem["soft_step"], 3 * t + 1)
                    act.activation(soft[:], soft[:], ACT.Exp, scale=-1.0).then_inc(sem["soft_step"], 1)
                    act.wait_ge(sem["soft_step"], 3 * t + 2)
                    act.activation(log[:], soft[:], ACT.Ln, bias=1.0).then_inc(sem["soft_step"], 1)
                    act.wait_ge(sem["dt_ready"], t + 1)
                    for n in range(STATES):
                        if not first or n >= 2:
                            act.wait_ge(sem["scanned"], t * STATES + n - 1)
                        a, b = (0, N - 1) if back else (1, N)
                        for c in range(IC):
                            ins = act.activation(decay[:, n % 2, c, :, a:b],
                                                 dt[:, c, :].rearrange("p (b n) -> p b n", b=MG)[:, :, a:b],
                                                 ACT.Exp, scale=A[:, c, n:n + 1])
                        ins.then_inc(sem["decay_ready"], 1)
                    if not first:
                        act.wait_ge(sem["mout_ready"], t)
                    for m in range(2):
                        piece(PIECES - 2 + m, o[:, m, :], ACT.Copy, src=work_ps[0:HALF, 0:MT])

                steps(act, MTILES, step)

            @block.vector
            def _(dve):
                dve.wait_ge(sem["a_ready"], 1)
                dve.tensor_scalar(A[:], A[:], -1.0, None, ALU.mult).then_inc(sem["a_ready"], 1)

                def step(t, first):
                    w0 = t * PIECES
                    s0 = t * STATES

                    def inject_(n):
                        dve.wait_ge(sem["bc_done"], s0 + n + 1)
                        dve.tensor_tensor(inject[:, n % 2], dtu[:],
                                          b_ps[:, n % 2, 0:MT].unsqueeze(1).broadcast_to([128, IC, MT]),
                                          ALU.mult).then_inc(sem["inject_ready"], 1)

                    dve.wait_ge(sem["work_read"], w0 + SILU_PIECES + 1)
                    k = 7 * t

                    def split(i, ins):
                        ins.then_inc(sem["xd_split"], 1)
                        dve.wait_ge(sem["xd_split"], k + i)

                    split(1, dve.tensor_copy(xd_part[:], xd[:]))
                    split(2, dve.tensor_copy(parts[0:64, :], xd_part[0:64, :]))
                    split(3, dve.tensor_tensor(xd_rest[:], xd[:], xd_part[:], ALU.subtract))
                    split(4, dve.tensor_copy(xd_part[:], xd_rest[:]))
                    split(5, dve.tensor_copy(parts[64:96, :], xd_part[64:96, :]))
                    split(6, dve.tensor_tensor(xd_rest[:], xd_rest[:], xd_part[:], ALU.subtract))
                    split(7, dve.tensor_copy(parts[96:128, :], xd_rest[96:128, :]))
                    dve.wait_ge(sem["soft_step"], 3 * t + 3)
                    k2 = 7 * t

                    def soften(i, ins):
                        ins.then_inc(sem["dt_step"], 1)
                        dve.wait_ge(sem["dt_step"], k2 + i)

                    soften(1, dve.tensor_scalar(series[:], soft[:], -0.25, None, ALU.mult))
                    for i, coefficient in ((2, 1 / 3), (3, -0.5), (4, 1.0)):
                        soften(i, dve.scalar_tensor_tensor(out=series[:], in0=series[:], scalar=coefficient,
                                                           in1=soft[:], op0=ALU.add, op1=ALU.mult))
                    soften(5, dve.scalar_tensor_tensor(out=series[:], in0=soft[:], scalar=SMALL, in1=series[:],
                                                       op0=ALU.is_lt, op1=ALU.mult))
                    soften(6, dve.scalar_tensor_tensor(out=log[:], in0=soft[:], scalar=SMALL, in1=log[:],
                                                       op0=ALU.is_ge, op1=ALU.mult))
                    soften(7, dve.tensor_tensor(log[:], log[:], series[:], ALU.add))
                    dve.scalar_tensor_tensor(out=dt[:], in0=pre[:], scalar=0.0, in1=log[:], op0=ALU.max,
                                             op1=ALU.add).then_inc(sem["dt_ready"], 1)
                    dve.wait_ge(sem["dt_ready"], t + 1)
                    dve.tensor_tensor(dtu[:], dt[:], uc[:], ALU.mult).then_inc(sem["dtu_ready"], 1)
                    dve.wait_ge(sem["dtu_ready"], t + 1)
                    inject_(0)
                    for n in range(STATES):
                        flat = [x[:, n % 2].rearrange(p, **kw) for x, p, kw in (
                            (state, "p c n -> p (c n)", {}), (decay, "p c b n -> p (c b n)", {}),
                            (inject, "p c n -> p (c n)", {}))]
                        if back:
                            flat = [x[:, ::-1] for x in flat]
                        dve.wait_ge(sem["decay_ready"], s0 + n + 1)
                        dve.wait_ge(sem["inject_ready"], s0 + n + 1)
                        dve.tensor_tensor_scan(flat[0], flat[1], flat[2], 0.0, ALU.mult,
                                               ALU.add).then_inc(sem["scanned"], 1)
                        if n + 1 < STATES:
                            inject_(n + 1)
                        dve.wait_ge(sem["scanned"], s0 + n + 1)
                        if not first or n >= 2:
                            dve.wait_ge(sem["summed"], s0 + n - 1)
                        dve.tensor_tensor(seen[:, n % 2], state[:, n % 2],
                                          c_ps[:, n % 2, 0:MT].unsqueeze(1).broadcast_to([128, IC, MT]),
                                          ALU.mult).then_inc(sem["seen_ready"], 1)
                    dve.wait_ge(sem["summed"], s0 + STATES)
                    for c in range(IC):
                        dve.scalar_tensor_tensor(out=yd[:, c, :], in0=uc[:, c, :], scalar=cols[:, c, DCONV + 2:DCONV + 3],
                                                 in1=y_ps[:, c, 0:MT], op0=ALU.mult,
                                                 op1=ALU.add).then_inc(sem["yd_ready"], 1)
                    dve.wait_ge(sem["yd_ready"], IC * (t + 1))
                    dve.tensor_tensor(gated[:], yd[:], sz[:], ALU.mult).then_inc(sem["gated_ready"], 1)
                    dve.wait_ge(sem["work_read"], w0 + PIECES)
                    base = mout if back else xn
                    dve.tensor_tensor(mout[:, :, tile(t)], o[:], base[:, :, tile(t)],
                                      ALU.add).then_inc(sem["mout_ready"], 1)

                steps(dve, MTILES, step)


def add_normed(nc, dram, h, mout):
    with Stage(nc, "addnorm") as st:
        averager = st.sb("averager", [HALF, HALF])
        eps = st.sb("eps", [HALF, 1])
        cols = st.sb("cols", [HALF, 2, 2])
        centred = st.sb("centred", [HALF, 2, TILE])
        squared = st.sb("squared", [HALF, 2, TILE])
        std = st.sb("std", [HALF, TILE])
        rstd = st.sb("rstd", [HALF, TILE])
        normed = st.sb("normed", [HALF, 2, TILE])
        scaled = st.sb("scaled", [HALF, 2, TILE])
        mean_ps = st.ps("mean", [HALF, 512])
        var_ps = st.ps("var", [HALF, 512])
        names = ("loaded consts mean_ready centred_ready squared_ready var_ready std_ready rstd_ready "
                 "normed_ready scaled_ready h_ready").split()
        sem = {n: st.sem(n) for n in names}
        with nc.Block() as block:
            @block.sync
            def _(sp):
                sp.dma_start(cols[:], dram["mamba_norm_cols"]).then_inc(sem["loaded"], 16)

            @block.gpsimd
            def _(pool):
                pool.memset(averager[:], 1.0 / D).then_inc(sem["consts"], 1)
                pool.memset(eps[:], 1e-12).then_inc(sem["consts"], 1)

            @block.tensor
            def _(pe):
                pe.wait_ge(sem["consts"], 2)
                for t in range(TILES):
                    for j in range(2):
                        mm = pe.matmul(mean_ps[:, 0:TILE], averager[:], mout[:, j, t * TILE:(t + 1) * TILE],
                                       start=(j == 0), stop=(j == 1))
                    mm.then_inc(sem["mean_ready"], 1)
                    pe.wait_ge(sem["squared_ready"], t + 1)
                    if t:
                        pe.wait_ge(sem["std_ready"], t)
                    for j in range(2):
                        mm = pe.matmul(var_ps[:, 0:TILE], averager[:], squared[:, j, :],
                                       start=(j == 0), stop=(j == 1))
                    mm.then_inc(sem["var_ready"], 1)

            @block.scalar
            def _(act):
                act.wait_ge(sem["consts"], 2)
                act.wait_ge(sem["loaded"], 16)
                for t in range(TILES):
                    act.wait_ge(sem["centred_ready"], t + 1)
                    act.activation(squared[:], centred[:], ACT.Square).then_inc(sem["squared_ready"], 1)
                    act.wait_ge(sem["var_ready"], t + 1)
                    if t:
                        act.wait_ge(sem["rstd_ready"], t)
                    act.activation(std[:], var_ps[:, 0:TILE], ACT.Sqrt, bias=eps[:]).then_inc(sem["std_ready"], 1)
                    act.wait_ge(sem["normed_ready"], t + 1)
                    if t:
                        act.wait_ge(sem["h_ready"], t)
                    for m in range(2):
                        act.activation(scaled[:, m, :], normed[:, m, :], ACT.Identity, bias=cols[:, 1, m:m + 1],
                                       scale=cols[:, 0, m:m + 1]).then_inc(sem["scaled_ready"], 1)

            @block.vector
            def _(dve):
                for t in range(TILES):
                    part = slice(t * TILE, (t + 1) * TILE)
                    dve.wait_ge(sem["mean_ready"], t + 1)
                    dve.tensor_tensor(centred[:], mout[:, :, part],
                                      mean_ps[:, 0:TILE].unsqueeze(1).broadcast_to([HALF, 2, TILE]),
                                      ALU.subtract).then_inc(sem["centred_ready"], 1)
                    dve.wait_ge(sem["std_ready"], t + 1)
                    dve.reciprocal(rstd[:], std[:]).then_inc(sem["rstd_ready"], 1)
                    dve.wait_ge(sem["rstd_ready"], t + 1)
                    dve.tensor_tensor(normed[:], centred[:], rstd[:].unsqueeze(1).broadcast_to([HALF, 2, TILE]),
                                      ALU.mult).then_inc(sem["normed_ready"], 1)
                    dve.wait_ge(sem["scaled_ready"], 2 * t + 2)
                    dve.tensor_tensor(h[:, :, part], h[:, :, part], scaled[:], ALU.add).then_inc(sem["h_ready"], 1)


def bidirectional_mamba(nc, dram, h, xn):
    with nc.sbuf_tensor("mout", [HALF, 2, T], F32) as mout:
        mamba(nc, dram, xn, mout, "f")
        mamba(nc, dram, xn, mout, "b")
        add_normed(nc, dram, h, mout)


def quantised_mlp(nc, dram, h, xn):
    HID = 768
    K = HID // 128
    LOW, HIGH = -8.0, 7.0
    ROUND = 1.5 * 2.0 ** 23
    with Stage(nc, "quant") as st:
        w1 = st.sb("w1", [HALF, 2, HID])
        w2 = st.sb("w2", [128, K, D])
        step_w1 = st.sb("step_w1", [HALF, HID])
        step_w2 = st.sb("step_w2", [128, D])
        inv_w1 = st.sb("inv_w1", [HALF, HID])
        inv_w2 = st.sb("inv_w2", [128, D])
        w1q = st.sb("w1q", [HALF, 2, HID], BF16)
        w2q = st.sb("w2q", [128, K, D], BF16)
        step_a1 = st.sb("step_a1", [HALF, 2])
        step_a2 = st.sb("step_a2", [HALF, HID // HALF])
        hid_cols = st.sb("hid_cols", [128, 2, K])
        out_cols = st.sb("out_cols", [HALF, 2, 2])
        ones = st.sb("ones", [HALF, 128])
        step_a = st.sb("step_a", [128, 2])
        inv_a = st.sb("inv_a", [128, 2])
        scale1 = st.sb("scale1", [128, K])
        scale2 = st.sb("scale2", [HALF, 2])
        xs = st.sb("xs", [HALF, 2, T])
        xq = st.sb("xq", [HALF, 2, T], BF16)
        g = st.sb("g", [128, K, TILE])
        gs = st.sb("gs", [128, K, TILE])
        gq = st.sb("gq", [128, K, TILE], BF16)
        y = st.sb("y", [HALF, 2, TILE])
        mean_ps = st.ps("mean_ps", [128, 2])
        up_ps = st.ps("up_ps", [128, 2, 512])
        y_ps = st.ps("y_ps", [HALF, 2, 512])
        loaded = st.sem("loaded")
        ones_ready = st.sem("ones_ready")
        mean_done = st.sem("mean_done")
        chain = st.sem("chain")
        ready = st.sem("ready")
        up_done = st.sem("up_done")
        g_ready = st.sem("g_ready")
        gq_step = st.sem("gq_step")
        gq_ready = st.sem("gq_ready")
        down_done = st.sem("down_done")
        y_ready = st.sem("y_ready")
        h_ready = st.sem("h_ready")
        with nc.Block() as block:
            @block.sync
            def _(sp):
                for dst, src in ((step_a1, "quant_a1"), (step_a2, "quant_a2"), (w1, "quant_w1"), (w2, "quant_w2"),
                                 (hid_cols, "quant_hid"), (out_cols, "quant_out")):
                    sp.dma_start(dst[:], dram[src]).then_inc(loaded, 16)
                sp.dma_start(step_w1[:], dram["quant_step_w1"].broadcast_to([HALF, HID])).then_inc(loaded, 16)
                sp.dma_start(step_w2[:], dram["quant_step_w2"].broadcast_to([128, D])).then_inc(loaded, 16)

            @block.gpsimd
            def _(pool):
                pool.memset(ones[:], 1.0).then_inc(ones_ready, 1)

            @block.tensor
            def _(pe):
                pe.wait_ge(loaded, 128)
                pe.wait_ge(ones_ready, 1)
                for i, steps_in in enumerate((step_a1, step_a2)):
                    n = steps_in[:].shape[1]
                    for j in range(n):
                        mm = pe.matmul(mean_ps[:, i:i + 1], ones[:], steps_in[:, j:j + 1],
                                       start=(j == 0), stop=(j == n - 1))
                mm.then_inc(mean_done, 1)
                pe.wait_ge(ready, 1)

                def step(t, first):
                    for k in range(K):
                        if not first or k >= 2:
                            pe.wait_ge(g_ready, t * K + k - 1)
                        for j in range(2):
                            mm = pe.matmul(up_ps[:, k % 2, 0:TILE], w1q[:, j, k * 128:(k + 1) * 128],
                                           xq[:, j, ds(t * TILE, TILE)], start=(j == 0), stop=(j == 1))
                        mm.then_inc(up_done, 1)
                    pe.wait_ge(gq_ready, t + 1)
                    if not first:
                        pe.wait_ge(y_ready, 2 * t)
                    for m in range(2):
                        for k in range(K):
                            mm = pe.matmul(y_ps[:, m, 0:TILE], w2q[:, k, m * HALF:(m + 1) * HALF], gq[:, k, :],
                                           start=(k == 0), stop=(k == K - 1))
                    mm.then_inc(down_done, 1)

                steps(pe, TILES, step)

            @block.scalar
            def _(act):
                act.wait_ge(ready, 1)

                def step(t, first):
                    if not first:
                        act.wait_ge(gq_step, 3 * t)
                    for k in range(K):
                        act.wait_ge(up_done, t * K + k + 1)
                        act.activation(g[:, k, :], up_ps[:, k % 2, 0:TILE], ACT.Gelu, bias=hid_cols[:, 1, k:k + 1],
                                       scale=scale1[:, k:k + 1]).then_inc(g_ready, 1)
                    act.wait_ge(down_done, t + 1)
                    if not first:
                        act.wait_ge(h_ready, t)
                    for m in range(2):
                        act.activation(y[:, m, :], y_ps[:, m, 0:TILE], ACT.Identity, bias=out_cols[:, 1, m:m + 1],
                                       scale=scale2[:, m:m + 1]).then_inc(y_ready, 1)

                steps(act, TILES, step)

            @block.vector
            def _(dve):
                count = [0]

                def link(ins):
                    count[0] += 1
                    ins.then_inc(chain, 1)
                    dve.wait_ge(chain, count[0])

                def quantise(out, scaled):
                    link(dve.tensor_scalar(scaled, scaled, HIGH, LOW, ALU.min, ALU.max))
                    link(dve.tensor_scalar(out, scaled, ROUND, ROUND, ALU.add, ALU.subtract))

                dve.wait_ge(loaded, 128)
                link(dve.reciprocal(inv_w1[:], step_w1[:]))
                link(dve.reciprocal(inv_w2[:], step_w2[:]))
                link(dve.tensor_tensor(w1[:], w1[:], inv_w1[:].unsqueeze(1).broadcast_to([HALF, 2, HID]), ALU.mult))
                quantise(w1q[:], w1[:])
                link(dve.tensor_tensor(w2[:], w2[:], inv_w2[:].unsqueeze(1).broadcast_to([128, K, D]), ALU.mult))
                quantise(w2q[:], w2[:])
                dve.wait_ge(mean_done, 1)
                link(dve.tensor_scalar(step_a[:, 0:1], mean_ps[:, 0:1], 1.0 / D, None, ALU.mult))
                link(dve.tensor_scalar(step_a[:, 1:2], mean_ps[:, 1:2], 1.0 / HID, None, ALU.mult))
                link(dve.reciprocal(inv_a[:], step_a[:]))
                link(dve.tensor_scalar(scale1[:], hid_cols[:, 0], step_a[:, 0:1], None, ALU.mult))
                link(dve.tensor_scalar(scale2[:], out_cols[:, 0], step_a[0:HALF, 1:2], None, ALU.mult))
                link(dve.tensor_scalar(xs[:], xn[:], inv_a[0:HALF, 0:1], None, ALU.mult))
                quantise(xq[:], xs[:])
                dve.nop().then_inc(ready, 1)

                def step(t, first):
                    dve.wait_ge(g_ready, (t + 1) * K)
                    dve.tensor_scalar(g[:], g[:], 10.0, -10.0, ALU.min, ALU.max).then_inc(gq_step, 1)
                    dve.wait_ge(gq_step, 3 * t + 1)
                    dve.tensor_scalar(gs[:], g[:], inv_a[:, 1:2], HIGH, ALU.mult, ALU.min).then_inc(gq_step, 1)
                    dve.wait_ge(gq_step, 3 * t + 2)
                    dve.tensor_scalar(gs[:], gs[:], LOW, ROUND, ALU.max, ALU.add).then_inc(gq_step, 1)
                    dve.wait_ge(gq_step, 3 * t + 3)
                    if not first:
                        dve.wait_ge(down_done, t)
                    dve.tensor_scalar(gq[:], gs[:], ROUND, None, ALU.subtract).then_inc(gq_ready, 1)
                    dve.wait_ge(y_ready, 2 * t + 2)
                    tile = h[:, :, ds(t * TILE, TILE)]
                    dve.tensor_tensor(tile, tile, y[:], ALU.add).then_inc(h_ready, 1)

                steps(dve, TILES, step)


CUT = ((0, 65), (65, 64))
QCUT = ((0, 65), (64, 65))


def group_attention(nc, dram, h, xn):
    GP = 49
    SCALE = D ** -0.5
    with Stage(nc, "groupattn") as st:
        w_qkv = st.sb("w_qkv", [HALF, 2, 3 * D])
        w_proj = st.sb("w_proj", [HALF, 2, D])
        w_gp = st.sb("w_gp", [HALF, 2, GP])
        cols = st.sb("cols", [HALF, 3, 2])
        v_bias = st.sb("v_bias", [65, D])
        ident = st.sb("ident", [65, 65])
        a = st.sb("a", [65, 4])
        x = st.sb("x", [HALF, 2, N])
        q = st.sb("q", [HALF, 2, N])
        k = st.sb("k", [HALF, 2, N])
        v = st.sb("v", [65, 2, D])
        g_in = st.sb("g_in", [65, 2, GP])
        g_top = st.sb("g_top", [65, 2])
        g_sum = st.sb("g_sum", [65, 2])
        g_inv = st.sb("g_inv", [65, 2])
        gw = st.sb("gw", [65, 2, GP])
        gwt = st.sb("gwt", [GP, N])
        top = st.sb("top", [65, 2])
        bias = st.sb("bias", [65, 2])
        total = st.sb("total", [65, 2])
        inv = st.sb("inv", [65, 2])
        e = st.sb("e", [65, 2, N])
        mix = st.sb("mix", [65, 2, N])
        wt = st.sb("wt", [65, 2, N])
        wtt = st.sb("wtt", [65, 2, N])
        heads = st.sb("heads", [HALF, 2, N])
        bank_a = st.ps("bank_a", [128, 512])
        bank_b = st.ps("bank_b", [128, 512])
        bank_c = st.ps("bank_c", [128, 512])
        bank_d = st.ps("bank_d", [128, 512])
        bank_e = st.ps("bank_e", [128, 512])
        bank_f = st.ps("bank_f", [128, 512])

        def view(bank, p, a_, b_):
            return bank[0:p, 0:a_ * b_].rearrange("p (a b) -> p a b", a=a_)

        q_ps = view(bank_a, HALF, 2, N)
        group_ps = view(bank_a, 65, 2, N)
        k_ps = view(bank_b, HALF, 2, N)
        out_ps = view(bank_b, HALF, 2, N)
        v_ps = view(bank_c, 65, 2, D)
        o_ps = view(bank_c, HALF, 2, N)
        g_ps = view(bank_d, 65, 2, GP)
        gwt_ps = bank_d[0:GP, 0:N]
        s_ps = view(bank_e, 65, 2, N)
        wtt_ps = view(bank_f, 65, 2, N)
        names = ("loaded x_ready qkv_done q_ready k_ready v_ready g_done g_top g_in g_exp g_sum g_inv gw_ready "
                 "gwt_done gwt_ready s_done top_ready bias_ready e_ready inv_ready group_done mix_ready wt_ready "
                 "wtt_done wtt_ready out_done heads_ready proj_done h_ready a_step").split()
        sem = {n: st.sem(n) for n in names}
        with nc.Block() as block:
            @block.sync
            def _(sp):
                for dst, src in ((w_qkv, "groupattn_qkv"), (w_proj, "groupattn_proj"), (w_gp, "groupattn_gp"),
                                 (cols, "groupattn_cols")):
                    sp.dma_start(dst[:], dram[src]).then_inc(sem["loaded"], 16)
                sp.dma_start(v_bias[:], dram["groupattn_v_bias"].broadcast_to([65, D])).then_inc(sem["loaded"], 16)
                sp.dma_start(a[:, 0:1], dram["groupattn_alpha"].broadcast_to([65, 1])).then_inc(sem["loaded"], 16)
                sp.dma_start(ident[:], dram["ident"][0:65, 0:65]).then_inc(sem["loaded"], 16)

            @block.gpsimd
            def _(pool):
                def step(b, first):
                    if not first:
                        pool.wait_ge(sem["qkv_done"], b)
                    pool.tensor_copy(x[:], xn[:, :, ds(b * N, N)]).then_inc(sem["x_ready"], 1)

                steps(pool, ITEMS, step)

            @block.tensor
            def _(pe):
                pe.wait_ge(sem["loaded"], 112)

                def step(b, first):
                    pe.wait_ge(sem["x_ready"], b + 1)
                    if not first:
                        pe.wait_ge(sem["h_ready"], 2 * b)
                    for ps, w0 in ((q_ps, 0), (k_ps, D)):
                        for m in range(2):
                            for j in range(2):
                                pe.matmul(ps[:, m, :], w_qkv[:, j, w0 + m * HALF:w0 + (m + 1) * HALF], x[:, j, :],
                                          start=(j == 0), stop=(j == 1))
                    for c, (c0, n) in enumerate(CUT):
                        for j in range(2):
                            mm = pe.matmul(v_ps[0:n, c, :], x[:, j, c0:c0 + n], w_qkv[:, j, 2 * D:],
                                           start=(j == 0), stop=(j == 1))
                    mm.then_inc(sem["qkv_done"], 1)
                    pe.wait_ge(sem["q_ready"], 2 * b + 2)
                    for c, (c0, n) in enumerate(CUT):
                        for j in range(2):
                            mm = pe.matmul(g_ps[0:n, c, :], q[:, j, c0:c0 + n], w_gp[:, j, :],
                                           start=(j == 0), stop=(j == 1))
                    mm.then_inc(sem["g_done"], 1)
                    pe.wait_ge(sem["k_ready"], 2 * b + 2)
                    for c, (c0, n) in enumerate(CUT):
                        for j in range(2):
                            mm = pe.matmul(s_ps[0:n, c, :], q[:, j, c0:c0 + n], k[:, j, :],
                                           start=(j == 0), stop=(j == 1))
                    mm.then_inc(sem["s_done"], 1)
                    pe.wait_ge(sem["loaded"], 112)
                    pe.wait_ge(sem["gw_ready"], 2 * b + 2)
                    for c, (c0, n) in enumerate(CUT):
                        mm = pe.transpose(gwt_ps[:, c0:c0 + n], gw[0:n, c, :], ident[0:n, 0:n])
                    mm.then_inc(sem["gwt_done"], 1)
                    pe.wait_ge(sem["gwt_ready"], b + 1)
                    for c, (c0, n) in enumerate(CUT):
                        mm = pe.matmul(group_ps[0:n, c, :], gwt[:, c0:c0 + n], gwt[:], start=True, stop=True)
                    mm.then_inc(sem["group_done"], 1)
                    pe.wait_ge(sem["loaded"], 112)
                    pe.wait_ge(sem["wt_ready"], 2 * b + 2)
                    for c, (c0, n) in enumerate(CUT):
                        for d, (d0, l) in enumerate(CUT):
                            mm = pe.transpose(wtt_ps[0:l, d, c0:c0 + n], wt[0:n, c, d0:d0 + l], ident[0:n, 0:n])
                    mm.then_inc(sem["wtt_done"], 1)
                    pe.wait_ge(sem["v_ready"], 2 * b + 2)
                    pe.wait_ge(sem["wtt_ready"], 2 * b + 2)
                    for m in range(2):
                        for d, (d0, l) in enumerate(CUT):
                            mm = pe.matmul(out_ps[:, m, :], v[0:l, d, m * HALF:(m + 1) * HALF], wtt[0:l, d, :],
                                           start=(d == 0), stop=(d == 1))
                    mm.then_inc(sem["out_done"], 1)
                    pe.wait_ge(sem["heads_ready"], b + 1)
                    for m in range(2):
                        for j in range(2):
                            mm = pe.matmul(o_ps[:, m, :], w_proj[:, j, m * HALF:(m + 1) * HALF], heads[:, j, :],
                                           start=(j == 0), stop=(j == 1))
                    mm.then_inc(sem["proj_done"], 1)

                steps(pe, ITEMS, step)

            @block.scalar
            def _(act):
                act.wait_ge(sem["loaded"], 112)
                act.activation(a[:, 1:2], a[:, 0:1], ACT.Exp, scale=-1.0).then_inc(sem["a_step"], 1)

                def step(b, first):
                    act.wait_ge(sem["qkv_done"], b + 1)
                    for m in range(2):
                        act.activation(q[:, m, :], q_ps[:, m, :], ACT.Identity,
                                       bias=cols[:, 0, m:m + 1]).then_inc(sem["q_ready"], 1)
                    act.wait_ge(sem["g_in"], 2 * b + 2)
                    for c, (c0, n) in enumerate(CUT):
                        act.activation(g_in[0:n, c, :], g_in[0:n, c, :], ACT.Exp,
                                       accum_out=g_sum[0:n, c:c + 1]).then_inc(sem["g_exp"], 1)
                    act.wait_ge(sem["bias_ready"], 2 * b + 2)
                    for c, (c0, n) in enumerate(CUT):
                        act.activation(e[0:n, c, :], s_ps[0:n, c, :], ACT.Exp, bias=bias[0:n, c:c + 1], scale=SCALE,
                                       accum_out=total[0:n, c:c + 1]).then_inc(sem["e_ready"], 1)
                    act.wait_ge(sem["gwt_done"], b + 1)
                    act.activation(gwt[:], gwt_ps, ACT.Copy).then_inc(sem["gwt_ready"], 1)
                    act.wait_ge(sem["wtt_done"], b + 1)
                    for d, (d0, l) in enumerate(CUT):
                        act.activation(wtt[0:l, d, :], wtt_ps[0:l, d, :], ACT.Copy).then_inc(sem["wtt_ready"], 1)
                    act.wait_ge(sem["out_done"], b + 1)
                    act.activation(heads[:], out_ps, ACT.Copy).then_inc(sem["heads_ready"], 1)

                steps(act, ITEMS, step)

            @block.vector
            def _(dve):
                dve.wait_ge(sem["a_step"], 1)
                dve.tensor_scalar(a[:, 3:4], a[:, 1:2], 1.0, None, ALU.add).then_inc(sem["a_step"], 1)
                dve.wait_ge(sem["a_step"], 2)
                dve.reciprocal(a[:, 2:3], a[:, 3:4]).then_inc(sem["a_step"], 1)
                dve.wait_ge(sem["a_step"], 3)
                dve.tensor_scalar(a[:, 3:4], a[:, 2:3], -1.0, 1.0, ALU.mult, ALU.add).then_inc(sem["a_step"], 1)
                dve.wait_ge(sem["a_step"], 4)

                def step(b, first):
                    dve.wait_ge(sem["qkv_done"], b + 1)
                    for m in range(2):
                        dve.tensor_scalar(k[:, m, :], k_ps[:, m, :], cols[:, 1, m:m + 1], None,
                                          ALU.add).then_inc(sem["k_ready"], 1)
                    for c, (c0, n) in enumerate(CUT):
                        dve.tensor_tensor(v[0:n, c, :], v_ps[0:n, c, :], v_bias[0:n, :],
                                          ALU.add).then_inc(sem["v_ready"], 1)
                    dve.wait_ge(sem["g_done"], b + 1)
                    for c, (c0, n) in enumerate(CUT):
                        dve.tensor_reduce(g_top[0:n, c:c + 1], g_ps[0:n, c, :], AX.X, ALU.max).then_inc(sem["g_top"], 1)
                    dve.wait_ge(sem["g_top"], 2 * b + 2)
                    for c, (c0, n) in enumerate(CUT):
                        dve.tensor_scalar(g_in[0:n, c, :], g_ps[0:n, c, :], g_top[0:n, c:c + 1], None,
                                          ALU.subtract).then_inc(sem["g_in"], 1)
                    dve.wait_ge(sem["s_done"], b + 1)
                    for c, (c0, n) in enumerate(CUT):
                        dve.tensor_reduce(top[0:n, c:c + 1], s_ps[0:n, c, :], AX.X, ALU.max).then_inc(sem["top_ready"], 1)
                    dve.wait_ge(sem["top_ready"], 2 * b + 2)
                    for c, (c0, n) in enumerate(CUT):
                        dve.tensor_scalar(bias[0:n, c:c + 1], top[0:n, c:c + 1], -SCALE, None,
                                          ALU.mult).then_inc(sem["bias_ready"], 1)
                    dve.wait_ge(sem["g_exp"], 2 * b + 2)
                    for c, (c0, n) in enumerate(CUT):
                        dve.reciprocal(g_inv[0:n, c:c + 1], g_sum[0:n, c:c + 1]).then_inc(sem["g_inv"], 1)
                    dve.wait_ge(sem["g_inv"], 2 * b + 2)
                    for c, (c0, n) in enumerate(CUT):
                        dve.tensor_scalar(gw[0:n, c, :], g_in[0:n, c, :], g_inv[0:n, c:c + 1], None,
                                          ALU.mult).then_inc(sem["gw_ready"], 1)
                    dve.wait_ge(sem["e_ready"], 2 * b + 2)
                    for c, (c0, n) in enumerate(CUT):
                        dve.reciprocal(inv[0:n, c:c + 1], total[0:n, c:c + 1]).then_inc(sem["inv_ready"], 1)
                    dve.wait_ge(sem["group_done"], b + 1)
                    for c, (c0, n) in enumerate(CUT):
                        dve.tensor_scalar(mix[0:n, c, :], group_ps[0:n, c, :], a[0:n, 3:4], a[0:n, 2:3], ALU.mult,
                                          ALU.add).then_inc(sem["mix_ready"], 1)
                    dve.wait_ge(sem["inv_ready"], 2 * b + 2)
                    dve.wait_ge(sem["mix_ready"], 2 * b + 2)
                    for c, (c0, n) in enumerate(CUT):
                        dve.scalar_tensor_tensor(out=wt[0:n, c, :], in0=e[0:n, c, :], scalar=inv[0:n, c:c + 1],
                                                 in1=mix[0:n, c, :], op0=ALU.mult,
                                                 op1=ALU.mult).then_inc(sem["wt_ready"], 1)
                    dve.wait_ge(sem["proj_done"], b + 1)
                    for m in range(2):
                        cols_b = h[:, m, ds(b * N, N)]
                        dve.scalar_tensor_tensor(out=cols_b, in0=o_ps[:, m, :], scalar=cols[:, 2, m:m + 1],
                                                 in1=cols_b, op0=ALU.add, op1=ALU.add).then_inc(sem["h_ready"], 1)

                steps(dve, ITEMS, step)


def collaborative_attention(nc, dram, h, xn):
    H, HEAD = 12, 16
    SCALE = HEAD ** -0.5
    R = (HALF + H, HALF)
    HG = 6
    ROUNDS = [(c, g) for c in range(2) for g in range(2)]
    with Stage(nc, "collab") as st:
        w_q = st.sb("w_q", [HALF, 2, D])
        w_k = st.sb("w_k", [HALF, 2, D + H])
        w_v = st.sb("w_v", [HALF, 2, D])
        w_proj = st.sb("w_proj", [HALF, 2, D])
        mixing = st.sb("mixing", [R[0], 2, H])
        cols = st.sb("cols", [HALF, 1, 2])
        v_bias = st.sb("v_bias", [65, D])
        ident = st.sb("ident", [65, 65])
        x = st.sb("x", [HALF, 2, N])
        q = st.sb("q", [R[0], 2, N])
        keys = st.sb("keys", [R[0], 2, H, N])
        v1 = st.sb("v1", [65, 2, H, HEAD + 1])
        top = st.sb("top", [65, 2, HG])
        e = st.sb("e", [65, 2, HG, N])
        et = st.sb("et", [65, 2, HG, 65])
        inv = st.sb("inv", [65, 2, H])
        att = st.sb("att", [65, 2, H, HEAD])
        heads = st.sb("heads", [HALF, 2, N])
        s_ps = [st.ps(f"s_ps{i}", [65, 2, 512]) for i in range(2)]
        et_ps = st.ps("et_ps", [128, 2, 512])
        bank_a = st.ps("bank_a", [128, 512])
        bank_b = st.ps("bank_b", [128, 512])

        def view(bank, p, a_, b_):
            return bank[0:p, 0:a_ * b_].rearrange("p (a b) -> p a b", a=a_)

        q_ps = view(bank_a, HALF, 2, N)
        av_ps = bank_a[0:65, 0:2 * H * (HEAD + 1)].rearrange("p (c h d) -> p c h d", c=2, h=H)
        o_ps = view(bank_a, HALF, 2, N)
        k_ps = view(bank_b, R[0], 2, N)
        heads_ps = view(bank_b, HALF, 2, N)
        v_ps = et_ps[0:65, 0, 0:2 * D].rearrange("p (c f) -> p c f", c=2)
        names = ("loaded ones_ready x_ready qkv_done q_ready keys_ready v_ready s_done top_ready shifted e_ready "
                 "et_done et_ready av_done inv_ready att_ready heads_done heads_ready proj_done h_ready").split()
        sem = {n: st.sem(n) for n in names}
        with nc.Block() as block:
            @block.sync
            def _(sp):
                for dst, src in ((w_q, "collab_q"), (w_k, "collab_k"), (w_v, "collab_v"), (w_proj, "collab_proj"),
                                 (mixing, "collab_mixing"), (cols, "collab_cols")):
                    sp.dma_start(dst[:], dram[src]).then_inc(sem["loaded"], 16)
                sp.dma_start(v_bias[:], dram["collab_v_bias"].broadcast_to([65, D])).then_inc(sem["loaded"], 16)
                sp.dma_start(ident[:], dram["ident"][0:65, 0:65]).then_inc(sem["loaded"], 16)

            @block.gpsimd
            def _(pool):
                pool.memset(v1[:, :, :, HEAD:], 1.0).then_inc(sem["ones_ready"], 1)
                pool.memset(q[HALF:R[0], 0, :], 1.0).then_inc(sem["ones_ready"], 1)

                def step(b, first):
                    if not first:
                        pool.wait_ge(sem["qkv_done"], b)
                    pool.tensor_copy(x[:], xn[:, :, ds(b * N, N)]).then_inc(sem["x_ready"], 1)

                steps(pool, ITEMS, step)

            @block.tensor
            def _(pe):
                pe.wait_ge(sem["loaded"], 128)
                pe.wait_ge(sem["ones_ready"], 2)

                def step(b, first):
                    def scores(r):
                        c, g = ROUNDS[r]
                        c0, n = QCUT[c]
                        if not first or r >= 2:
                            pe.wait_ge(sem["shifted"], 4 * b + r - 1)
                        for i in range(2):
                            for j in range(2):
                                f = g * HG + 3 * i
                                mm = pe.matmul(s_ps[r % 2][0:n, i, 0:3 * N], q[0:R[j], j, c0:c0 + n],
                                               keys[0:R[j], j, f:f + 3, :].rearrange("p h n -> p (h n)"),
                                               start=(j == 0), stop=(j == 1))
                        mm.then_inc(sem["s_done"], 1)

                    pe.wait_ge(sem["x_ready"], b + 1)
                    if not first:
                        pe.wait_ge(sem["h_ready"], 2 * b)
                    for m in range(2):
                        for j in range(2):
                            pe.matmul(q_ps[:, m, :], w_q[:, j, m * HALF:(m + 1) * HALF], x[:, j, :],
                                      start=(j == 0), stop=(j == 1))
                    for m in range(2):
                        for j in range(2):
                            w = w_k[:, j, 0:R[0]] if m == 0 else w_k[:, j, R[0]:]
                            pe.matmul(k_ps[0:R[m], m, :], w, x[:, j, :], start=(j == 0), stop=(j == 1))
                    for c, (c0, n) in enumerate(CUT):
                        for j in range(2):
                            mm = pe.matmul(v_ps[0:n, c, :], x[:, j, c0:c0 + n], w_v[:, j, :],
                                           start=(j == 0), stop=(j == 1))
                    mm.then_inc(sem["qkv_done"], 1)
                    pe.wait_ge(sem["q_ready"], b + 1)
                    pe.wait_ge(sem["keys_ready"], 2 * b + 2)
                    scores(0)
                    pe.wait_ge(sem["v_ready"], 2 * b + 2)
                    for r, (c, g) in enumerate(ROUNDS):
                        n = QCUT[c][1]
                        if r + 1 < len(ROUNDS):
                            scores(r + 1)
                        pe.wait_ge(sem["loaded"], 128)
                        pe.wait_ge(sem["e_ready"], 4 * b + r + 1)
                        for f in range(HG):
                            for d, (d0, l) in enumerate(CUT):
                                mm = pe.transpose(et_ps[0:l, d, f * 65:f * 65 + n], e[0:n, r % 2, f, d0:d0 + l],
                                                  ident[0:n, 0:n])
                        mm.then_inc(sem["et_done"], 1)
                        pe.wait_ge(sem["et_ready"], 8 * b + 2 * r + 2)
                        for f in range(HG):
                            for d, (d0, l) in enumerate(CUT):
                                mm = pe.matmul(av_ps[0:n, c, g * HG + f, :], et[0:l, d, f, 0:n],
                                               v1[0:l, d, g * HG + f, :], start=(d == 0), stop=(d == 1))
                        mm.then_inc(sem["av_done"], 1)
                    pe.wait_ge(sem["loaded"], 128)
                    pe.wait_ge(sem["att_ready"], b + 1)
                    for c, (c0, n) in enumerate(QCUT):
                        flat = att[0:n, c].rearrange("p h d -> p (h d)")
                        for m in range(2):
                            mm = pe.transpose(heads_ps[:, m, c0:c0 + n], flat[:, m * HALF:(m + 1) * HALF],
                                              ident[0:n, 0:n])
                    mm.then_inc(sem["heads_done"], 1)
                    pe.wait_ge(sem["heads_ready"], b + 1)
                    for m in range(2):
                        for j in range(2):
                            mm = pe.matmul(o_ps[:, m, :], w_proj[:, j, m * HALF:(m + 1) * HALF], heads[:, j, :],
                                           start=(j == 0), stop=(j == 1))
                    mm.then_inc(sem["proj_done"], 1)

                steps(pe, ITEMS, step)

            @block.scalar
            def _(act):
                def step(b, first):
                    act.wait_ge(sem["qkv_done"], b + 1)
                    act.activation(q[0:HALF], q_ps, ACT.Copy).then_inc(sem["q_ready"], 1)
                    for r, (c, g) in enumerate(ROUNDS):
                        n = QCUT[c][1]
                        act.wait_ge(sem["shifted"], 4 * b + r + 1)
                        act.activation(e[0:n, r % 2], e[0:n, r % 2], ACT.Exp, scale=SCALE).then_inc(sem["e_ready"], 1)
                        act.wait_ge(sem["et_done"], 4 * b + r + 1)
                        for d, (d0, l) in enumerate(CUT):
                            act.activation(et[0:l, d, :, 0:n],
                                           et_ps[0:l, d, 0:HG * 65].rearrange("p (f n) -> p f n", f=HG)[:, :, 0:n],
                                           ACT.Copy).then_inc(sem["et_ready"], 1)
                    act.wait_ge(sem["heads_done"], b + 1)
                    act.activation(heads[:], heads_ps, ACT.Copy).then_inc(sem["heads_ready"], 1)

                steps(act, ITEMS, step)

            @block.vector
            def _(dve):
                dve.wait_ge(sem["loaded"], 128)
                dve.wait_ge(sem["ones_ready"], 2)

                def step(b, first):
                    dve.wait_ge(sem["qkv_done"], b + 1)
                    for j in range(2):
                        dve.tensor_tensor(keys[0:R[j], j], k_ps[0:R[j], j, :].unsqueeze(1).broadcast_to([R[j], H, N]),
                                          mixing[0:R[j], j, :].unsqueeze(2).broadcast_to([R[j], H, N]),
                                          ALU.mult).then_inc(sem["keys_ready"], 1)
                    for c, (c0, n) in enumerate(CUT):
                        dve.tensor_tensor(v1[0:n, c, :, 0:HEAD], v_ps[0:n, c, :].rearrange("p (h d) -> p h d", h=H),
                                          v_bias[0:n, :].rearrange("p (h d) -> p h d", h=H),
                                          ALU.add).then_inc(sem["v_ready"], 1)
                    for r, (c, g) in enumerate(ROUNDS):
                        n = QCUT[c][1]
                        dve.wait_ge(sem["s_done"], 4 * b + r + 1)
                        s = s_ps[r % 2][0:n, :, 0:3 * N].rearrange("p i (h m) -> p i h m", h=3)
                        t = top[0:n, r % 2].rearrange("p (i h) -> p i h", i=2)
                        dve.tensor_reduce(t, s, AX.X, ALU.max).then_inc(sem["top_ready"], 1)
                        dve.wait_ge(sem["top_ready"], 4 * b + r + 1)
                        if not first or r >= 2:
                            dve.wait_ge(sem["et_done"], 4 * b + r - 1)
                        dve.tensor_tensor(e[0:n, r % 2].rearrange("p (i h) m -> p i h m", i=2), s,
                                          t.unsqueeze(3).broadcast_to([n, 2, 3, N]),
                                          ALU.subtract).then_inc(sem["shifted"], 1)
                    dve.wait_ge(sem["av_done"], 4 * b + 4)
                    dve.reciprocal(inv[:], av_ps[:, :, :, HEAD]).then_inc(sem["inv_ready"], 1)
                    dve.wait_ge(sem["inv_ready"], b + 1)
                    dve.tensor_tensor(att[:], av_ps[:, :, :, 0:HEAD],
                                      inv[:].unsqueeze(3).broadcast_to([65, 2, H, HEAD]),
                                      ALU.mult).then_inc(sem["att_ready"], 1)
                    dve.wait_ge(sem["proj_done"], b + 1)
                    for m in range(2):
                        cols_b = h[:, m, ds(b * N, N)]
                        dve.scalar_tensor_tensor(out=cols_b, in0=o_ps[:, m, :], scalar=cols[:, 0, m:m + 1],
                                                 in1=cols_b, op0=ALU.add, op1=ALU.add).then_inc(sem["h_ready"], 1)

                steps(dve, ITEMS, step)


def store_output(nc, h, out):
    with Stage(nc, "store") as st:
        stored = st.sem("stored")
        with nc.Block() as block:
            @block.sync
            def _(sp):
                for j in range(2):
                    sp.dma_start(out[:, j, :], h[:, j, :]).then_inc(stored, 16)
                sp.wait_ge(stored, 32)


STAGES = [embed_tokens, linear_attention, grouped_experts, bidirectional_mamba, quantised_mlp, group_attention, shared_experts,
          collaborative_attention, gelu_experts]


def build(nc, dram, out):
    with nc.sbuf_tensor("h", [HALF, 2, T], F32) as h, nc.sbuf_tensor("xn", [HALF, 2, T], F32) as xn:
        for i, stage in enumerate(STAGES):
            if stage is not embed_tokens:
                layer_norm(nc, h, xn, f"norm{i}")
            stage(nc, dram, h, xn)
        store_output(nc, h, out)


def lay_out(i):
    import numpy as np
    a = {k: np.asarray(v) for k, v in i.items()}

    def halves(w):
        return np.ascontiguousarray(w.reshape((2, HALF) + w.shape[1:]).swapaxes(0, 1))

    def columns(*vs):
        return np.stack([halves(v.reshape(D)) for v in vs], axis=1)

    d = {}
    d["x"] = halves(a["x"][..., 0].transpose(2, 0, 1))
    d["embed_taps"] = halves(a["L0_tok_dw_w"].reshape(D, 7))
    d["embed_point_w"] = halves(a["L0_tok_pw_w"].T)
    d["embed_cols"] = columns(a["L0_tok_pw_b"], a["L0_tok_ln_g"], a["L0_tok_ln_b"], a["cls_tok"])
    d["linattn_qkv"] = halves(a["L0_attn_qkv_w"].T)
    d["linattn_proj"] = halves(a["L0_attn_proj_w"].T)
    d["linattn_cols"] = columns(a["L0_attn_proj_b"])
    head = np.arange(HALF) // 16
    mask = (head[:, None] == head[None, :]).astype(np.float32)
    d["head_mask"] = np.stack([mask, mask], axis=1)
    d["ident"] = np.eye(128, dtype=np.float32)
    for n in (8, 16):
        d[f"lower{n}"] = np.broadcast_to(np.tril(np.ones((n, n), np.float32), -1), (RT, n, n))
    sel = np.zeros((SPLIT, 16, 128), np.float32)
    for e in range(16):
        sel[e::32, e] = 1.0
    d["sel"] = sel.astype(mybir.dt.np(BF16))

    def per_expert(w):
        return halves(w.transpose(1, 0, 2).reshape(D, -1))

    d["grouped_router_w"] = halves(a["L0_ffn_gate_w"])
    d["grouped_router_b"] = np.stack([a["L0_ffn_gate_b"], a["L0_ffn_bias"]])
    for mine, theirs in (("up", "Wu"), ("gate", "Wg")):
        d["grouped_" + mine] = halves(np.concatenate([a["L0_ffn_" + theirs], a["L0_ffn_s" + theirs][None]])
                                      .transpose(1, 0, 2))
    d["grouped_down"] = np.concatenate([a["L0_ffn_Wd"], a["L0_ffn_sWd"][None]]).transpose(1, 0, 2)
    d["grouped_bias"] = np.stack([np.concatenate([a["L0_ffn_" + b], a["L0_ffn_s" + b][None]]).T
                                  for b in ("bu", "bg")], axis=1)
    bd = np.zeros((3, 32, D), np.float32)
    bd[:, 0:16] = a["L0_ffn_bd"]
    d["grouped_bd"] = bd.reshape(SPLIT, D)
    d["grouped_cols"] = columns(a["L0_ffn_sbd"])
    d["shared_router_w"] = halves(np.concatenate([a["L2_ffn_router_w"], a["L2_ffn_sg_w"]], axis=1))
    zeros8 = np.zeros(8, np.float32)
    d["shared_router_b"] = np.stack([np.concatenate([zeros8, a["L2_ffn_sg_b"]]), np.zeros(9, np.float32)])
    for mine, theirs in (("up", "gate"), ("gate", "up")):
        d["shared_" + mine] = np.concatenate([per_expert(a["L2_ffn_w_" + theirs]),
                                              halves(a["L2_ffn_ws_" + theirs])], axis=2)
    d["shared_down_r"] = a["L2_ffn_w_down"].reshape(16, HALF, D).transpose(1, 0, 2)
    d["shared_down_s"] = a["L2_ffn_ws_down"].reshape(6, 128, D).transpose(1, 0, 2)
    d["geluexp_router_w"] = halves(a["L3_ffn_router_w"].T)
    d["geluexp_router_b"] = np.zeros((2, 8), np.float32)
    d["geluexp_up"] = per_expert(a["L3_ffn_w1"])
    d["geluexp_down"] = a["L3_ffn_w2"].reshape(48, 128, D).transpose(1, 0, 2)
    def chunks(w):
        return np.ascontiguousarray(w.reshape((IC, 128) + w.shape[1:]).swapaxes(0, 1))

    for which in ("f", "b"):
        m = {k: a[f"L1_attn_{which}_{k}"] for k in ("in_w", "conv_w", "conv_b", "xproj_w", "dt_w", "dt_b",
                                                    "A_log", "D_skip", "out_w")}
        p = f"mamba_{which}_"
        d[p + "in"] = halves(m["in_w"].T)
        xw = np.zeros((INNER, 128), np.float32)
        xw[:, 0:RANK] = m["xproj_w"][0:RANK].T
        for r in (32, 64, 96):
            xw[:, r:r + 2 * STATES] = m["xproj_w"][RANK:].T
        d[p + "x"] = chunks(xw)
        d[p + "dt"] = m["dt_w"].T
        d[p + "out"] = chunks(m["out_w"].T)
        d[p + "cols"] = chunks(np.concatenate([m["conv_w"], m["conv_b"][:, None], m["dt_b"][:, None],
                                               m["D_skip"][:, None]], axis=1))
        d[p + "A_log"] = chunks(m["A_log"])
    d["mamba_norm_cols"] = columns(a["L1_attn_ln_g"], a["L1_attn_ln_b"])
    state_sel = np.zeros((128, 2 * STATES, 128), np.float32)
    for e in range(2 * STATES):
        state_sel[32 + e::32, e] = 1.0
    d["state_sel"] = state_sel.astype(mybir.dt.np(BF16))
    d["quant_w1"] = halves(a["L1_ffn_w1"].T)
    d["quant_w2"] = a["L1_ffn_w2"].T.reshape(6, 128, D).transpose(1, 0, 2)
    d["quant_step_w1"] = a["L1_ffn_alpha_w1"][None]
    d["quant_step_w2"] = a["L1_ffn_alpha_w2"][None]
    d["quant_a1"] = a["L1_ffn_alpha_a1"].reshape(HALF, 2)
    d["quant_a2"] = a["L1_ffn_alpha_a2"].reshape(HALF, 8)
    d["quant_hid"] = np.stack([a["L1_ffn_alpha_w1"].reshape(6, 128).T, a["L1_ffn_b1"].reshape(6, 128).T], axis=1)
    d["quant_out"] = columns(a["L1_ffn_alpha_w2"], a["L1_ffn_b2"])
    d["groupattn_qkv"] = halves(a["L2_attn_W_qkv"])
    d["groupattn_proj"] = halves(a["L2_attn_W_proj"])
    d["groupattn_gp"] = halves(a["L2_attn_W_gp"])
    b_qkv = a["L2_attn_b_qkv"]
    d["groupattn_cols"] = columns(b_qkv[0:D], b_qkv[D:2 * D], a["L2_attn_b_proj"])
    d["groupattn_v_bias"] = b_qkv[None, 2 * D:]
    d["groupattn_alpha"] = a["L2_attn_alpha"][None]
    d["collab_q"] = halves(a["L3_attn_Wq"].T)
    wk = a["L3_attn_Wk"].T
    d["collab_k"] = halves(np.concatenate([wk[:, 0:HALF], a["L3_attn_Wcb"].T, wk[:, HALF:]], axis=1))
    d["collab_v"] = halves(a["L3_attn_Wv"].T)
    d["collab_proj"] = halves(a["L3_attn_Wproj"].T)
    mixing = np.zeros((HALF + 12, 2, 12), np.float32)
    mixing[HALF:, 0] = np.eye(12, dtype=np.float32)
    mixing[0:HALF] = halves(a["L3_attn_Wmix"].T)
    d["collab_mixing"] = mixing
    d["collab_cols"] = columns(a["L3_attn_bproj"])
    d["collab_v_bias"] = a["L3_attn_bv"][None]
    return d


def kernel(**inputs):
    import numpy as np
    import concourse.bacc as bacc
    from concourse.bass_utils import run_bass_kernel_spmd

    nc = bacc.Bacc("TRN2", target_bir_lowering=False, num_devices=1)
    arrays = {f"in_{k}": np.ascontiguousarray(v) for k, v in lay_out(inputs).items()}
    dram = {k[3:]: nc.dram_tensor(k, v.shape, mybir.dt.from_np(v.dtype), kind="ExternalInput").ap()
            for k, v in arrays.items()}
    out = nc.dram_tensor("out_h", (HALF, 2, T), F32, kind="ExternalOutput").ap()
    build(nc, dram, out)
    r = run_bass_kernel_spmd(nc, [arrays], core_ids=[0])
    got = r.results[0]["out_h"]
    return np.ascontiguousarray(got.reshape(HALF, 2, ITEMS, N).transpose(2, 3, 1, 0).reshape(ITEMS, N, D))
```

```python
from contextlib import ExitStack, contextmanager

import concourse.bass as bass
from concourse import mybir

ALU = mybir.AluOpType
ACT = mybir.ActivationFunctionType
AX = mybir.AxisListType
F32 = mybir.dt.float32
BF16 = mybir.dt.bfloat16
ds = bass.ds

ITEMS = 16
PATCHES = 128
N = PATCHES + 1
D = 192
HALF = D // 2
T = ITEMS * N
TILE = 344
TILES = T // TILE
assert TILES * TILE == T


class Stage:
    used = []

    def __init__(self, nc, name):
        self.nc, self.name, self.ctx, self.sems = nc, name, ExitStack(), []

    def __enter__(self):
        self.ctx.__enter__()
        return self

    def sb(self, name, shape, dt=F32):
        return self.ctx.enter_context(self.nc.sbuf_tensor(f"{self.name}_{name}", shape, dt))

    def ps(self, name, shape, dt=F32):
        return self.ctx.enter_context(self.nc.psum_tensor(f"{self.name}_{name}", shape, dt))

    def sem(self, name):
        s = self.nc.alloc_semaphore(f"{self.name}_{name}")
        self.sems.append(s)
        return s

    @contextmanager
    def block(self):
        zeroed = list(Stage.used)
        with self.nc.Block(no_gpsimd_drain=True) as block:
            if zeroed:
                @block.gpsimd
                def _(pool):
                    for s in zeroed:
                        pool.sem_clear(s)
            yield block
        for s in zeroed:
            Stage.used.remove(s)
            self.nc.release_semaphore(s)

    def __exit__(self, *exc):
        Stage.used.extend(self.sems)
        return self.ctx.__exit__(*exc)


def layer_norm(nc, h, xn, name):
    with Stage(nc, name) as st:
        averager = st.sb("averager", [HALF, HALF])
        eps = st.sb("eps", [HALF, 1])
        centred = st.sb("centred", [HALF, 2, 2, TILE])
        squared = st.sb("squared", [HALF, 2, 2, TILE])
        std = st.sb("std", [HALF, 2, TILE])
        rstd = st.sb("rstd", [HALF, 2, TILE])
        mean_ps = st.ps("mean", [HALF, 2, 512])
        var_ps = st.ps("var", [HALF, 2, 512])
        consts = st.sem("consts")
        mean_ready = st.sem("mean_ready")
        centred_ready = st.sem("centred_ready")
        squared_ready = st.sem("squared_ready")
        var_ready = st.sem("var_ready")
        std_ready = st.sem("std_ready")
        rstd_ready = st.sem("rstd_ready")
        xn_ready = st.sem("xn_ready")

        def cols(t):
            return slice(t * TILE, (t + 1) * TILE)

        with st.block() as block:
            @block.gpsimd
            def _(pool):
                pool.memset(averager[:], 1.0 / D).then_inc(consts, 1)
                pool.memset(eps[:], 1e-5).then_inc(consts, 1)

            @block.tensor
            def _(pe):
                def mean(t):
                    if t >= 2:
                        pe.wait_ge(centred_ready, t - 1)
                    for j in range(2):
                        mm = pe.matmul(mean_ps[:, t % 2, 0:TILE], averager[:], h[:, j, cols(t)],
                                       start=(j == 0), stop=(j == 1))
                    mm.then_inc(mean_ready, 1)

                pe.wait_ge(consts, 2)
                mean(0)
                for t in range(TILES):
                    if t + 1 < TILES:
                        mean(t + 1)
                    pe.wait_ge(squared_ready, t + 1)
                    if t >= 2:
                        pe.wait_ge(std_ready, t - 1)
                    for j in range(2):
                        mm = pe.matmul(var_ps[:, t % 2, 0:TILE], averager[:], squared[:, t % 2, j, :],
                                       start=(j == 0), stop=(j == 1))
                    mm.then_inc(var_ready, 1)

            @block.scalar
            def _(act):
                def square(t):
                    act.wait_ge(centred_ready, t + 1)
                    if t >= 2:
                        act.wait_ge(var_ready, t - 1)
                    act.activation(squared[:, t % 2], centred[:, t % 2], ACT.Square).then_inc(squared_ready, 1)

                act.wait_ge(consts, 2)
                square(0)
                for t in range(TILES):
                    if t + 1 < TILES:
                        square(t + 1)
                    act.wait_ge(var_ready, t + 1)
                    if t >= 2:
                        act.wait_ge(rstd_ready, t - 1)
                    act.activation(std[:, t % 2], var_ps[:, t % 2, 0:TILE], ACT.Sqrt,
                                   bias=eps[:]).then_inc(std_ready, 1)

            @block.vector
            def _(dve):
                def centre(t):
                    dve.wait_ge(mean_ready, t + 1)
                    if t >= 2:
                        dve.wait_ge(squared_ready, t - 1)
                        dve.wait_ge(xn_ready, t - 1)
                    dve.tensor_tensor(centred[:, t % 2], h[:, :, cols(t)],
                                      mean_ps[:, t % 2, 0:TILE].unsqueeze(1).broadcast_to([HALF, 2, TILE]),
                                      ALU.subtract).then_inc(centred_ready, 1)

                centre(0)
                for t in range(TILES):
                    if t + 1 < TILES:
                        centre(t + 1)
                    dve.wait_ge(std_ready, t + 1)
                    if t >= 2:
                        dve.wait_ge(xn_ready, t - 1)
                    dve.reciprocal(rstd[:, t % 2], std[:, t % 2]).then_inc(rstd_ready, 1)
                    dve.wait_ge(rstd_ready, t + 1)
                    dve.tensor_tensor(xn[:, :, cols(t)], centred[:, t % 2],
                                      rstd[:, t % 2].unsqueeze(1).broadcast_to([HALF, 2, TILE]),
                                      ALU.mult).then_inc(xn_ready, 1)


def steps(engine, count, body):
    body(0, True)
    with engine.Fori(1, count) as s:
        body(s, False)


def embed_tokens(nc, dram, h, xn):
    TAPS = 7
    PAD = TAPS // 2
    G = 2
    COLS = G * PATCHES
    STEPS = ITEMS // G
    with Stage(nc, "embed") as st:
        x = st.sb("x", [HALF, 2, ITEMS, PATCHES + 2 * PAD])
        taps = st.sb("taps", [HALF, 2, TAPS])
        diag = st.sb("diag", [HALF, 2, TAPS, HALF])
        ones = st.sb("ones", [HALF, HALF])
        averager = st.sb("averager", [HALF, HALF])
        point_w = st.sb("point_w", [HALF, 2, D])
        cols = st.sb("cols", [HALF, 4, 2])
        eps = st.sb("eps", [HALF, 1])
        conv = st.sb("conv", [HALF, 2, COLS])
        y = st.sb("y", [HALF, 2, COLS])
        centred = st.sb("centred", [HALF, 2, COLS])
        squared = st.sb("squared", [HALF, 2, COLS])
        std = st.sb("std", [HALF, COLS])
        rstd = st.sb("rstd", [HALF, COLS])
        normed = st.sb("normed", [HALF, 2, COLS])
        conv_ps = st.ps("conv_ps", [HALF, 2, COLS])
        y_ps = st.ps("y_ps", [HALF, 2, COLS])
        mean_ps = st.ps("mean_ps", [HALF, COLS])
        var_ps = st.ps("var_ps", [HALF, COLS])
        x_loaded = st.sem("x_loaded")
        weights_loaded = st.sem("weights_loaded")
        padded = st.sem("padded")
        consts = st.sem("consts")
        diag_ready = st.sem("diag_ready")
        conv_done = st.sem("conv_done")
        conv_ready = st.sem("conv_ready")
        y_done = st.sem("y_done")
        y_ready = st.sem("y_ready")
        mean_ready = st.sem("mean_ready")
        centred_ready = st.sem("centred_ready")
        squared_ready = st.sem("squared_ready")
        var_ready = st.sem("var_ready")
        std_ready = st.sem("std_ready")
        rstd_ready = st.sem("rstd_ready")
        normed_ready = st.sem("normed_ready")
        h_ready = st.sem("h_ready")
        h_items = h[:].rearrange("p j (b n) -> p j b n", n=N)
        with st.block() as block:
            @block.sync
            def _(sp):
                for j in range(2):
                    sp.dma_start(x[:, j, :, PAD:PAD + PATCHES], dram["x"][:, j]).then_inc(x_loaded, 16)
                sp.dma_start(taps[:], dram["embed_taps"]).then_inc(weights_loaded, 16)
                sp.dma_start(point_w[:], dram["embed_point_w"]).then_inc(weights_loaded, 16)
                sp.dma_start(cols[:], dram["embed_cols"]).then_inc(weights_loaded, 16)

            @block.gpsimd
            def _(pool):
                pool.memset(x[:, :, :, 0:PAD], 0.0).then_inc(padded, 1)
                pool.memset(x[:, :, :, PAD + PATCHES:], 0.0).then_inc(padded, 1)
                pool.memset(ones[:], 1.0).then_inc(consts, 1)
                pool.memset(averager[:], 1.0 / D).then_inc(consts, 1)
                pool.memset(eps[:], 1e-6).then_inc(consts, 1)
                pool.wait_ge(weights_loaded, 48)
                pool.wait_ge(consts, 3)
                for j in range(2):
                    for k in range(TAPS):
                        pool.tensor_scalar(diag[:, j, k, :], ones[:], taps[:, j, k:k + 1], None,
                                           ALU.mult).then_inc(diag_ready, 1)
                pool.wait_ge(diag_ready, 2 * TAPS)
                for j in range(2):
                    pool.affine_select(out=diag[:, j], in_=diag[:, j], compare_op=ALU.is_equal, fill=0.0,
                                       base=0, pattern=[[0, TAPS], [-1, HALF]],
                                       channel_multiplier=1).then_inc(diag_ready, 1)

            @block.tensor
            def _(pe):
                pe.wait_ge(diag_ready, 2 * TAPS + 2)
                pe.wait_ge(padded, 2)
                pe.wait_ge(x_loaded, 32)
                pe.wait_ge(weights_loaded, 48)

                def step(s, first):
                    for j in range(2):
                        for k in range(TAPS):
                            mm = pe.matmul(conv_ps[:, j, :].rearrange("p (b n) -> p b n", b=G), diag[:, j, k, :],
                                           x[:, j, ds(s * G, G), k:k + PATCHES],
                                           start=(k == 0), stop=(k == TAPS - 1))
                    mm.then_inc(conv_done, 1)
                    pe.wait_ge(conv_ready, s + 1)
                    for m in range(2):
                        for j in range(2):
                            mm = pe.matmul(y_ps[:, m, :], point_w[:, j, m * HALF:(m + 1) * HALF], conv[:, j, :],
                                           start=(j == 0), stop=(j == 1))
                    mm.then_inc(y_done, 1)
                    pe.wait_ge(y_ready, 2 * s + 2)
                    for j in range(2):
                        mm = pe.matmul(mean_ps[:], averager[:], y[:, j, :], start=(j == 0), stop=(j == 1))
                    mm.then_inc(mean_ready, 1)
                    pe.wait_ge(squared_ready, s + 1)
                    if not first:
                        pe.wait_ge(std_ready, s)
                    for j in range(2):
                        mm = pe.matmul(var_ps[:], averager[:], squared[:, j, :], start=(j == 0), stop=(j == 1))
                    mm.then_inc(var_ready, 1)

                steps(pe, STEPS, step)

            @block.scalar
            def _(act):
                act.wait_ge(weights_loaded, 48)
                act.wait_ge(consts, 3)

                def step(s, first):
                    act.wait_ge(conv_done, s + 1)
                    act.activation(conv[:], conv_ps[:], ACT.Copy).then_inc(conv_ready, 1)
                    act.wait_ge(y_done, s + 1)
                    for m in range(2):
                        act.activation(y[:, m, :], y_ps[:, m, :], ACT.Identity,
                                       bias=cols[:, 0, m:m + 1]).then_inc(y_ready, 1)
                    act.wait_ge(centred_ready, s + 1)
                    act.activation(squared[:], centred[:], ACT.Square).then_inc(squared_ready, 1)
                    act.wait_ge(var_ready, s + 1)
                    if not first:
                        act.wait_ge(rstd_ready, s)
                    act.activation(std[:], var_ps[:], ACT.Sqrt, bias=eps[:]).then_inc(std_ready, 1)
                    act.wait_ge(normed_ready, s + 1)
                    for m in range(2):
                        act.activation(h_items[:, m, ds(s * G, G), 1:N],
                                       normed[:, m, :].rearrange("p (b n) -> p b n", b=G), ACT.Relu,
                                       bias=cols[:, 2, m:m + 1], scale=cols[:, 1, m:m + 1]).then_inc(h_ready, 1)

                steps(act, STEPS, step)

            @block.vector
            def _(dve):
                dve.wait_ge(weights_loaded, 48)
                for m in range(2):
                    dve.tensor_copy(h_items[:, m, :, 0], cols[:, 3, m:m + 1].broadcast_to([HALF, ITEMS]))

                def step(s, first):
                    dve.wait_ge(mean_ready, s + 1)
                    if not first:
                        dve.wait_ge(normed_ready, s)
                    dve.tensor_tensor(centred[:], y[:], mean_ps[:].unsqueeze(1).broadcast_to([HALF, 2, COLS]),
                                      ALU.subtract).then_inc(centred_ready, 1)
                    dve.wait_ge(std_ready, s + 1)
                    dve.reciprocal(rstd[:], std[:]).then_inc(rstd_ready, 1)
                    dve.wait_ge(rstd_ready, s + 1)
                    if not first:
                        dve.wait_ge(h_ready, 2 * s)
                    dve.tensor_tensor(normed[:], centred[:], rstd[:].unsqueeze(1).broadcast_to([HALF, 2, COLS]),
                                      ALU.mult).then_inc(normed_ready, 1)

                steps(dve, STEPS, step)


def linear_attention(nc, dram, h, xn):
    HEAD = 16
    SCALE = HEAD ** -0.5
    CHUNKS = ((0, 65), (65, 64))
    with Stage(nc, "linattn") as st:
        w_qkv = st.sb("w_qkv", [HALF, 2, 3 * D])
        w_proj = st.sb("w_proj", [HALF, 2, D])
        b_proj = st.sb("b_proj", [HALF, 1, 2])
        mask = st.sb("mask", [HALF, 2, HALF])
        x = st.sb("x", [HALF, 2, N])
        q = st.sb("q", [HALF, 2, N])
        k = st.sb("k", [65, 2, D])
        v1 = st.sb("v1", [65, 2, 2, 2, HALF])
        kv = st.sb("kv", [HALF, 2, 2, HALF])
        den = st.sb("den", [HALF, 2, N])
        rden = st.sb("rden", [HALF, 2, N])
        heads = st.sb("heads", [HALF, 2, N])
        q_ps = st.ps("q_ps", [HALF, 2, N])
        k_v_ps = st.ps("k_v_ps", [65, 2, 512])
        kv_ps = st.ps("kv_ps", [HALF, 2, 2, HALF])
        num_ps = st.ps("num_ps", [HALF, 2, N])
        den_ps = st.ps("den_ps", [HALF, 2, N])
        o_ps = st.ps("o_ps", [HALF, 2, N])
        loaded = st.sem("loaded")
        ones_ready = st.sem("ones_ready")
        x_ready = st.sem("x_ready")
        qkv_done = st.sem("qkv_done")
        v_ready = st.sem("v_ready")
        k_ready = st.sem("k_ready")
        q_ready = st.sem("q_ready")
        kv_done = st.sem("kv_done")
        kv_ready = st.sem("kv_ready")
        num_done = st.sem("num_done")
        den_ready = st.sem("den_ready")
        rden_ready = st.sem("rden_ready")
        heads_ready = st.sem("heads_ready")
        proj_done = st.sem("proj_done")
        h_ready = st.sem("h_ready")
        with st.block() as block:
            @block.sync
            def _(sp):
                sp.dma_start(w_qkv[:], dram["linattn_qkv"]).then_inc(loaded, 16)
                sp.dma_start(w_proj[:], dram["linattn_proj"]).then_inc(loaded, 16)
                sp.dma_start(b_proj[:], dram["linattn_cols"]).then_inc(loaded, 16)
                sp.dma_start(mask[:], dram["head_mask"]).then_inc(loaded, 16)

            @block.gpsimd
            def _(pool):
                pool.memset(v1[:, :, :, 1, :], 1.0).then_inc(ones_ready, 1)

                def step(b, first):
                    if not first:
                        pool.wait_ge(qkv_done, b)
                    pool.tensor_copy(x[:], xn[:, :, ds(b * N, N)]).then_inc(x_ready, 1)

                steps(pool, ITEMS, step)

            @block.tensor
            def _(pe):
                pe.wait_ge(loaded, 64)
                pe.wait_ge(ones_ready, 1)

                def step(b, first):
                    pe.wait_ge(x_ready, b + 1)
                    for c, (c0, n) in enumerate(CHUNKS):
                        for j in range(2):
                            pe.matmul(k_v_ps[0:n, c, 0:2 * D], x[:, j, c0:c0 + n], w_qkv[:, j, D:3 * D],
                                      start=(j == 0), stop=(j == 1))
                    for m in range(2):
                        for j in range(2):
                            mm = pe.matmul(q_ps[:, m, :], w_qkv[:, j, m * HALF:(m + 1) * HALF], x[:, j, :],
                                           start=(j == 0), stop=(j == 1))
                    mm.then_inc(qkv_done, 1)
                    pe.wait_ge(v_ready, 2 * b + 2)
                    pe.wait_ge(k_ready, 2 * b + 2)
                    for j in range(2):
                        for c, (c0, n) in enumerate(CHUNKS):
                            mm = pe.matmul(kv_ps[:, j], k[0:n, c, j * HALF:(j + 1) * HALF], v1[0:n, c, j],
                                           start=(c == 0), stop=(c == 1))
                    mm.then_inc(kv_done, 1)
                    pe.wait_ge(kv_ready, b + 1)
                    pe.wait_ge(q_ready, b + 1)
                    for j in range(2):
                        pe.matmul(num_ps[:, j, :], kv[:, j, 0, :], q[:, j, :], start=True, stop=True)
                        mm = pe.matmul(den_ps[:, j, :], kv[:, j, 1, :], q[:, j, :], start=True, stop=True)
                    mm.then_inc(num_done, 1)
                    pe.wait_ge(heads_ready, b + 1)
                    if not first:
                        pe.wait_ge(h_ready, 2 * b)
                    for m in range(2):
                        for j in range(2):
                            mm = pe.matmul(o_ps[:, m, :], w_proj[:, j, m * HALF:(m + 1) * HALF], heads[:, j, :],
                                           start=(j == 0), stop=(j == 1))
                    mm.then_inc(proj_done, 1)

                steps(pe, ITEMS, step)

            @block.scalar
            def _(act):
                def step(b, first):
                    act.wait_ge(qkv_done, b + 1)
                    if not first:
                        act.wait_ge(kv_done, b)
                    for c, (c0, n) in enumerate(CHUNKS):
                        act.activation(v1[0:n, c, :, 0, :],
                                       k_v_ps[0:n, c, D:2 * D].rearrange("p (j f) -> p j f", j=2),
                                       ACT.Copy).then_inc(v_ready, 1)

                steps(act, ITEMS, step)

            @block.vector
            def _(dve):
                dve.wait_ge(loaded, 64)

                def step(b, first):
                    dve.wait_ge(qkv_done, b + 1)
                    if not first:
                        dve.wait_ge(kv_done, b)
                    dve.tensor_scalar(q[:], q_ps[:], 0.0, SCALE, ALU.max, ALU.add).then_inc(q_ready, 1)
                    dve.wait_ge(v_ready, 2 * b + 2)
                    for c, (c0, n) in enumerate(CHUNKS):
                        dve.tensor_scalar(k[0:n, c, :], k_v_ps[0:n, c, 0:D], 0.0, SCALE, ALU.max,
                                          ALU.add).then_inc(k_ready, 1)
                    dve.wait_ge(kv_done, b + 1)
                    dve.tensor_tensor(kv[:], kv_ps[:], mask[:].unsqueeze(1).broadcast_to([HALF, 2, 2, HALF]),
                                      ALU.mult).then_inc(kv_ready, 1)
                    dve.wait_ge(num_done, b + 1)
                    dve.tensor_scalar(den[:], den_ps[:], 1e-6, None, ALU.add).then_inc(den_ready, 1)
                    dve.wait_ge(den_ready, b + 1)
                    dve.reciprocal(rden[:], den[:]).then_inc(rden_ready, 1)
                    dve.wait_ge(rden_ready, b + 1)
                    if not first:
                        dve.wait_ge(proj_done, b)
                    dve.tensor_tensor(heads[:], num_ps[:], rden[:], ALU.mult).then_inc(heads_ready, 1)
                    dve.wait_ge(proj_done, b + 1)
                    for m in range(2):
                        dve.scalar_tensor_tensor(out=h[:, m, ds(b * N, N)], in0=o_ps[:, m, :],
                                                 scalar=b_proj[:, 0, m:m + 1], in1=h[:, m, ds(b * N, N)],
                                                 op0=ALU.add, op1=ALU.add).then_inc(h_ready, 1)

                steps(dve, ITEMS, step)


RT = 86
CHUNKS = T // RT
SPLIT = 96
assert CHUNKS * RT == T and TILE % RT == 0


def router(nc, dram, xn, gates, name, experts, choose, extra=0):
    E = experts + extra
    with Stage(nc, name + "_router") as st:
        w = st.sb("w", [HALF, 2, E])
        ident = st.sb("ident", [RT, RT])
        b = {k: st.sb(k, [RT, E]) for k in ("logit_bias", "score_bias", "scratch_bias")}
        lower = st.sb("lower", [RT, E, E])
        big = {k: st.sb(k, [RT, CHUNKS, experts, experts], BF16) for k in ("greater", "equal")}
        f = {k: st.sb(k, [RT, CHUNKS, E]) for k in ("logits", "exps", "probs", "scores", "rank", "mask", "weight")}
        g = {k: st.sb(k, [RT, CHUNKS, 8]) for k in ("group", "group_rank", "group_mask")}
        c = {k: st.sb(k, [RT, CHUNKS]) for k in ("top", "total", "recip", "u", "v")}
        wide = st.sb("wide", [RT, CHUNKS, SPLIT])
        full = st.sb("full", [SPLIT, T])
        rest = st.sb("rest", [SPLIT, T])
        part = st.sb("part", [SPLIT, T], BF16)
        logits_ps = st.ps("logits_ps", [RT, CHUNKS, E])
        turned_ps = st.ps("turned_ps", [SPLIT, TILES, 512])
        loaded = st.sem("loaded")
        logits_done = st.sem("logits_done")
        exp_in_ready = st.sem("exp_in_ready")
        exp_ready = st.sem("exp_ready")
        wide_ready = st.sem("wide_ready")
        turned_done = st.sem("turned_done")
        full_ready = st.sem("full_ready")
        chain = st.sem("chain")
        with st.block() as block:
            @block.sync
            def _(sp):
                sp.dma_start(w[:], dram[name + "_router_w"]).then_inc(loaded, 16)
                sp.dma_start(b["logit_bias"][:], dram[name + "_router_b"][0:1].broadcast_to([RT, E])).then_inc(loaded, 16)
                sp.dma_start(b["score_bias"][:], dram[name + "_router_b"][1:2].broadcast_to([RT, E])).then_inc(loaded, 16)
                sp.dma_start(ident[:], dram["ident"][0:RT, 0:RT]).then_inc(loaded, 16)
                sp.dma_start(lower[:, 0:experts, 0:experts], dram[f"lower{experts}"]).then_inc(loaded, 16)

            @block.tensor
            def _(pe):
                pe.wait_ge(loaded, 80)
                for t in range(CHUNKS):
                    for j in range(2):
                        mm = pe.matmul(logits_ps[:, t, :], xn[:, j, t * RT:(t + 1) * RT], w[:, j, :],
                                       start=(j == 0), stop=(j == 1))
                mm.then_inc(logits_done, 1)
                pe.wait_ge(wide_ready, 1)
                per = TILE // RT
                for t in range(CHUNKS):
                    mm = pe.transpose(turned_ps[:, t // per, (t % per) * RT:(t % per + 1) * RT],
                                      wide[:, t, :], ident[:])
                mm.then_inc(turned_done, 1)

            @block.scalar
            def _(act):
                act.wait_ge(exp_in_ready, 1)
                act.activation(f["exps"][:], f["logits"][:], ACT.Exp).then_inc(exp_ready, 1)
                act.wait_ge(turned_done, 1)
                act.activation(full[:].rearrange("p (t n) -> p t n", n=TILE), turned_ps[:, :, 0:TILE],
                               ACT.Copy).then_inc(full_ready, 1)

            @block.vector
            def _(dve):
                count = [0]

                def link(ins):
                    count[0] += 1
                    ins.then_inc(chain, 1)
                    dve.wait_ge(chain, count[0])

                def over(ap, n):
                    return ap.unsqueeze(1).broadcast_to([RT, CHUNKS, n])

                def last(ap, n):
                    return ap.unsqueeze(2).broadcast_to([RT, CHUNKS, n])

                def rank(out, score, n, kind):
                    this = score.unsqueeze(3).broadcast_to([RT, CHUNKS, n, n])
                    other = score.unsqueeze(2).broadcast_to([RT, CHUNKS, n, n])
                    gt = big["greater"][:].rearrange("p c a b -> p c (a b)")[:, :, 0:n * n].rearrange("p c (a b) -> p c a b", a=n)
                    eq = big["equal"][:].rearrange("p c a b -> p c (a b)")[:, :, 0:n * n].rearrange("p c (a b) -> p c a b", a=n)
                    link(dve.tensor_tensor(gt, other, this, ALU.is_gt))
                    link(dve.tensor_tensor(eq, other, this, ALU.is_equal))
                    link(dve.tensor_tensor(eq, eq, lower[:, 0:n, 0:n].unsqueeze(1).broadcast_to([RT, CHUNKS, n, n]),
                                           ALU.mult))
                    link(dve.tensor_tensor(gt, gt, eq, ALU.add))
                    link(dve.tensor_reduce(out, gt, AX.X, ALU.add))

                link(dve.memset(wide[:], 0.0))
                dve.wait_ge(loaded, 80)
                dve.wait_ge(logits_done, 1)
                L = f["logits"]
                n = experts
                link(dve.tensor_tensor(L[:], logits_ps[:], over(b["logit_bias"][:], E), ALU.add))
                link(dve.tensor_reduce(c["top"][:], L[:, :, 0:n], AX.X, ALU.max))
                link(dve.tensor_tensor(L[:, :, 0:n], L[:, :, 0:n], last(c["top"][:], n), ALU.subtract))
                if extra:
                    link(dve.tensor_scalar(L[:, :, n:E], L[:, :, n:E], -1.0, None, ALU.mult))
                dve.nop().then_inc(exp_in_ready, 1)
                dve.wait_ge(exp_ready, 1)
                link(dve.tensor_reduce(c["total"][:], f["exps"][:, :, 0:n], AX.X, ALU.add))
                link(dve.reciprocal(c["recip"][:], c["total"][:]))
                link(dve.tensor_tensor(f["probs"][:, :, 0:n], f["exps"][:, :, 0:n], last(c["recip"][:], n), ALU.mult))
                choose(dve, link, rank, over, last, b, f, g, c)
                for r in range(3):
                    ins = dve.tensor_copy(wide[:, :, 32 * r:32 * r + E], f["weight"][:])
                ins.then_inc(wide_ready, 1)
                dve.wait_ge(full_ready, 1)
                link(dve.tensor_copy(part[:], full[:]))
                link(dve.tensor_copy(gates[0:32, :], part[0:32, :]))
                link(dve.tensor_tensor(rest[:], full[:], part[:], ALU.subtract))
                link(dve.tensor_copy(part[:], rest[:]))
                link(dve.tensor_copy(gates[32:64, :], part[32:64, :]))
                link(dve.tensor_tensor(rest[:], rest[:], part[:], ALU.subtract))
                link(dve.tensor_copy(gates[64:96, :], rest[64:96, :]))


def expert_mlps(nc, h, xn, gates, sel, name, units, act_fn, bias, y_bias, extra_down):
    U = len(units)
    with Stage(nc, name + "_mlp") as st:
        s = st.sb("s", [128, 2, TILE])
        prod = st.sb("prod", [128, 2, TILE])
        hid = st.sb("hid", [128, 2, TILE])
        up_ps = st.ps("up_ps", [128, 2, 512])
        gate_ps = st.ps("gate_ps", [128, 2, 512])
        wide_ps = st.ps("wide_ps", [128, 2, 512])
        y_ps = st.ps("y_ps", [HALF, 2, 512])
        up_done = st.sem("up_done")
        side_done = st.sem("side_done")
        s_ready = st.sem("s_ready")
        prod_ready = st.sem("prod_ready")
        hid_ready = st.sem("hid_ready")
        down_done = st.sem("down_done")
        h_ready = st.sem("h_ready")
        gated = [k for k, u in enumerate(units) if u["row"] is not None and u["gate"] is not None]
        prods = len(gated)
        with st.block() as block:
            @block.tensor
            def _(pe):
                def down(t, first, k):
                    u = units[k]
                    pe.wait_ge(hid_ready, t * U + k + 1)
                    if k == 0 and not first:
                        pe.wait_ge(h_ready, 2 * t)
                    if k == 0:
                        for i, w in enumerate(extra_down):
                            for m in range(2):
                                pe.matmul(y_ps[:, m, 0:TILE], w[:, m * HALF:(m + 1) * HALF],
                                          gates[:, ds(t * TILE, TILE)], start=(i == 0), stop=False)
                    for m in range(2):
                        mm = pe.matmul(y_ps[:, m, 0:TILE], u["down"][:, m * HALF:(m + 1) * HALF],
                                       hid[0:u["n"], k % 2, :], start=(k == 0 and not extra_down),
                                       stop=(k == U - 1))
                    mm.then_inc(down_done, 1)

                def step(t, first):
                    x = [xn[:, j, ds(t * TILE, TILE)] for j in range(2)]
                    for k, u in enumerate(units):
                        n = u["n"]
                        for j in range(2):
                            mm = pe.matmul(up_ps[0:n, k % 2, 0:TILE], u["up"][:, j, :], x[j],
                                           start=(j == 0), stop=(j == 1))
                        mm.then_inc(up_done, 1)
                        if u["gate"] is not None:
                            for j in range(2):
                                mm = pe.matmul(gate_ps[0:n, k % 2, 0:TILE], u["gate"][:, j, :], x[j],
                                               start=(j == 0), stop=(j == 1))
                        if u["row"] is not None:
                            mm = pe.matmul(wide_ps[0:n, k % 2, 0:TILE], sel[:, u["row"], 0:n],
                                           gates[:, ds(t * TILE, TILE)], start=True, stop=True)
                        mm.then_inc(side_done, 1)
                        if k:
                            down(t, first, k - 1)
                    down(t, first, U - 1)

                steps(pe, TILES, step)

            @block.scalar
            def _(act):
                def step(t, first):
                    for k, u in enumerate(units):
                        n = u["n"]
                        act.wait_ge(up_done, t * U + k + 1)
                        if not first or k >= 2:
                            act.wait_ge(hid_ready, t * U + k - 1)
                        act.activation(s[0:n, k % 2, :], up_ps[0:n, k % 2, 0:TILE], act_fn,
                                       bias=0.0 if bias is None else bias[0:n, 0, k:k + 1]).then_inc(s_ready, 1)

                steps(act, TILES, step)

            @block.vector
            def _(dve):
                def step(t, first):
                    done = 0
                    for k, u in enumerate(units):
                        n = u["n"]
                        g_bias = 0.0 if bias is None else bias[0:n, 1, k:k + 1]
                        dve.wait_ge(s_ready, t * U + k + 1)
                        dve.wait_ge(side_done, t * U + k + 1)
                        if not first or k >= 2:
                            dve.wait_ge(down_done, t * U + k - 1)
                        if u["gate"] is not None and u["row"] is not None:
                            done += 1
                            dve.scalar_tensor_tensor(out=prod[0:n, k % 2, :], in0=gate_ps[0:n, k % 2, 0:TILE],
                                                     scalar=g_bias, in1=s[0:n, k % 2, :], op0=ALU.add,
                                                     op1=ALU.mult).then_inc(prod_ready, 1)
                            dve.wait_ge(prod_ready, t * prods + done)
                            dve.tensor_tensor(hid[0:n, k % 2, :], prod[0:n, k % 2, :], wide_ps[0:n, k % 2, 0:TILE],
                                              ALU.mult).then_inc(hid_ready, 1)
                        elif u["gate"] is not None:
                            dve.scalar_tensor_tensor(out=hid[0:n, k % 2, :], in0=gate_ps[0:n, k % 2, 0:TILE],
                                                     scalar=g_bias, in1=s[0:n, k % 2, :], op0=ALU.add,
                                                     op1=ALU.mult).then_inc(hid_ready, 1)
                        else:
                            dve.tensor_tensor(hid[0:n, k % 2, :], s[0:n, k % 2, :], wide_ps[0:n, k % 2, 0:TILE],
                                              ALU.mult).then_inc(hid_ready, 1)
                    dve.wait_ge(down_done, (t + 1) * U)
                    for m in range(2):
                        tile = h[:, m, ds(t * TILE, TILE)]
                        dve.scalar_tensor_tensor(out=tile, in0=y_ps[:, m, 0:TILE],
                                                 scalar=0.0 if y_bias is None else y_bias[:, 0, m:m + 1],
                                                 in1=tile, op0=ALU.add, op1=ALU.add).then_inc(h_ready, 1)

                steps(dve, TILES, step)


def load(nc, name, pairs):
    with Stage(nc, name) as st:
        loaded = st.sem("loaded")
        with st.block() as block:
            @block.sync
            def _(sp):
                for dst, src in pairs:
                    sp.dma_start(dst, src).then_inc(loaded, 16)
                sp.wait_ge(loaded, 16 * len(pairs))


def split_weights(nc, name, w, rest, parts):
    with Stage(nc, name) as st:
        chain = st.sem("chain")
        with st.block() as block:
            @block.vector
            def _(dve):
                source = w
                for i in range(3):
                    dve.tensor_copy(parts[:, i], source[:]).then_inc(chain, 1)
                    dve.wait_ge(chain, 2 * i + 1)
                    if i < 2:
                        dve.tensor_tensor(rest[:], source[:], parts[:, i], ALU.subtract).then_inc(chain, 1)
                        dve.wait_ge(chain, 2 * i + 2)
                        source = rest


def grouped_experts(nc, dram, h, xn):
    E, HID, BIG = 16, 128, 1e30

    def choose(dve, link, rank, over, last, b, f, g, c):
        link(dve.tensor_tensor(f["scores"][:], f["probs"][:], over(b["score_bias"][:], E), ALU.add))
        pairs = f["scores"][:].rearrange("p c (g i) -> p c g i", i=2)
        link(dve.tensor_tensor(g["group"][:], pairs[:, :, :, 0], pairs[:, :, :, 1], ALU.add))
        rank(g["group_rank"][:], g["group"][:], 8, "group")
        link(dve.tensor_scalar(g["group_mask"][:], g["group_rank"][:], 3.5, None, ALU.is_lt))
        gm = g["group_mask"][:].unsqueeze(3).broadcast_to([RT, CHUNKS, 8, 2])
        link(dve.tensor_tensor(pairs, pairs, gm, ALU.mult))
        link(dve.tensor_scalar(g["group_mask"][:], g["group_mask"][:], BIG, -BIG, ALU.mult, ALU.add))
        link(dve.tensor_tensor(pairs, pairs, gm, ALU.add))
        rank(f["rank"][:], f["scores"][:], E, "expert")
        link(dve.tensor_scalar(f["mask"][:], f["rank"][:], 3.5, 2.5, ALU.is_lt, ALU.mult))
        link(dve.tensor_tensor(f["weight"][:], f["probs"][:], f["mask"][:], ALU.mult))

    with Stage(nc, "grouped") as st:
        gates = st.sb("gates", [SPLIT, T], BF16)
        sel = st.sb("sel", [SPLIT, E, 128], BF16)
        router(nc, dram, xn, gates, "grouped", E, choose)
        up = st.sb("up", [HALF, 2, E + 1, HID])
        gate = st.sb("gate", [HALF, 2, E + 1, HID])
        down = st.sb("down", [HID, E + 1, D])
        bias = st.sb("bias", [HID, 2, E + 1])
        bd = st.sb("bd", [SPLIT, D])
        bd_rest = st.sb("bd_rest", [SPLIT, D])
        bd_parts = st.sb("bd_parts", [SPLIT, 3, D], BF16)
        y_bias = st.sb("y_bias", [HALF, 1, 2])
        load(nc, "grouped_load", [(up[:], dram["grouped_up"]), (gate[:], dram["grouped_gate"]),
                                  (down[:], dram["grouped_down"]), (bias[:], dram["grouped_bias"]),
                                  (bd[:], dram["grouped_bd"]), (y_bias[:], dram["grouped_cols"]),
                                  (sel[:], dram["sel"][:, 0:E])])
        split_weights(nc, "grouped_bd_split", bd, bd_rest, bd_parts)
        units = [dict(up=up[:, :, e], gate=gate[:, :, e], down=down[:, e], n=HID, row=e if e < E else None)
                 for e in range(E + 1)]
        expert_mlps(nc, h, xn, gates, sel, "grouped", units, ACT.Silu, bias, y_bias,
                    [bd_parts[:, i] for i in range(3)])


def top2(n):
    def choose(dve, link, rank, over, last, b, f, g, c):
        rank(f["rank"][:, :, 0:n], f["probs"][:, :, 0:n], n, "expert")
        link(dve.tensor_scalar(f["mask"][:, :, 0:n], f["rank"][:, :, 0:n], 1.5, None, ALU.is_lt))
        link(dve.tensor_tensor(f["weight"][:, :, 0:n], f["probs"][:, :, 0:n], f["mask"][:, :, 0:n], ALU.mult))
    return choose


def shared_experts(nc, dram, h, xn):
    E, HID, SHARED = 8, 192, 768

    def choose(dve, link, rank, over, last, b, f, g, c):
        top2(E)(dve, link, rank, over, last, b, f, g, c)
        w, alpha = f["weight"][:, :, 0:E], f["weight"][:, :, E]
        link(dve.tensor_reduce(c["total"][:], w, AX.X, ALU.add))
        link(dve.reciprocal(c["recip"][:], c["total"][:]))
        link(dve.tensor_tensor(w, w, last(c["recip"][:], E), ALU.mult))
        link(dve.tensor_scalar(c["u"][:], f["exps"][:, :, E], 1.0, None, ALU.add))
        link(dve.reciprocal(c["v"][:], c["u"][:]))
        link(dve.tensor_copy(alpha, c["v"][:]))
        link(dve.tensor_scalar(c["u"][:], c["v"][:], -1.0, 1.0, ALU.mult, ALU.add))
        link(dve.tensor_tensor(w, w, last(c["u"][:], E), ALU.mult))

    with Stage(nc, "shared") as st:
        gates = st.sb("gates", [SPLIT, T], BF16)
        sel = st.sb("sel", [SPLIT, E + 1, 128], BF16)
        router(nc, dram, xn, gates, "shared", E, choose, extra=1)
        W = E * HID + SHARED
        up = st.sb("up", [HALF, 2, W])
        gate = st.sb("gate", [HALF, 2, W])
        down_r = st.sb("down_r", [HALF, E * 2, D])
        down_s = st.sb("down_s", [128, SHARED // 128, D])
        load(nc, "shared_load", [(up[:], dram["shared_up"]), (gate[:], dram["shared_gate"]),
                                 (down_r[:], dram["shared_down_r"]), (down_s[:], dram["shared_down_s"]),
                                 (sel[:], dram["sel"][:, 0:E + 1])])
        units = [dict(up=up[:, :, k * HALF:(k + 1) * HALF], gate=gate[:, :, k * HALF:(k + 1) * HALF],
                      down=down_r[:, k], n=HALF, row=k // 2) for k in range(2 * E)]
        for k in range(SHARED // 128):
            cols = slice(E * HID + k * 128, E * HID + (k + 1) * 128)
            units.append(dict(up=up[:, :, cols], gate=gate[:, :, cols], down=down_s[:, k], n=128, row=E))
        expert_mlps(nc, h, xn, gates, sel, "shared", units, ACT.Silu, None, None, [])


def gelu_experts(nc, dram, h, xn):
    E, HID = 8, 768
    with Stage(nc, "geluexp") as st:
        gates = st.sb("gates", [SPLIT, T], BF16)
        sel = st.sb("sel", [SPLIT, E, 128], BF16)
        router(nc, dram, xn, gates, "geluexp", E, top2(E))
        up = st.sb("up", [HALF, 2, E * HID])
        down = st.sb("down", [128, E * HID // 128, D])
        load(nc, "geluexp_load", [(up[:], dram["geluexp_up"]), (down[:], dram["geluexp_down"]),
                                  (sel[:], dram["sel"][:, 0:E])])
        units = [dict(up=up[:, :, k * 128:(k + 1) * 128], gate=None, down=down[:, k], n=128,
                      row=k // (HID // 128)) for k in range(E * HID // 128)]
        expert_mlps(nc, h, xn, gates, sel, "geluexp", units, ACT.Gelu_apprx_tanh, None, None, [])


INNER = 2 * D
IC = INNER // 128
STATES = 16
DCONV = 4
RANK = 12
MG = 2
MT = MG * N
MTILES = ITEMS // MG
AHEAD = 2
FLAGS_AT = 7
COLLECT_AT = 12
SMALL = 1 / 32


def mamba(nc, dram, xn, mout, which):
    back = which == "b"
    PREP = [("u", 0), ("u", 1), ("u", 2), ("conv", 0), ("conv", 1), ("conv", 2), ("xd", 0),
            ("dt", 0), ("dt", 1), ("dt", 2), ("z", 0), ("z", 1), ("z", 2)]
    SLOTS = [[("u", 0), ("u", 1)], [("u", 2), ("conv", 0)], [("conv", 1)], [("conv", 2)], [("xd", 0)],
             [("dt", 0), ("dt", 1)], [("dt", 2)], [("out", 0)], [("out", 1)], [("z", 0)], [("z", 1)], [("z", 2)]]
    SLOTS += [[] for _ in range(STATES - len(SLOTS))]
    PER_STEP = len(PREP) + 2
    LAST = MTILES - 1

    def slots(first, last):
        count, out = 0, []
        for pieces in SLOTS:
            kept = [(k, c) for k, c in pieces if not (first and k == "out") and not (last and k != "out")]
            out.append([(count + i, k, c) for i, (k, c) in enumerate(kept)])
            count += len(kept)
        return out

    def pieces_before(t, first):
        return len(PREP) if first else 2 * len(PREP) + PER_STEP * (t - 1)

    def run(engine, body):
        body(0, 0, True, False)
        with engine.Fori(0, (MTILES - 2) // 2) as i:
            body(2 * i + 1, 1, False, False)
            body(2 * i + 2, 0, False, False)
        body(LAST, LAST % 2, False, True)

    with Stage(nc, "mamba_" + which) as st:
        in_w = st.sb("in_w", [HALF, 2, 2 * INNER])
        x_w = st.sb("x_w", [128, IC, 128])
        dt_w = st.sb("dt_w", [RANK, INNER])
        out_w = st.sb("out_w", [128, IC, D])
        cols = st.sb("cols", [128, IC, DCONV + 3])
        A = st.sb("A", [128, IC, STATES])
        A_log = st.sb("A_log", [128, IC, STATES])
        ident = st.sb("ident", [128, 128])
        diag = st.sb("diag", [128, IC, DCONV, 128])
        sel = st.sb("sel", [128, 2 * STATES, 128], BF16)
        upad = st.sb("upad", [128, IC, MG, N + 2 * (DCONV - 1)])
        uc = st.sb("uc", [128, 2, IC, MT])
        sz = st.sb("sz", [128, 2, IC, MT])
        xd = st.sb("xd", [128, MT])
        xd_rest = st.sb("xd_rest", [128, MT])
        xd_part = st.sb("xd_part", [128, MT], BF16)
        zeros = st.sb("zeros", [128, MT])
        parts = st.sb("parts", [128, 2, MT], BF16)
        pre = st.sb("pre", [128, IC, MT])
        soft = st.sb("soft", [128, IC, MT])
        log = st.sb("log", [128, IC, MT])
        series = st.sb("series", [128, IC, MT])
        e2 = st.sb("e2", [128, IC, MT])
        third = st.sb("third", [128, IC, MT])
        small = st.sb("small", [128, 2, IC, MT])
        dt = st.sb("dt", [128, 2, IC, MT])
        dtu = st.sb("dtu", [128, 2, IC, MT])
        decay = st.sb("decay", [128, AHEAD + 2, IC, MG, N])
        inject = st.sb("inject", [128, 2, IC, MT])
        state = st.sb("state", [128, 2, IC, MT])
        seen = st.sb("seen", [128, 2, IC, MT])
        yd = st.sb("yd", [128, IC, MT])
        gated = st.sb("gated", [128, IC, MT])
        o = st.sb("o", [HALF, 2, MT])
        work_ps = st.ps("work_ps", [128, 512])
        y_ps = st.ps("y_ps", [128, IC, 512])
        b_ps = st.ps("b_ps", [128, 2, 512])
        c_ps = st.ps("c_ps", [128, 2, 512])
        names = ("loaded zeroed consts a_ready work_done work_read uc_ready sz_ready parts_ready soft_step small_ready "
                 "own_step dt_ready dtu_ready bc_done decay_ready inject_ready scanned seen_ready summed yd_ready "
                 "gated_ready mout_ready").split()
        sem = {n: st.sem(n) for n in names}

        def tile(t):
            return ds(t * MT, MT)

        with st.block() as block:
            @block.sync
            def _(sp):
                for dst, src in ((in_w, which + "_in"), (x_w, which + "_x"), (dt_w, which + "_dt"),
                                 (out_w, which + "_out"), (cols, which + "_cols"), (A_log, which + "_A_log")):
                    sp.dma_start(dst[:], dram["mamba_" + src]).then_inc(sem["loaded"], 16)
                sp.dma_start(ident[:], dram["ident"]).then_inc(sem["loaded"], 16)
                sp.dma_start(sel[:], dram["state_sel"]).then_inc(sem["loaded"], 16)

            @block.gpsimd
            def _(pool):
                pool.memset(zeros[:], 0.0).then_inc(sem["zeroed"], 1)
                pool.memset(upad[:], 0.0).then_inc(sem["zeroed"], 1)
                pool.memset(decay[:], 0.0).then_inc(sem["zeroed"], 1)
                pool.wait_ge(sem["loaded"], 128)
                for c in range(IC):
                    for k in range(DCONV):
                        pool.tensor_scalar(diag[:, c, k, :], ident[:], cols[:, c, k:k + 1], None,
                                           ALU.mult).then_inc(sem["consts"], 1)

                def copy(out, in_):
                    return pool.tensor_scalar(out, in_, 1.0, 0.0, ALU.mult, ALU.add)

                def prepare(t, q, read, fresh):
                    count = [0]

                    def then(ins):
                        count[0] += 1
                        ins.then_inc(sem["own_step"], 1)
                        pool.wait_ge(sem["own_step"], count[0])

                    pool.sem_clear(sem["own_step"])
                    pool.wait_ge(sem["work_read"], read)
                    if not fresh:
                        pool.wait_ge(sem["bc_done"], STATES * (t - 1))
                    then(pool.tensor_tensor(xd_part[:], xd[:], zeros[:], ALU.add))
                    then(copy(parts[0:64, q, :], xd_part[0:64, :]))
                    then(pool.tensor_tensor(xd_rest[:], xd[:], xd_part[:], ALU.subtract))
                    then(copy(xd_part[:], xd_rest[:]))
                    then(copy(parts[64:96, q, :], xd_part[64:96, :]))
                    then(pool.tensor_tensor(xd_rest[:], xd_rest[:], xd_part[:], ALU.subtract))
                    copy(parts[96:128, q, :], xd_rest[96:128, :]).then_inc(sem["parts_ready"], 1)
                    pool.wait_ge(sem["parts_ready"], t + 1)
                    pool.wait_ge(sem["soft_step"], 3 * t + 2)
                    if not fresh:
                        pool.wait_ge(sem["decay_ready"], STATES * (t - 1))
                        pool.wait_ge(sem["inject_ready"], STATES * (t - 1))
                    then(pool.tensor_tensor(e2[:], soft[:], soft[:], ALU.mult))
                    then(pool.tensor_scalar(series[:], e2[:], -0.25, -0.5, ALU.mult, ALU.add))
                    then(pool.tensor_scalar(third[:], soft[:], 1 / 3, 0.0, ALU.mult, ALU.add))
                    then(pool.tensor_tensor(series[:], series[:], third[:], ALU.add))
                    then(pool.tensor_tensor(series[:], series[:], e2[:], ALU.mult))
                    then(pool.tensor_tensor(series[:], series[:], soft[:], ALU.add))
                    pool.wait_ge(sem["small_ready"], 2 * t + 2)
                    then(pool.tensor_tensor(series[:], series[:], small[:, 0], ALU.mult))
                    pool.wait_ge(sem["soft_step"], 3 * t + 3)
                    then(pool.tensor_tensor(log[:], log[:], small[:, 1], ALU.mult))
                    then(pool.tensor_tensor(log[:], log[:], series[:], ALU.add))
                    then(pool.tensor_scalar(series[:], pre[:], 3e38, 0.0, ALU.min, ALU.max))
                    pool.tensor_tensor(dt[:, q], series[:], log[:], ALU.add).then_inc(sem["dt_ready"], 1)
                    pool.wait_ge(sem["dt_ready"], t + 1)
                    pool.wait_ge(sem["uc_ready"], t + 1)
                    pool.tensor_tensor(dtu[:, q], dt[:, q], uc[:, q], ALU.mult).then_inc(sem["dtu_ready"], 1)

                pool.wait_ge(sem["zeroed"], 3)
                prepare(0, 0, 7, True)

                def body(t, p, first, last):
                    at = {(k, c): i for slot in slots(first, last) for i, k, c in slot}
                    w0 = pieces_before(t, first)
                    if not last:
                        prepare(t + 1, 1 - p, w0 + at["xd", 0] + 1, first)

                run(pool, body)

            @block.tensor
            def _(pe):
                pe.wait_ge(sem["loaded"], 128)
                pe.wait_ge(sem["consts"], IC * DCONV)
                pe.wait_ge(sem["zeroed"], 3)

                def piece(t, q, kind, c, w, none_before=False):
                    if not none_before:
                        pe.wait_ge(sem["work_read"], w)
                    if kind in ("u", "z"):
                        col = (c if kind == "u" else IC + c) * 128
                        for j in range(2):
                            mm = pe.matmul(work_ps[:, 0:MT], in_w[:, j, col:col + 128], xn[:, j, tile(t)],
                                           start=(j == 0), stop=(j == 1))
                    elif kind == "conv":
                        for k in range(DCONV):
                            shift = 2 * (DCONV - 1) - k if back else k
                            mm = pe.matmul(work_ps[:, 0:MT].rearrange("p (b n) -> p b n", b=MG), diag[:, c, k, :],
                                           upad[:, c, :, shift:shift + N], start=(k == 0), stop=(k == DCONV - 1))
                    elif kind == "xd":
                        pe.wait_ge(sem["uc_ready"], t + 1)
                        for k in range(IC):
                            mm = pe.matmul(work_ps[:, 0:MT], x_w[:, k, :], uc[:, q, k, :], start=(k == 0),
                                           stop=(k == IC - 1))
                    elif kind == "dt":
                        mm = pe.matmul(work_ps[:, 0:MT], dt_w[:, c * 128:(c + 1) * 128], xd[0:RANK, :], start=True,
                                       stop=True)
                    else:
                        pe.wait_ge(sem["gated_ready"], t + 1)
                        for k in range(IC):
                            mm = pe.matmul(work_ps[0:HALF, 0:MT], out_w[:, k, c * HALF:(c + 1) * HALF], gated[:, k, :],
                                           start=(k == 0), stop=(k == IC - 1))
                    mm.then_inc(sem["work_done"], 1)

                def broadcast(n, q):
                    pe.matmul(b_ps[:, n % 2, 0:MT], sel[:, n, :], parts[:, q, :], start=True, stop=True)
                    pe.matmul(c_ps[:, n % 2, 0:MT], sel[:, STATES + n, :], parts[:, q, :], start=True,
                              stop=True).then_inc(sem["bc_done"], 1)

                for i, (kind, c) in enumerate(PREP):
                    piece(0, 0, kind, c, i, i == 0)
                pe.wait_ge(sem["parts_ready"], 1)
                for n in range(AHEAD):
                    broadcast(n, 0)

                def body(t, p, first, last):
                    w0 = pieces_before(t, first)

                    for n, slot in enumerate(slots(first, last)):
                        pe.wait_ge(sem["seen_ready"], t * STATES + n + 1)
                        if n + AHEAD < STATES:
                            broadcast(n + AHEAD, p)
                        elif not last:
                            pe.wait_ge(sem["parts_ready"], t + 2)
                            broadcast(n + AHEAD - STATES, 1 - p)
                        if n == 0 and not first:
                            pe.wait_ge(sem["yd_ready"], IC * t)
                        for c in range(IC):
                            mm = pe.matmul(y_ps[:, c, 0:MT], ident[:], seen[:, n % 2, c, :], start=(n == 0),
                                           stop=(n == STATES - 1))
                        mm.then_inc(sem["summed"], 1)
                        for i, kind, c in slot:
                            if kind == "out":
                                piece(t - 1, 1 - p, kind, c, w0 + i)
                            else:
                                piece(t + 1, 1 - p, kind, c, w0 + i)

                run(pe, body)
                for m in range(2):
                    piece(LAST, LAST % 2, "out", m, pieces_before(LAST, False) + 2 + m)

            @block.scalar
            def _(act):
                act.wait_ge(sem["loaded"], 128)
                act.wait_ge(sem["zeroed"], 3)
                act.activation(A[:], A_log[:], ACT.Exp).then_inc(sem["a_ready"], 1)
                act.wait_ge(sem["a_ready"], 2)

                def piece(t, q, kind, c, w, fresh):
                    def empty(out, func, src=work_ps[:, 0:MT], **kw):
                        act.wait_ge(sem["work_done"], w + 1)
                        act.activation(out, src, func, **kw).then_inc(sem["work_read"], 1)

                    if kind == "u":
                        empty(upad[:, c, :, DCONV - 1:DCONV - 1 + N], ACT.Copy,
                              src=work_ps[:, 0:MT].rearrange("p (b n) -> p b n", b=MG))
                    elif kind == "conv":
                        if c == 0 and not fresh:
                            act.wait_ge(sem["yd_ready"], IC * (t - 1))
                        empty(uc[:, q, c, :], ACT.Identity, bias=cols[:, c, DCONV:DCONV + 1])
                        if c == IC - 1:
                            act.wait_ge(sem["work_read"], w + 1)
                            act.activation(uc[:, q], uc[:, q], ACT.Silu).then_inc(sem["uc_ready"], 1)
                    elif kind == "xd":
                        empty(xd[:], ACT.Copy)
                    elif kind == "dt":
                        empty(pre[:, c, :], ACT.Identity, bias=cols[:, c, DCONV + 1:DCONV + 2])
                        if c == IC - 1:
                            act.wait_ge(sem["work_read"], w + 1)
                            act.activation(soft[:], pre[:], ACT.Abs).then_inc(sem["soft_step"], 1)
                            act.wait_ge(sem["soft_step"], 3 * t + 1)
                            act.activation(soft[:], soft[:], ACT.Exp, scale=-1.0).then_inc(sem["soft_step"], 1)
                            act.wait_ge(sem["soft_step"], 3 * t + 2)
                            act.activation(log[:], soft[:], ACT.Ln, bias=1.0).then_inc(sem["soft_step"], 1)
                    elif kind == "z":
                        if c == 0 and not fresh:
                            act.wait_ge(sem["gated_ready"], t - 1)
                        empty(sz[:, q, c, :], ACT.Copy)
                    else:
                        empty(o[:, c, :], ACT.Copy, src=work_ps[0:HALF, 0:MT])

                a, b = (0, N - 1) if back else (1, N)

                def decays(n, q):
                    for c in range(IC):
                        ins = act.activation(decay[:, n % (AHEAD + 2), c, :, a:b],
                                             dt[:, q, c, :].rearrange("p (b n) -> p b n", b=MG)[:, :, a:b],
                                             ACT.Exp, scale=A[:, c, n:n + 1])
                    ins.then_inc(sem["decay_ready"], 1)

                for i, (kind, c) in enumerate(PREP):
                    piece(0, 0, kind, c, i, True)
                act.wait_ge(sem["dt_ready"], 1)
                for n in range(AHEAD):
                    decays(n, 0)

                def body(t, p, first, last):
                    w0 = pieces_before(t, first)
                    def silu_z():
                        act.wait_ge(sem["work_read"], w0)
                        act.activation(sz[:, p], sz[:, p], ACT.Silu).then_inc(sem["sz_ready"], 1)

                    for n, slot in enumerate(slots(first, last)):
                        if not first or n >= 2:
                            act.wait_ge(sem["scanned"], t * STATES + n - 1)
                        if n + AHEAD < STATES:
                            decays(n + AHEAD, p)
                        elif not last:
                            act.wait_ge(sem["dt_ready"], t + 2)
                            decays(n + AHEAD - STATES, 1 - p)
                        for i, kind, c in slot:
                            if kind == "out":
                                piece(t - 1, 1 - p, kind, c, w0 + i, False)
                            else:
                                piece(t + 1, 1 - p, kind, c, w0 + i, first)
                            if (kind, c) == ("conv", IC - 1):
                                silu_z()
                    if last:
                        silu_z()

                run(act, body)
                act.wait_ge(sem["mout_ready"], LAST)
                for m in range(2):
                    piece(LAST, LAST % 2, "out", m, pieces_before(LAST, False) + 2 + m, False)

            @block.vector
            def _(dve):
                dve.wait_ge(sem["a_ready"], 1)
                dve.tensor_scalar(A[:], A[:], -1.0, None, ALU.mult).then_inc(sem["a_ready"], 1)

                def flags(t, fresh):
                    dve.wait_ge(sem["soft_step"], 3 * t + 2)
                    if not fresh:
                        dve.wait_ge(sem["dt_ready"], t)
                    dve.tensor_scalar(small[:, 0], soft[:], SMALL, None, ALU.is_lt).then_inc(sem["small_ready"], 1)
                    dve.tensor_scalar(small[:, 1], soft[:], SMALL, None, ALU.is_ge).then_inc(sem["small_ready"], 1)

                def gate(t, p):
                    dve.wait_ge(sem["summed"], STATES * (t + 1))
                    for c in range(IC):
                        dve.scalar_tensor_tensor(out=yd[:, c, :], in0=uc[:, p, c, :], scalar=cols[:, c, DCONV + 2:DCONV + 3],
                                                 in1=y_ps[:, c, 0:MT], op0=ALU.mult,
                                                 op1=ALU.add).then_inc(sem["yd_ready"], 1)
                    dve.wait_ge(sem["yd_ready"], IC * (t + 1))
                    dve.wait_ge(sem["sz_ready"], t + 1)
                    dve.tensor_tensor(gated[:], yd[:], sz[:, p], ALU.mult).then_inc(sem["gated_ready"], 1)

                def collect(t, read):
                    dve.wait_ge(sem["work_read"], read)
                    base = mout if back else xn
                    dve.tensor_tensor(mout[:, :, tile(t)], o[:], base[:, :, tile(t)],
                                      ALU.add).then_inc(sem["mout_ready"], 1)

                flags(0, True)

                def body(t, p, first, last):
                    s0 = t * STATES

                    def inject_(n):
                        dve.wait_ge(sem["bc_done"], s0 + n + 1)
                        dve.tensor_tensor(inject[:, n % 2], dtu[:, p],
                                          b_ps[:, n % 2, 0:MT].unsqueeze(1).broadcast_to([128, IC, MT]),
                                          ALU.mult).then_inc(sem["inject_ready"], 1)

                    dve.wait_ge(sem["dtu_ready"], t + 1)
                    inject_(0)
                    for n in range(STATES):
                        flat = [state[:, n % 2].rearrange("p c n -> p (c n)"),
                                decay[:, n % (AHEAD + 2)].rearrange("p c b n -> p (c b n)"),
                                inject[:, n % 2].rearrange("p c n -> p (c n)")]
                        if back:
                            flat = [x[:, ::-1] for x in flat]
                        dve.wait_ge(sem["decay_ready"], s0 + n + 1)
                        dve.wait_ge(sem["inject_ready"], s0 + n + 1)
                        dve.tensor_tensor_scan(flat[0], flat[1], flat[2], 0.0, ALU.mult,
                                               ALU.add).then_inc(sem["scanned"], 1)
                        if n + 1 < STATES:
                            inject_(n + 1)
                        if n == 0 and not first:
                            gate(t - 1, 1 - p)
                        dve.wait_ge(sem["scanned"], s0 + n + 1)
                        if not first or n >= 2:
                            dve.wait_ge(sem["summed"], s0 + n - 1)
                        dve.tensor_tensor(seen[:, n % 2], state[:, n % 2],
                                          c_ps[:, n % 2, 0:MT].unsqueeze(1).broadcast_to([128, IC, MT]),
                                          ALU.mult).then_inc(sem["seen_ready"], 1)
                        if n == FLAGS_AT and not last:
                            flags(t + 1, False)
                        if n == COLLECT_AT and not first:
                            at = {(k, c): i for slot in slots(first, last) for i, k, c in slot}
                            collect(t - 1, pieces_before(t, first) + at["out", 1] + 1)

                run(dve, body)
                gate(LAST, LAST % 2)
                collect(LAST, pieces_before(LAST, False) + 4)


def add_normed(nc, dram, h, mout):
    with Stage(nc, "addnorm") as st:
        averager = st.sb("averager", [HALF, HALF])
        eps = st.sb("eps", [HALF, 1])
        cols = st.sb("cols", [HALF, 2, 2])
        centred = st.sb("centred", [HALF, 2, TILE])
        squared = st.sb("squared", [HALF, 2, TILE])
        std = st.sb("std", [HALF, TILE])
        rstd = st.sb("rstd", [HALF, TILE])
        normed = st.sb("normed", [HALF, 2, TILE])
        scaled = st.sb("scaled", [HALF, 2, TILE])
        mean_ps = st.ps("mean", [HALF, 512])
        var_ps = st.ps("var", [HALF, 512])
        names = ("loaded consts mean_ready centred_ready squared_ready var_ready std_ready rstd_ready "
                 "normed_ready scaled_ready h_ready").split()
        sem = {n: st.sem(n) for n in names}
        with st.block() as block:
            @block.sync
            def _(sp):
                sp.dma_start(cols[:], dram["mamba_norm_cols"]).then_inc(sem["loaded"], 16)

            @block.gpsimd
            def _(pool):
                pool.memset(averager[:], 1.0 / D).then_inc(sem["consts"], 1)
                pool.memset(eps[:], 1e-12).then_inc(sem["consts"], 1)

            @block.tensor
            def _(pe):
                pe.wait_ge(sem["consts"], 2)
                for t in range(TILES):
                    for j in range(2):
                        mm = pe.matmul(mean_ps[:, 0:TILE], averager[:], mout[:, j, t * TILE:(t + 1) * TILE],
                                       start=(j == 0), stop=(j == 1))
                    mm.then_inc(sem["mean_ready"], 1)
                    pe.wait_ge(sem["squared_ready"], t + 1)
                    if t:
                        pe.wait_ge(sem["std_ready"], t)
                    for j in range(2):
                        mm = pe.matmul(var_ps[:, 0:TILE], averager[:], squared[:, j, :],
                                       start=(j == 0), stop=(j == 1))
                    mm.then_inc(sem["var_ready"], 1)

            @block.scalar
            def _(act):
                act.wait_ge(sem["consts"], 2)
                act.wait_ge(sem["loaded"], 16)
                for t in range(TILES):
                    act.wait_ge(sem["centred_ready"], t + 1)
                    act.activation(squared[:], centred[:], ACT.Square).then_inc(sem["squared_ready"], 1)
                    act.wait_ge(sem["var_ready"], t + 1)
                    if t:
                        act.wait_ge(sem["rstd_ready"], t)
                    act.activation(std[:], var_ps[:, 0:TILE], ACT.Sqrt, bias=eps[:]).then_inc(sem["std_ready"], 1)
                    act.wait_ge(sem["normed_ready"], t + 1)
                    if t:
                        act.wait_ge(sem["h_ready"], t)
                    for m in range(2):
                        act.activation(scaled[:, m, :], normed[:, m, :], ACT.Identity, bias=cols[:, 1, m:m + 1],
                                       scale=cols[:, 0, m:m + 1]).then_inc(sem["scaled_ready"], 1)

            @block.vector
            def _(dve):
                for t in range(TILES):
                    part = slice(t * TILE, (t + 1) * TILE)
                    dve.wait_ge(sem["mean_ready"], t + 1)
                    dve.tensor_tensor(centred[:], mout[:, :, part],
                                      mean_ps[:, 0:TILE].unsqueeze(1).broadcast_to([HALF, 2, TILE]),
                                      ALU.subtract).then_inc(sem["centred_ready"], 1)
                    dve.wait_ge(sem["std_ready"], t + 1)
                    dve.reciprocal(rstd[:], std[:]).then_inc(sem["rstd_ready"], 1)
                    dve.wait_ge(sem["rstd_ready"], t + 1)
                    dve.tensor_tensor(normed[:], centred[:], rstd[:].unsqueeze(1).broadcast_to([HALF, 2, TILE]),
                                      ALU.mult).then_inc(sem["normed_ready"], 1)
                    dve.wait_ge(sem["scaled_ready"], 2 * t + 2)
                    dve.tensor_tensor(h[:, :, part], h[:, :, part], scaled[:], ALU.add).then_inc(sem["h_ready"], 1)


def bidirectional_mamba(nc, dram, h, xn):
    with nc.sbuf_tensor("mout", [HALF, 2, T], F32) as mout:
        mamba(nc, dram, xn, mout, "f")
        mamba(nc, dram, xn, mout, "b")
        add_normed(nc, dram, h, mout)


def quantised_mlp(nc, dram, h, xn):
    HID = 768
    K = HID // 128
    LOW, HIGH = -8.0, 7.0
    ROUND = 1.5 * 2.0 ** 23
    with Stage(nc, "quant") as st:
        w1 = st.sb("w1", [HALF, 2, HID])
        w2 = st.sb("w2", [128, K, D])
        step_w1 = st.sb("step_w1", [HALF, HID])
        step_w2 = st.sb("step_w2", [128, D])
        inv_w1 = st.sb("inv_w1", [HALF, HID])
        inv_w2 = st.sb("inv_w2", [128, D])
        w1q = st.sb("w1q", [HALF, 2, HID], BF16)
        w2q = st.sb("w2q", [128, K, D], BF16)
        step_a1 = st.sb("step_a1", [HALF, 2])
        step_a2 = st.sb("step_a2", [HALF, HID // HALF])
        hid_cols = st.sb("hid_cols", [128, 2, K])
        out_cols = st.sb("out_cols", [HALF, 2, 2])
        ones = st.sb("ones", [HALF, 128])
        step_a = st.sb("step_a", [128, 2])
        inv_a = st.sb("inv_a", [128, 2])
        scale1 = st.sb("scale1", [128, K])
        scale2 = st.sb("scale2", [HALF, 2])
        xs = st.sb("xs", [HALF, 2, T])
        xq = st.sb("xq", [HALF, 2, T], BF16)
        g = st.sb("g", [128, K, TILE])
        gs = st.sb("gs", [128, K, TILE])
        gq = st.sb("gq", [128, K, TILE], BF16)
        y = st.sb("y", [HALF, 2, TILE])
        mean_ps = st.ps("mean_ps", [128, 2])
        up_ps = st.ps("up_ps", [128, 2, 512])
        y_ps = st.ps("y_ps", [HALF, 2, 512])
        loaded = st.sem("loaded")
        ones_ready = st.sem("ones_ready")
        mean_done = st.sem("mean_done")
        chain = st.sem("chain")
        ready = st.sem("ready")
        up_done = st.sem("up_done")
        g_ready = st.sem("g_ready")
        gq_step = st.sem("gq_step")
        gq_ready = st.sem("gq_ready")
        down_done = st.sem("down_done")
        y_ready = st.sem("y_ready")
        h_ready = st.sem("h_ready")
        with st.block() as block:
            @block.sync
            def _(sp):
                for dst, src in ((step_a1, "quant_a1"), (step_a2, "quant_a2"), (w1, "quant_w1"), (w2, "quant_w2"),
                                 (hid_cols, "quant_hid"), (out_cols, "quant_out")):
                    sp.dma_start(dst[:], dram[src]).then_inc(loaded, 16)
                sp.dma_start(step_w1[:], dram["quant_step_w1"].broadcast_to([HALF, HID])).then_inc(loaded, 16)
                sp.dma_start(step_w2[:], dram["quant_step_w2"].broadcast_to([128, D])).then_inc(loaded, 16)

            @block.gpsimd
            def _(pool):
                pool.memset(ones[:], 1.0).then_inc(ones_ready, 1)

            @block.tensor
            def _(pe):
                pe.wait_ge(loaded, 128)
                pe.wait_ge(ones_ready, 1)
                for i, steps_in in enumerate((step_a1, step_a2)):
                    n = steps_in[:].shape[1]
                    for j in range(n):
                        mm = pe.matmul(mean_ps[:, i:i + 1], ones[:], steps_in[:, j:j + 1],
                                       start=(j == 0), stop=(j == n - 1))
                mm.then_inc(mean_done, 1)
                pe.wait_ge(ready, 1)

                def step(t, first):
                    for k in range(K):
                        if not first or k >= 2:
                            pe.wait_ge(g_ready, t * K + k - 1)
                        for j in range(2):
                            mm = pe.matmul(up_ps[:, k % 2, 0:TILE], w1q[:, j, k * 128:(k + 1) * 128],
                                           xq[:, j, ds(t * TILE, TILE)], start=(j == 0), stop=(j == 1))
                        mm.then_inc(up_done, 1)
                    pe.wait_ge(gq_ready, t + 1)
                    if not first:
                        pe.wait_ge(y_ready, 2 * t)
                    for m in range(2):
                        for k in range(K):
                            mm = pe.matmul(y_ps[:, m, 0:TILE], w2q[:, k, m * HALF:(m + 1) * HALF], gq[:, k, :],
                                           start=(k == 0), stop=(k == K - 1))
                    mm.then_inc(down_done, 1)

                steps(pe, TILES, step)

            @block.scalar
            def _(act):
                act.wait_ge(ready, 1)

                def step(t, first):
                    if not first:
                        act.wait_ge(gq_step, 3 * t)
                    for k in range(K):
                        act.wait_ge(up_done, t * K + k + 1)
                        act.activation(g[:, k, :], up_ps[:, k % 2, 0:TILE], ACT.Gelu, bias=hid_cols[:, 1, k:k + 1],
                                       scale=scale1[:, k:k + 1]).then_inc(g_ready, 1)
                    act.wait_ge(down_done, t + 1)
                    if not first:
                        act.wait_ge(h_ready, t)
                    for m in range(2):
                        act.activation(y[:, m, :], y_ps[:, m, 0:TILE], ACT.Identity, bias=out_cols[:, 1, m:m + 1],
                                       scale=scale2[:, m:m + 1]).then_inc(y_ready, 1)

                steps(act, TILES, step)

            @block.vector
            def _(dve):
                count = [0]

                def link(ins):
                    count[0] += 1
                    ins.then_inc(chain, 1)
                    dve.wait_ge(chain, count[0])

                def quantise(out, scaled):
                    link(dve.tensor_scalar(scaled, scaled, HIGH, LOW, ALU.min, ALU.max))
                    link(dve.tensor_scalar(out, scaled, ROUND, ROUND, ALU.add, ALU.subtract))

                dve.wait_ge(loaded, 128)
                link(dve.reciprocal(inv_w1[:], step_w1[:]))
                link(dve.reciprocal(inv_w2[:], step_w2[:]))
                link(dve.tensor_tensor(w1[:], w1[:], inv_w1[:].unsqueeze(1).broadcast_to([HALF, 2, HID]), ALU.mult))
                quantise(w1q[:], w1[:])
                link(dve.tensor_tensor(w2[:], w2[:], inv_w2[:].unsqueeze(1).broadcast_to([128, K, D]), ALU.mult))
                quantise(w2q[:], w2[:])
                dve.wait_ge(mean_done, 1)
                link(dve.tensor_scalar(step_a[:, 0:1], mean_ps[:, 0:1], 1.0 / D, None, ALU.mult))
                link(dve.tensor_scalar(step_a[:, 1:2], mean_ps[:, 1:2], 1.0 / HID, None, ALU.mult))
                link(dve.reciprocal(inv_a[:], step_a[:]))
                link(dve.tensor_scalar(scale1[:], hid_cols[:, 0], step_a[:, 0:1], None, ALU.mult))
                link(dve.tensor_scalar(scale2[:], out_cols[:, 0], step_a[0:HALF, 1:2], None, ALU.mult))
                link(dve.tensor_scalar(xs[:], xn[:], inv_a[0:HALF, 0:1], None, ALU.mult))
                quantise(xq[:], xs[:])
                dve.nop().then_inc(ready, 1)

                def step(t, first):
                    dve.wait_ge(g_ready, (t + 1) * K)
                    dve.tensor_scalar(g[:], g[:], 10.0, -10.0, ALU.min, ALU.max).then_inc(gq_step, 1)
                    dve.wait_ge(gq_step, 3 * t + 1)
                    dve.tensor_scalar(gs[:], g[:], inv_a[:, 1:2], HIGH, ALU.mult, ALU.min).then_inc(gq_step, 1)
                    dve.wait_ge(gq_step, 3 * t + 2)
                    dve.tensor_scalar(gs[:], gs[:], LOW, ROUND, ALU.max, ALU.add).then_inc(gq_step, 1)
                    dve.wait_ge(gq_step, 3 * t + 3)
                    if not first:
                        dve.wait_ge(down_done, t)
                    dve.tensor_scalar(gq[:], gs[:], ROUND, None, ALU.subtract).then_inc(gq_ready, 1)
                    dve.wait_ge(y_ready, 2 * t + 2)
                    tile = h[:, :, ds(t * TILE, TILE)]
                    dve.tensor_tensor(tile, tile, y[:], ALU.add).then_inc(h_ready, 1)

                steps(dve, TILES, step)


CUT = ((0, 65), (65, 64))
QCUT = ((0, 65), (64, 65))


def group_attention(nc, dram, h, xn):
    GP = 49
    SCALE = D ** -0.5
    with Stage(nc, "groupattn") as st:
        w_qkv = st.sb("w_qkv", [HALF, 2, 3 * D])
        w_proj = st.sb("w_proj", [HALF, 2, D])
        w_gp = st.sb("w_gp", [HALF, 2, GP])
        cols = st.sb("cols", [HALF, 3, 2])
        v_bias = st.sb("v_bias", [65, D])
        ident = st.sb("ident", [65, 65])
        a = st.sb("a", [65, 4])
        x = st.sb("x", [HALF, 2, N])
        q = st.sb("q", [HALF, 2, N])
        k = st.sb("k", [HALF, 2, N])
        v = st.sb("v", [65, 2, D])
        g_in = st.sb("g_in", [65, 2, GP])
        g_top = st.sb("g_top", [65, 2])
        g_sum = st.sb("g_sum", [65, 2])
        g_inv = st.sb("g_inv", [65, 2])
        gw = st.sb("gw", [65, 2, GP])
        gwt = st.sb("gwt", [GP, N])
        top = st.sb("top", [65, 2])
        bias = st.sb("bias", [65, 2])
        total = st.sb("total", [65, 2])
        inv = st.sb("inv", [65, 2])
        e = st.sb("e", [65, 2, N])
        mix = st.sb("mix", [65, 2, N])
        wt = st.sb("wt", [65, 2, N])
        wtt = st.sb("wtt", [65, 2, N])
        heads = st.sb("heads", [HALF, 2, N])
        bank_a = st.ps("bank_a", [128, 512])
        bank_b = st.ps("bank_b", [128, 512])
        bank_c = st.ps("bank_c", [128, 512])
        bank_d = st.ps("bank_d", [128, 512])
        bank_e = st.ps("bank_e", [128, 512])
        bank_f = st.ps("bank_f", [128, 512])

        def view(bank, p, a_, b_):
            return bank[0:p, 0:a_ * b_].rearrange("p (a b) -> p a b", a=a_)

        q_ps = view(bank_a, HALF, 2, N)
        group_ps = view(bank_a, 65, 2, N)
        k_ps = view(bank_b, HALF, 2, N)
        out_ps = view(bank_b, HALF, 2, N)
        v_ps = view(bank_c, 65, 2, D)
        o_ps = view(bank_c, HALF, 2, N)
        g_ps = view(bank_d, 65, 2, GP)
        gwt_ps = bank_d[0:GP, 0:N]
        s_ps = view(bank_e, 65, 2, N)
        wtt_ps = view(bank_f, 65, 2, N)
        names = ("loaded x_ready qkv_done q_ready k_ready v_ready g_done g_top g_in g_exp g_sum g_inv gw_ready "
                 "gwt_done gwt_ready s_done top_ready bias_ready e_ready inv_ready group_done mix_ready wt_ready "
                 "wtt_done wtt_ready out_done heads_ready proj_done h_ready a_step").split()
        sem = {n: st.sem(n) for n in names}
        with st.block() as block:
            @block.sync
            def _(sp):
                for dst, src in ((w_qkv, "groupattn_qkv"), (w_proj, "groupattn_proj"), (w_gp, "groupattn_gp"),
                                 (cols, "groupattn_cols")):
                    sp.dma_start(dst[:], dram[src]).then_inc(sem["loaded"], 16)
                sp.dma_start(v_bias[:], dram["groupattn_v_bias"].broadcast_to([65, D])).then_inc(sem["loaded"], 16)
                sp.dma_start(a[:, 0:1], dram["groupattn_alpha"].broadcast_to([65, 1])).then_inc(sem["loaded"], 16)
                sp.dma_start(ident[:], dram["ident"][0:65, 0:65]).then_inc(sem["loaded"], 16)

            @block.gpsimd
            def _(pool):
                def step(b, first):
                    if not first:
                        pool.wait_ge(sem["qkv_done"], b)
                    pool.tensor_copy(x[:], xn[:, :, ds(b * N, N)]).then_inc(sem["x_ready"], 1)

                steps(pool, ITEMS, step)

            @block.tensor
            def _(pe):
                pe.wait_ge(sem["loaded"], 112)

                def step(b, first):
                    pe.wait_ge(sem["x_ready"], b + 1)
                    if not first:
                        pe.wait_ge(sem["h_ready"], 2 * b)
                    for ps, w0 in ((q_ps, 0), (k_ps, D)):
                        for m in range(2):
                            for j in range(2):
                                pe.matmul(ps[:, m, :], w_qkv[:, j, w0 + m * HALF:w0 + (m + 1) * HALF], x[:, j, :],
                                          start=(j == 0), stop=(j == 1))
                    for c, (c0, n) in enumerate(CUT):
                        for j in range(2):
                            mm = pe.matmul(v_ps[0:n, c, :], x[:, j, c0:c0 + n], w_qkv[:, j, 2 * D:],
                                           start=(j == 0), stop=(j == 1))
                    mm.then_inc(sem["qkv_done"], 1)
                    pe.wait_ge(sem["q_ready"], 2 * b + 2)
                    for c, (c0, n) in enumerate(CUT):
                        for j in range(2):
                            mm = pe.matmul(g_ps[0:n, c, :], q[:, j, c0:c0 + n], w_gp[:, j, :],
                                           start=(j == 0), stop=(j == 1))
                    mm.then_inc(sem["g_done"], 1)
                    pe.wait_ge(sem["k_ready"], 2 * b + 2)
                    for c, (c0, n) in enumerate(CUT):
                        for j in range(2):
                            mm = pe.matmul(s_ps[0:n, c, :], q[:, j, c0:c0 + n], k[:, j, :],
                                           start=(j == 0), stop=(j == 1))
                    mm.then_inc(sem["s_done"], 1)
                    pe.wait_ge(sem["loaded"], 112)
                    pe.wait_ge(sem["gw_ready"], 2 * b + 2)
                    for c, (c0, n) in enumerate(CUT):
                        mm = pe.transpose(gwt_ps[:, c0:c0 + n], gw[0:n, c, :], ident[0:n, 0:n])
                    mm.then_inc(sem["gwt_done"], 1)
                    pe.wait_ge(sem["gwt_ready"], b + 1)
                    for c, (c0, n) in enumerate(CUT):
                        mm = pe.matmul(group_ps[0:n, c, :], gwt[:, c0:c0 + n], gwt[:], start=True, stop=True)
                    mm.then_inc(sem["group_done"], 1)
                    pe.wait_ge(sem["loaded"], 112)
                    pe.wait_ge(sem["wt_ready"], 2 * b + 2)
                    for c, (c0, n) in enumerate(CUT):
                        for d, (d0, l) in enumerate(CUT):
                            mm = pe.transpose(wtt_ps[0:l, d, c0:c0 + n], wt[0:n, c, d0:d0 + l], ident[0:n, 0:n])
                    mm.then_inc(sem["wtt_done"], 1)
                    pe.wait_ge(sem["v_ready"], 2 * b + 2)
                    pe.wait_ge(sem["wtt_ready"], 2 * b + 2)
                    for m in range(2):
                        for d, (d0, l) in enumerate(CUT):
                            mm = pe.matmul(out_ps[:, m, :], v[0:l, d, m * HALF:(m + 1) * HALF], wtt[0:l, d, :],
                                           start=(d == 0), stop=(d == 1))
                    mm.then_inc(sem["out_done"], 1)
                    pe.wait_ge(sem["heads_ready"], b + 1)
                    for m in range(2):
                        for j in range(2):
                            mm = pe.matmul(o_ps[:, m, :], w_proj[:, j, m * HALF:(m + 1) * HALF], heads[:, j, :],
                                           start=(j == 0), stop=(j == 1))
                    mm.then_inc(sem["proj_done"], 1)

                steps(pe, ITEMS, step)

            @block.scalar
            def _(act):
                act.wait_ge(sem["loaded"], 112)
                act.activation(a[:, 1:2], a[:, 0:1], ACT.Exp, scale=-1.0).then_inc(sem["a_step"], 1)

                def step(b, first):
                    act.wait_ge(sem["qkv_done"], b + 1)
                    for m in range(2):
                        act.activation(q[:, m, :], q_ps[:, m, :], ACT.Identity,
                                       bias=cols[:, 0, m:m + 1]).then_inc(sem["q_ready"], 1)
                    act.wait_ge(sem["g_in"], 2 * b + 2)
                    for c, (c0, n) in enumerate(CUT):
                        act.activation(g_in[0:n, c, :], g_in[0:n, c, :], ACT.Exp,
                                       accum_out=g_sum[0:n, c:c + 1]).then_inc(sem["g_exp"], 1)
                    act.wait_ge(sem["bias_ready"], 2 * b + 2)
                    for c, (c0, n) in enumerate(CUT):
                        act.activation(e[0:n, c, :], s_ps[0:n, c, :], ACT.Exp, bias=bias[0:n, c:c + 1], scale=SCALE,
                                       accum_out=total[0:n, c:c + 1]).then_inc(sem["e_ready"], 1)
                    act.wait_ge(sem["gwt_done"], b + 1)
                    act.activation(gwt[:], gwt_ps, ACT.Copy).then_inc(sem["gwt_ready"], 1)
                    act.wait_ge(sem["wtt_done"], b + 1)
                    for d, (d0, l) in enumerate(CUT):
                        act.activation(wtt[0:l, d, :], wtt_ps[0:l, d, :], ACT.Copy).then_inc(sem["wtt_ready"], 1)
                    act.wait_ge(sem["out_done"], b + 1)
                    act.activation(heads[:], out_ps, ACT.Copy).then_inc(sem["heads_ready"], 1)

                steps(act, ITEMS, step)

            @block.vector
            def _(dve):
                dve.wait_ge(sem["a_step"], 1)
                dve.tensor_scalar(a[:, 3:4], a[:, 1:2], 1.0, None, ALU.add).then_inc(sem["a_step"], 1)
                dve.wait_ge(sem["a_step"], 2)
                dve.reciprocal(a[:, 2:3], a[:, 3:4]).then_inc(sem["a_step"], 1)
                dve.wait_ge(sem["a_step"], 3)
                dve.tensor_scalar(a[:, 3:4], a[:, 2:3], -1.0, 1.0, ALU.mult, ALU.add).then_inc(sem["a_step"], 1)
                dve.wait_ge(sem["a_step"], 4)

                def step(b, first):
                    dve.wait_ge(sem["qkv_done"], b + 1)
                    for m in range(2):
                        dve.tensor_scalar(k[:, m, :], k_ps[:, m, :], cols[:, 1, m:m + 1], None,
                                          ALU.add).then_inc(sem["k_ready"], 1)
                    for c, (c0, n) in enumerate(CUT):
                        dve.tensor_tensor(v[0:n, c, :], v_ps[0:n, c, :], v_bias[0:n, :],
                                          ALU.add).then_inc(sem["v_ready"], 1)
                    dve.wait_ge(sem["g_done"], b + 1)
                    for c, (c0, n) in enumerate(CUT):
                        dve.tensor_reduce(g_top[0:n, c:c + 1], g_ps[0:n, c, :], AX.X, ALU.max).then_inc(sem["g_top"], 1)
                    dve.wait_ge(sem["g_top"], 2 * b + 2)
                    for c, (c0, n) in enumerate(CUT):
                        dve.tensor_scalar(g_in[0:n, c, :], g_ps[0:n, c, :], g_top[0:n, c:c + 1], None,
                                          ALU.subtract).then_inc(sem["g_in"], 1)
                    dve.wait_ge(sem["s_done"], b + 1)
                    for c, (c0, n) in enumerate(CUT):
                        dve.tensor_reduce(top[0:n, c:c + 1], s_ps[0:n, c, :], AX.X, ALU.max).then_inc(sem["top_ready"], 1)
                    dve.wait_ge(sem["top_ready"], 2 * b + 2)
                    for c, (c0, n) in enumerate(CUT):
                        dve.tensor_scalar(bias[0:n, c:c + 1], top[0:n, c:c + 1], -SCALE, None,
                                          ALU.mult).then_inc(sem["bias_ready"], 1)
                    dve.wait_ge(sem["g_exp"], 2 * b + 2)
                    for c, (c0, n) in enumerate(CUT):
                        dve.reciprocal(g_inv[0:n, c:c + 1], g_sum[0:n, c:c + 1]).then_inc(sem["g_inv"], 1)
                    dve.wait_ge(sem["g_inv"], 2 * b + 2)
                    for c, (c0, n) in enumerate(CUT):
                        dve.tensor_scalar(gw[0:n, c, :], g_in[0:n, c, :], g_inv[0:n, c:c + 1], None,
                                          ALU.mult).then_inc(sem["gw_ready"], 1)
                    dve.wait_ge(sem["e_ready"], 2 * b + 2)
                    for c, (c0, n) in enumerate(CUT):
                        dve.reciprocal(inv[0:n, c:c + 1], total[0:n, c:c + 1]).then_inc(sem["inv_ready"], 1)
                    dve.wait_ge(sem["group_done"], b + 1)
                    for c, (c0, n) in enumerate(CUT):
                        dve.tensor_scalar(mix[0:n, c, :], group_ps[0:n, c, :], a[0:n, 3:4], a[0:n, 2:3], ALU.mult,
                                          ALU.add).then_inc(sem["mix_ready"], 1)
                    dve.wait_ge(sem["inv_ready"], 2 * b + 2)
                    dve.wait_ge(sem["mix_ready"], 2 * b + 2)
                    for c, (c0, n) in enumerate(CUT):
                        dve.scalar_tensor_tensor(out=wt[0:n, c, :], in0=e[0:n, c, :], scalar=inv[0:n, c:c + 1],
                                                 in1=mix[0:n, c, :], op0=ALU.mult,
                                                 op1=ALU.mult).then_inc(sem["wt_ready"], 1)
                    dve.wait_ge(sem["proj_done"], b + 1)
                    for m in range(2):
                        cols_b = h[:, m, ds(b * N, N)]
                        dve.scalar_tensor_tensor(out=cols_b, in0=o_ps[:, m, :], scalar=cols[:, 2, m:m + 1],
                                                 in1=cols_b, op0=ALU.add, op1=ALU.add).then_inc(sem["h_ready"], 1)

                steps(dve, ITEMS, step)


def collaborative_attention(nc, dram, h, xn):
    H, HEAD = 12, 16
    SCALE = HEAD ** -0.5
    R = (HALF + H, HALF)
    HG = 6
    ROUNDS = [(c, g) for c in range(2) for g in range(2)]
    LAST = ITEMS - 1
    with Stage(nc, "collab") as st:
        w_q = st.sb("w_q", [HALF, 2, D])
        w_k = st.sb("w_k", [HALF, 2, D + H])
        w_v = st.sb("w_v", [HALF, 2, D])
        w_proj = st.sb("w_proj", [HALF, 2, D])
        mixing = st.sb("mixing", [R[0], 2, H])
        cols = st.sb("cols", [HALF, 1, 2])
        v_bias = st.sb("v_bias", [65, D])
        ident = st.sb("ident", [65, 65])
        q_all = st.sb("q_all", [HALF, 2, T])
        k_all = st.sb("k_all", [R[0], 2, T])
        x = st.sb("x", [HALF, 2, N])
        q = st.sb("q", [R[0], 2, 2, N])
        keys = st.sb("keys", [R[0], 2, 2, H, N])
        v1 = st.sb("v1", [65, 2, 2, H, HEAD + 1])
        top = st.sb("top", [65, 2, HG])
        e = st.sb("e", [65, 2, HG, N])
        et = st.sb("et", [65, 2, HG, 65])
        inv = st.sb("inv", [65, 2, H])
        att = st.sb("att", [65, 2, H, HEAD])
        heads = st.sb("heads", [HALF, 2, N])
        loaded = st.sem("loaded")
        with Stage(nc, "collabproj") as pst:
            q_ps = pst.ps("q_ps", [HALF, 2, 512])
            k_ps = pst.ps("k_ps", [R[0], 2, 512])
            projected = pst.sem("projected")
            q_copied = pst.sem("q_copied")
            k_copied = pst.sem("k_copied")
            with pst.block() as block:
                @block.sync
                def _(sp):
                    for dst, src in ((w_q, "collab_q"), (w_k, "collab_k"), (w_v, "collab_v"),
                                     (w_proj, "collab_proj"), (mixing, "collab_mixing"), (cols, "collab_cols")):
                        sp.dma_start(dst[:], dram[src]).then_inc(loaded, 16)
                    sp.dma_start(v_bias[:], dram["collab_v_bias"].broadcast_to([65, D])).then_inc(loaded, 16)
                    sp.dma_start(ident[:], dram["ident"][0:65, 0:65]).then_inc(loaded, 16)

                @block.tensor
                def _(pe):
                    pe.wait_ge(loaded, 128)

                    def step(t, first):
                        if not first:
                            pe.wait_ge(q_copied, t)
                        for m in range(2):
                            for j in range(2):
                                pe.matmul(q_ps[:, m, 0:TILE], w_q[:, j, m * HALF:(m + 1) * HALF],
                                          xn[:, j, ds(t * TILE, TILE)], start=(j == 0), stop=(j == 1))
                        if not first:
                            pe.wait_ge(k_copied, 2 * t)
                        for m in range(2):
                            w = [w_k[:, j, 0:R[0]] if m == 0 else w_k[:, j, R[0]:] for j in range(2)]
                            for j in range(2):
                                mm = pe.matmul(k_ps[0:R[m], m, 0:TILE], w[j], xn[:, j, ds(t * TILE, TILE)],
                                               start=(j == 0), stop=(j == 1))
                        mm.then_inc(projected, 1)

                    steps(pe, TILES, step)

                @block.scalar
                def _(act):
                    def step(t, first):
                        act.wait_ge(projected, t + 1)
                        act.activation(q_all[:, :, ds(t * TILE, TILE)], q_ps[:, :, 0:TILE],
                                       ACT.Copy).then_inc(q_copied, 1)

                    steps(act, TILES, step)

                @block.vector
                def _(dve):
                    def step(t, first):
                        dve.wait_ge(projected, t + 1)
                        for m in range(2):
                            dve.tensor_copy(k_all[0:R[m], m, ds(t * TILE, TILE)],
                                            k_ps[0:R[m], m, 0:TILE]).then_inc(k_copied, 1)

                    steps(dve, TILES, step)

        s_ps = [st.ps(f"s_ps{i}", [65, 2, 512]) for i in range(2)]
        et_ps = st.ps("et_ps", [65, 2, 512])
        av_bank = st.ps("av_bank", [65, 512])
        bank_b = st.ps("bank_b", [128, 512])
        av_ps = av_bank[:, 0:2 * H * (HEAD + 1)].rearrange("p (c h d) -> p c h d", c=2, h=H)
        heads_ps = bank_b[0:HALF, 0:2 * N].rearrange("p (a b) -> p a b", a=2)
        o_ps = heads_ps
        v_ps = bank_b[0:65, 0:2 * D].rearrange("p (c f) -> p c f", c=2)
        names = ("ones_ready q_ready x_ready keys_ready v_done v_ready s_done top_ready shifted e_ready "
                 "et_done et_ready av_done inv_ready att_ready heads_done heads_ready proj_done h_ready").split()
        sem = {n: st.sem(n) for n in names}

        def run(engine, body):
            body(0, 0, True, False)
            with engine.Fori(0, (ITEMS - 2) // 2) as i:
                body(2 * i + 1, 1, False, False)
                body(2 * i + 2, 0, False, False)
            body(LAST, LAST % 2, False, True)

        with st.block() as block:
            @block.gpsimd
            def _(pool):
                pool.memset(v1[:, :, :, :, HEAD:], 1.0).then_inc(sem["ones_ready"], 1)
                pool.memset(q[HALF:R[0], :, 0, :], 1.0).then_inc(sem["ones_ready"], 1)
                pool.tensor_copy(q[0:HALF, 0], q_all[:, :, 0:N]).then_inc(sem["q_ready"], 1)
                pool.tensor_copy(x[:], xn[:, :, 0:N]).then_inc(sem["x_ready"], 1)

                def body(b, p, first, last):
                    if last:
                        return
                    if not first:
                        pool.wait_ge(sem["s_done"], 4 * b)
                    pool.wait_ge(sem["v_done"], b + 1)
                    pool.tensor_copy(q[0:HALF, 1 - p], q_all[:, :, ds((b + 1) * N, N)]).then_inc(sem["q_ready"], 1)
                    pool.tensor_copy(x[:], xn[:, :, ds((b + 1) * N, N)]).then_inc(sem["x_ready"], 1)

                run(pool, body)

            @block.tensor
            def _(pe):
                def scores(r, i, p):
                    c, g = ROUNDS[i]
                    c0, n = QCUT[c]
                    for u in range(2):
                        for j in range(2):
                            f = g * HG + 3 * u
                            mm = pe.matmul(s_ps[i % 2][0:n, u, 0:3 * N], q[0:R[j], p, j, c0:c0 + n],
                                           keys[0:R[j], p, j, f:f + 3, :].rearrange("p h n -> p (h n)"),
                                           start=(j == 0), stop=(j == 1))
                    mm.then_inc(sem["s_done"], 1)

                def values(b):
                    pe.wait_ge(sem["x_ready"], b + 1)
                    for c, (c0, n) in enumerate(CUT):
                        for j in range(2):
                            mm = pe.matmul(v_ps[0:n, c, :], x[:, j, c0:c0 + n], w_v[:, j, :],
                                           start=(j == 0), stop=(j == 1))
                    mm.then_inc(sem["v_done"], 1)

                def turn_heads(b):
                    pe.wait_ge(loaded, 128)
                    pe.wait_ge(sem["att_ready"], b + 1)
                    for c, (c0, n) in enumerate(QCUT):
                        flat = att[0:n, c].rearrange("p h d -> p (h d)")
                        for m in range(2):
                            mm = pe.transpose(heads_ps[:, m, c0:c0 + n], flat[:, m * HALF:(m + 1) * HALF],
                                              ident[0:n, 0:n])
                    mm.then_inc(sem["heads_done"], 1)

                def project(b):
                    pe.wait_ge(sem["heads_ready"], b + 1)
                    for m in range(2):
                        for j in range(2):
                            mm = pe.matmul(o_ps[:, m, :], w_proj[:, j, m * HALF:(m + 1) * HALF], heads[:, j, :],
                                           start=(j == 0), stop=(j == 1))
                    mm.then_inc(sem["proj_done"], 1)

                pe.wait_ge(sem["ones_ready"], 2)
                values(0)
                pe.wait_ge(sem["q_ready"], 1)
                pe.wait_ge(sem["keys_ready"], 2)
                scores(0, 0, 0)
                scores(1, 1, 0)

                def body(b, p, first, last):
                    for i, (c, g) in enumerate(ROUNDS):
                        r = 4 * b + i
                        n = QCUT[c][1]
                        pe.wait_ge(sem["e_ready"], r + 1)
                        for f in range(HG):
                            for d, (d0, l) in enumerate(CUT):
                                mm = pe.transpose(et_ps[0:l, d, f * 65:f * 65 + n], e[0:n, i % 2, f, d0:d0 + l],
                                                  ident[0:n, 0:n])
                        mm.then_inc(sem["et_done"], 1)
                        if i + 2 < 4:
                            scores(r + 2, i + 2, p)
                        elif not last:
                            if i == 2:
                                pe.wait_ge(sem["q_ready"], b + 2)
                                pe.wait_ge(sem["keys_ready"], 2 * b + 4)
                            scores(r + 2, i - 2, 1 - p)
                        if i == 0:
                            pe.wait_ge(sem["v_ready"], 2 * b + 2)
                            if not first:
                                pe.wait_ge(sem["att_ready"], b)
                        pe.wait_ge(sem["et_ready"], 2 * r + 2)
                        for f in range(HG):
                            for d, (d0, l) in enumerate(CUT):
                                mm = pe.matmul(av_ps[0:n, c, g * HG + f, :], et[0:l, d, f, 0:n],
                                               v1[0:l, p, d, g * HG + f, :], start=(d == 0), stop=(d == 1))
                        mm.then_inc(sem["av_done"], 1)
                        if i == 0 and not first:
                            turn_heads(b - 1)
                        if i == 1 and not first:
                            project(b - 1)
                        if i == 2 and not last:
                            if not first:
                                pe.wait_ge(sem["h_ready"], 2 * b)
                            values(b + 1)

                run(pe, body)
                turn_heads(LAST)
                project(LAST)

            @block.scalar
            def _(act):
                def copy_heads(b):
                    act.wait_ge(sem["heads_done"], b + 1)
                    act.activation(heads[:], heads_ps, ACT.Copy).then_inc(sem["heads_ready"], 1)

                def body(b, p, first, last):
                    for i, (c, g) in enumerate(ROUNDS):
                        r = 4 * b + i
                        n = QCUT[c][1]
                        act.wait_ge(sem["shifted"], r + 1)
                        act.activation(e[0:n, i % 2], e[0:n, i % 2], ACT.Exp, scale=SCALE).then_inc(sem["e_ready"], 1)
                        if i == 1 and not first:
                            copy_heads(b - 1)
                        act.wait_ge(sem["et_done"], r + 1)
                        if not first or i:
                            act.wait_ge(sem["av_done"], r)
                        for d, (d0, l) in enumerate(CUT):
                            act.activation(et[0:l, d, :, 0:n],
                                           et_ps[0:l, d, 0:HG * 65].rearrange("p (f n) -> p f n", f=HG)[:, :, 0:n],
                                           ACT.Copy).then_inc(sem["et_ready"], 1)

                run(act, body)
                copy_heads(LAST)

            @block.vector
            def _(dve):
                def make_keys(b, p):
                    for j in range(2):
                        dve.tensor_tensor(keys[0:R[j], p, j],
                                          k_all[0:R[j], j, ds(b * N, N)].unsqueeze(1).broadcast_to([R[j], H, N]),
                                          mixing[0:R[j], j, :].unsqueeze(2).broadcast_to([R[j], H, N]),
                                          ALU.mult).then_inc(sem["keys_ready"], 1)

                def copy_values(b, p):
                    dve.wait_ge(sem["v_done"], b + 1)
                    for c, (c0, n) in enumerate(CUT):
                        dve.tensor_tensor(v1[0:n, p, c, :, 0:HEAD], v_ps[0:n, c, :].rearrange("p (h d) -> p h d", h=H),
                                          v_bias[0:n, :].rearrange("p (h d) -> p h d", h=H),
                                          ALU.add).then_inc(sem["v_ready"], 1)

                def normalise(b):
                    dve.wait_ge(sem["av_done"], 4 * b + 4)
                    dve.reciprocal(inv[:], av_ps[:, :, :, HEAD]).then_inc(sem["inv_ready"], 1)
                    dve.wait_ge(sem["inv_ready"], b + 1)
                    dve.tensor_tensor(att[:], av_ps[:, :, :, 0:HEAD],
                                      inv[:].unsqueeze(3).broadcast_to([65, 2, H, HEAD]),
                                      ALU.mult).then_inc(sem["att_ready"], 1)

                def add_output(b):
                    dve.wait_ge(sem["proj_done"], b + 1)
                    for m in range(2):
                        cols_b = h[:, m, ds(b * N, N)]
                        dve.scalar_tensor_tensor(out=cols_b, in0=o_ps[:, m, :], scalar=cols[:, 0, m:m + 1],
                                                 in1=cols_b, op0=ALU.add, op1=ALU.add).then_inc(sem["h_ready"], 1)

                dve.wait_ge(sem["ones_ready"], 2)
                make_keys(0, 0)
                copy_values(0, 0)

                def body(b, p, first, last):
                    for i, (c, g) in enumerate(ROUNDS):
                        r = 4 * b + i
                        n = QCUT[c][1]
                        dve.wait_ge(sem["s_done"], r + 1)
                        s = s_ps[i % 2][0:n, :, 0:3 * N].rearrange("p i (h m) -> p i h m", h=3)
                        t = top[0:n, i % 2].rearrange("p (i h) -> p i h", i=2)
                        dve.tensor_reduce(t, s, AX.X, ALU.max).then_inc(sem["top_ready"], 1)
                        dve.wait_ge(sem["top_ready"], r + 1)
                        if not first or i >= 2:
                            dve.wait_ge(sem["et_done"], r - 1)
                        dve.tensor_tensor(e[0:n, i % 2].rearrange("p (i h) m -> p i h m", i=2), s,
                                          t.unsqueeze(3).broadcast_to([n, 2, 3, N]),
                                          ALU.subtract).then_inc(sem["shifted"], 1)
                        if i == 0:
                            if not first:
                                normalise(b - 1)
                            if not last:
                                if not first:
                                    dve.wait_ge(sem["s_done"], 4 * b)
                                make_keys(b + 1, 1 - p)
                        if i == 2 and not first:
                            add_output(b - 1)
                        if i == 3 and not last:
                            copy_values(b + 1, 1 - p)

                run(dve, body)
                normalise(LAST)
                add_output(LAST)


def store_output(nc, h, out):
    with Stage(nc, "store") as st:
        stored = st.sem("stored")
        with st.block() as block:
            @block.sync
            def _(sp):
                for j in range(2):
                    sp.dma_start(out[:, j, :], h[:, j, :]).then_inc(stored, 16)
                sp.wait_ge(stored, 32)


STAGES = [embed_tokens, linear_attention, grouped_experts, bidirectional_mamba, quantised_mlp, group_attention, shared_experts,
          collaborative_attention, gelu_experts]


def build(nc, dram, out):
    Stage.used = []
    with nc.sbuf_tensor("h", [HALF, 2, T], F32) as h, nc.sbuf_tensor("xn", [HALF, 2, T], F32) as xn:
        for i, stage in enumerate(STAGES):
            if stage is not embed_tokens:
                layer_norm(nc, h, xn, f"norm{i}")
            stage(nc, dram, h, xn)
        store_output(nc, h, out)


def lay_out(i):
    import numpy as np
    a = {k: np.asarray(v) for k, v in i.items()}

    def halves(w):
        return np.ascontiguousarray(w.reshape((2, HALF) + w.shape[1:]).swapaxes(0, 1))

    def columns(*vs):
        return np.stack([halves(v.reshape(D)) for v in vs], axis=1)

    d = {}
    d["x"] = halves(a["x"][..., 0].transpose(2, 0, 1))
    d["embed_taps"] = halves(a["L0_tok_dw_w"].reshape(D, 7))
    d["embed_point_w"] = halves(a["L0_tok_pw_w"].T)
    d["embed_cols"] = columns(a["L0_tok_pw_b"], a["L0_tok_ln_g"], a["L0_tok_ln_b"], a["cls_tok"])
    d["linattn_qkv"] = halves(a["L0_attn_qkv_w"].T)
    d["linattn_proj"] = halves(a["L0_attn_proj_w"].T)
    d["linattn_cols"] = columns(a["L0_attn_proj_b"])
    head = np.arange(HALF) // 16
    mask = (head[:, None] == head[None, :]).astype(np.float32)
    d["head_mask"] = np.stack([mask, mask], axis=1)
    d["ident"] = np.eye(128, dtype=np.float32)
    for n in (8, 16):
        d[f"lower{n}"] = np.broadcast_to(np.tril(np.ones((n, n), np.float32), -1), (RT, n, n))
    sel = np.zeros((SPLIT, 16, 128), np.float32)
    for e in range(16):
        sel[e::32, e] = 1.0
    d["sel"] = sel.astype(mybir.dt.np(BF16))

    def per_expert(w):
        return halves(w.transpose(1, 0, 2).reshape(D, -1))

    d["grouped_router_w"] = halves(a["L0_ffn_gate_w"])
    d["grouped_router_b"] = np.stack([a["L0_ffn_gate_b"], a["L0_ffn_bias"]])
    for mine, theirs in (("up", "Wu"), ("gate", "Wg")):
        d["grouped_" + mine] = halves(np.concatenate([a["L0_ffn_" + theirs], a["L0_ffn_s" + theirs][None]])
                                      .transpose(1, 0, 2))
    d["grouped_down"] = np.concatenate([a["L0_ffn_Wd"], a["L0_ffn_sWd"][None]]).transpose(1, 0, 2)
    d["grouped_bias"] = np.stack([np.concatenate([a["L0_ffn_" + b], a["L0_ffn_s" + b][None]]).T
                                  for b in ("bu", "bg")], axis=1)
    bd = np.zeros((3, 32, D), np.float32)
    bd[:, 0:16] = a["L0_ffn_bd"]
    d["grouped_bd"] = bd.reshape(SPLIT, D)
    d["grouped_cols"] = columns(a["L0_ffn_sbd"])
    d["shared_router_w"] = halves(np.concatenate([a["L2_ffn_router_w"], a["L2_ffn_sg_w"]], axis=1))
    zeros8 = np.zeros(8, np.float32)
    d["shared_router_b"] = np.stack([np.concatenate([zeros8, a["L2_ffn_sg_b"]]), np.zeros(9, np.float32)])
    for mine, theirs in (("up", "gate"), ("gate", "up")):
        d["shared_" + mine] = np.concatenate([per_expert(a["L2_ffn_w_" + theirs]),
                                              halves(a["L2_ffn_ws_" + theirs])], axis=2)
    d["shared_down_r"] = a["L2_ffn_w_down"].reshape(16, HALF, D).transpose(1, 0, 2)
    d["shared_down_s"] = a["L2_ffn_ws_down"].reshape(6, 128, D).transpose(1, 0, 2)
    d["geluexp_router_w"] = halves(a["L3_ffn_router_w"].T)
    d["geluexp_router_b"] = np.zeros((2, 8), np.float32)
    d["geluexp_up"] = per_expert(a["L3_ffn_w1"])
    d["geluexp_down"] = a["L3_ffn_w2"].reshape(48, 128, D).transpose(1, 0, 2)
    def chunks(w):
        return np.ascontiguousarray(w.reshape((IC, 128) + w.shape[1:]).swapaxes(0, 1))

    for which in ("f", "b"):
        m = {k: a[f"L1_attn_{which}_{k}"] for k in ("in_w", "conv_w", "conv_b", "xproj_w", "dt_w", "dt_b",
                                                    "A_log", "D_skip", "out_w")}
        p = f"mamba_{which}_"
        d[p + "in"] = halves(m["in_w"].T)
        xw = np.zeros((INNER, 128), np.float32)
        xw[:, 0:RANK] = m["xproj_w"][0:RANK].T
        for r in (32, 64, 96):
            xw[:, r:r + 2 * STATES] = m["xproj_w"][RANK:].T
        d[p + "x"] = chunks(xw)
        d[p + "dt"] = m["dt_w"].T
        d[p + "out"] = chunks(m["out_w"].T)
        d[p + "cols"] = chunks(np.concatenate([m["conv_w"], m["conv_b"][:, None], m["dt_b"][:, None],
                                               m["D_skip"][:, None]], axis=1))
        d[p + "A_log"] = chunks(m["A_log"])
    d["mamba_norm_cols"] = columns(a["L1_attn_ln_g"], a["L1_attn_ln_b"])
    state_sel = np.zeros((128, 2 * STATES, 128), np.float32)
    for e in range(2 * STATES):
        state_sel[32 + e::32, e] = 1.0
    d["state_sel"] = state_sel.astype(mybir.dt.np(BF16))
    d["quant_w1"] = halves(a["L1_ffn_w1"].T)
    d["quant_w2"] = a["L1_ffn_w2"].T.reshape(6, 128, D).transpose(1, 0, 2)
    d["quant_step_w1"] = a["L1_ffn_alpha_w1"][None]
    d["quant_step_w2"] = a["L1_ffn_alpha_w2"][None]
    d["quant_a1"] = a["L1_ffn_alpha_a1"].reshape(HALF, 2)
    d["quant_a2"] = a["L1_ffn_alpha_a2"].reshape(HALF, 8)
    d["quant_hid"] = np.stack([a["L1_ffn_alpha_w1"].reshape(6, 128).T, a["L1_ffn_b1"].reshape(6, 128).T], axis=1)
    d["quant_out"] = columns(a["L1_ffn_alpha_w2"], a["L1_ffn_b2"])
    d["groupattn_qkv"] = halves(a["L2_attn_W_qkv"])
    d["groupattn_proj"] = halves(a["L2_attn_W_proj"])
    d["groupattn_gp"] = halves(a["L2_attn_W_gp"])
    b_qkv = a["L2_attn_b_qkv"]
    d["groupattn_cols"] = columns(b_qkv[0:D], b_qkv[D:2 * D], a["L2_attn_b_proj"])
    d["groupattn_v_bias"] = b_qkv[None, 2 * D:]
    d["groupattn_alpha"] = a["L2_attn_alpha"][None]
    d["collab_q"] = halves(a["L3_attn_Wq"].T)
    wk = a["L3_attn_Wk"].T
    d["collab_k"] = halves(np.concatenate([wk[:, 0:HALF], a["L3_attn_Wcb"].T, wk[:, HALF:]], axis=1))
    d["collab_v"] = halves(a["L3_attn_Wv"].T)
    d["collab_proj"] = halves(a["L3_attn_Wproj"].T)
    mixing = np.zeros((HALF + 12, 2, 12), np.float32)
    mixing[HALF:, 0] = np.eye(12, dtype=np.float32)
    mixing[0:HALF] = halves(a["L3_attn_Wmix"].T)
    d["collab_mixing"] = mixing
    d["collab_cols"] = columns(a["L3_attn_bproj"])
    d["collab_v_bias"] = a["L3_attn_bv"][None]
    return d


def kernel(**inputs):
    import numpy as np
    import concourse.bacc as bacc
    from concourse.bass_utils import run_bass_kernel_spmd

    nc = bacc.Bacc("TRN2", target_bir_lowering=False, num_devices=1)
    arrays = {f"in_{k}": np.ascontiguousarray(v) for k, v in lay_out(inputs).items()}
    dram = {k[3:]: nc.dram_tensor(k, v.shape, mybir.dt.from_np(v.dtype), kind="ExternalInput").ap()
            for k, v in arrays.items()}
    out = nc.dram_tensor("out_h", (HALF, 2, T), F32, kind="ExternalOutput").ap()
    build(nc, dram, out)
    r = run_bass_kernel_spmd(nc, [arrays], core_ids=[0])
    got = r.results[0]["out_h"]
    return np.ascontiguousarray(got.reshape(HALF, 2, ITEMS, N).transpose(2, 3, 1, 0).reshape(ITEMS, N, D))
```

```python
from contextlib import ExitStack, contextmanager

import concourse.bass as bass
from concourse import mybir

ALU = mybir.AluOpType
ACT = mybir.ActivationFunctionType
AX = mybir.AxisListType
F32 = mybir.dt.float32
BF16 = mybir.dt.bfloat16
ds = bass.ds

ITEMS = 16
PATCHES = 128
N = PATCHES + 1
D = 192
HALF = D // 2
T = ITEMS * N
TILE = 344
TILES = T // TILE
assert TILES * TILE == T
RT = 86


class Stage:
    used = []

    def __init__(self, nc, name):
        self.nc, self.name, self.ctx, self.sems = nc, name, ExitStack(), []

    def __enter__(self):
        self.ctx.__enter__()
        return self

    def sb(self, name, shape, dt=F32):
        return self.ctx.enter_context(self.nc.sbuf_tensor(f"{self.name}_{name}", shape, dt))

    def ps(self, name, shape, dt=F32):
        return self.ctx.enter_context(self.nc.psum_tensor(f"{self.name}_{name}", shape, dt))

    def sem(self, name):
        s = self.nc.alloc_semaphore(f"{self.name}_{name}")
        self.sems.append(s)
        return s

    @contextmanager
    def block(self):
        zeroed = list(Stage.used)
        with self.nc.Block(no_gpsimd_drain=True) as block:
            if zeroed:
                @block.gpsimd
                def _(pool):
                    for s in zeroed:
                        pool.sem_clear(s)
            yield block
        for s in zeroed:
            Stage.used.remove(s)
            self.nc.release_semaphore(s)

    def __exit__(self, *exc):
        Stage.used.extend(self.sems)
        return self.ctx.__exit__(*exc)


def layer_norm(nc, dram, h, xn, name, prefetch=None, epsilon=1e-5):
    PER = TILE // RT
    with Stage(nc, name) as st:
        averager = st.sb("averager", [HALF, HALF])
        ident = st.sb("ident", [RT, RT])
        eps = st.sb("eps", [RT, 1])
        added = st.sb("added", [HALF, T])
        centred = st.sb("centred", [HALF, 4, 2, TILE])
        squared = st.sb("squared", [HALF, 2, 2, TILE])
        squares = st.sb("squares", [HALF, 2, TILE])
        std = st.sb("std", [RT, TILES, PER])
        rstd = st.sb("rstd", [RT, TILES, PER])
        mean_ps = st.ps("mean", [HALF, 2, 512])
        var_ps = st.ps("var", [RT, 2, 512])
        wide_ps = st.ps("wide", [HALF, 2, 512])
        loaded = st.sem("loaded")
        consts = st.sem("consts")
        added_ready = st.sem("added_ready")
        squares_ready = st.sem("squares_ready")
        mean_ready = st.sem("mean_ready")
        centred_ready = st.sem("centred_ready")
        squared_ready = st.sem("squared_ready")
        var_ready = st.sem("var_ready")
        std_ready = st.sem("std_ready")
        rstd_ready = st.sem("rstd_ready")
        wide_ready = st.sem("wide_ready")
        xn_ready = st.sem("xn_ready")

        def cols(t):
            return slice(t * TILE, (t + 1) * TILE)

        with st.block() as block:
            @block.sync
            def _(sp):
                sp.dma_start(ident[:], dram["ident"][0:RT, 0:RT]).then_inc(loaded, 16)
                if prefetch:
                    prefetch(sp)

            @block.gpsimd
            def _(pool):
                pool.memset(averager[:], 1.0 / D).then_inc(consts, 1)
                pool.memset(eps[:], epsilon).then_inc(consts, 1)

                def add(t):
                    pool.tensor_tensor(added[:, cols(t)], h[:, 0, cols(t)], h[:, 1, cols(t)],
                                       ALU.add).then_inc(added_ready, 1)

                for t in range(3):
                    add(t)
                for t in range(TILES):
                    pool.wait_ge(squared_ready, t + 1)
                    if t >= 2:
                        pool.wait_ge(var_ready, t - 1)
                    pool.tensor_tensor(squares[:, t % 2, :], squared[:, t % 2, 0, :], squared[:, t % 2, 1, :],
                                       ALU.add).then_inc(squares_ready, 1)
                    if t + 3 < TILES:
                        add(t + 3)

            @block.tensor
            def _(pe):
                def mean(t):
                    if t >= 2:
                        pe.wait_ge(centred_ready, t - 1)
                    pe.wait_ge(added_ready, t + 1)
                    pe.matmul(mean_ps[:, t % 2, 0:TILE], averager[:], added[:, cols(t)],
                              start=True, stop=True).then_inc(mean_ready, 1)

                def variance(t):
                    pe.wait_ge(squares_ready, t + 1)
                    if t >= 2:
                        pe.wait_ge(std_ready, t - 1)
                    for c in range(PER):
                        mm = pe.matmul(var_ps[:, t % 2, c:c + 1], squares[:, t % 2, c * RT:(c + 1) * RT],
                                       averager[:, 0:1], start=True, stop=True)
                    mm.then_inc(var_ready, 1)

                def spread(t):
                    pe.wait_ge(rstd_ready, t + 1)
                    if t >= 2:
                        pe.wait_ge(xn_ready, t - 1)
                    for c in range(PER):
                        mm = pe.matmul(wide_ps[:, t % 2, c * RT:(c + 1) * RT],
                                       rstd[:, t, c:c + 1].broadcast_to([RT, HALF]), ident[:], start=True, stop=True)
                    mm.then_inc(wide_ready, 1)

                pe.wait_ge(consts, 2)
                mean(0)
                mean(1)
                pe.wait_ge(loaded, 16)
                for t in range(TILES):
                    if t + 2 < TILES:
                        mean(t + 2)
                    variance(t)
                    if t:
                        spread(t - 1)
                spread(TILES - 1)

            @block.scalar
            def _(act):
                def square(t):
                    act.wait_ge(centred_ready, t + 1)
                    if t >= 2:
                        act.wait_ge(squares_ready, t - 1)
                    act.activation(squared[:, t % 2], centred[:, t % 4], ACT.Square).then_inc(squared_ready, 1)

                act.wait_ge(consts, 2)
                square(0)
                for t in range(TILES):
                    if t + 1 < TILES:
                        square(t + 1)
                    act.wait_ge(var_ready, t + 1)
                    act.activation(std[:, t], var_ps[:, t % 2, 0:PER], ACT.Sqrt, bias=eps[:]).then_inc(std_ready, 1)

            @block.vector
            def _(dve):
                def centre(t):
                    dve.wait_ge(mean_ready, t + 1)
                    if t >= 4:
                        dve.wait_ge(squared_ready, t - 3)
                        dve.wait_ge(xn_ready, t - 3)
                    dve.tensor_tensor(centred[:, t % 4], h[:, :, cols(t)],
                                      mean_ps[:, t % 2, 0:TILE].unsqueeze(1).broadcast_to([HALF, 2, TILE]),
                                      ALU.subtract).then_inc(centred_ready, 1)

                def scale(t):
                    dve.wait_ge(wide_ready, t + 1)
                    dve.tensor_tensor(xn[:, :, cols(t)], centred[:, t % 4],
                                      wide_ps[:, t % 2, 0:TILE].unsqueeze(1).broadcast_to([HALF, 2, TILE]),
                                      ALU.mult).then_inc(xn_ready, 1)

                centre(0)
                centre(1)
                for t in range(TILES):
                    if t + 2 < TILES:
                        centre(t + 2)
                    dve.wait_ge(std_ready, t + 1)
                    dve.reciprocal(rstd[:, t], std[:, t]).then_inc(rstd_ready, 1)
                    if t:
                        scale(t - 1)
                scale(TILES - 1)


CUT = ((0, 65), (65, 64))
QCUT = ((0, 65), (64, 65))
KEYS = (64, 65)
PAIR = 2
PAIRS = ITEMS // PAIR


def steps(engine, count, body):
    body(0, True)
    with engine.Fori(1, count) as s:
        body(s, False)


def embed_tokens(nc, dram, h, xn):
    TAPS = 7
    PAD = TAPS // 2
    G = 2
    COLS = G * PATCHES
    STEPS = ITEMS // G
    with Stage(nc, "embed") as st:
        x = st.sb("x", [HALF, 2, ITEMS, PATCHES + 2 * PAD])
        taps = st.sb("taps", [HALF, 2, TAPS])
        diag = st.sb("diag", [HALF, 2, TAPS, HALF])
        ones = st.sb("ones", [HALF, HALF])
        averager = st.sb("averager", [HALF, HALF])
        point_w = st.sb("point_w", [HALF, 2, D])
        cols = st.sb("cols", [HALF, 4, 2])
        eps = st.sb("eps", [HALF, 1])
        conv = st.sb("conv", [HALF, 2, COLS])
        y = st.sb("y", [HALF, 2, COLS])
        centred = st.sb("centred", [HALF, 2, COLS])
        squared = st.sb("squared", [HALF, 2, COLS])
        std = st.sb("std", [HALF, COLS])
        rstd = st.sb("rstd", [HALF, COLS])
        normed = st.sb("normed", [HALF, 2, COLS])
        conv_ps = st.ps("conv_ps", [HALF, 2, COLS])
        y_ps = st.ps("y_ps", [HALF, 2, COLS])
        mean_ps = st.ps("mean_ps", [HALF, COLS])
        var_ps = st.ps("var_ps", [HALF, COLS])
        x_loaded = st.sem("x_loaded")
        weights_loaded = st.sem("weights_loaded")
        padded = st.sem("padded")
        consts = st.sem("consts")
        rows_ready = st.sem("rows_ready")
        diag_ready = st.sem("diag_ready")
        conv_done = st.sem("conv_done")
        conv_ready = st.sem("conv_ready")
        y_done = st.sem("y_done")
        y_ready = st.sem("y_ready")
        mean_ready = st.sem("mean_ready")
        centred_ready = st.sem("centred_ready")
        squared_ready = st.sem("squared_ready")
        var_ready = st.sem("var_ready")
        std_ready = st.sem("std_ready")
        rstd_ready = st.sem("rstd_ready")
        normed_ready = st.sem("normed_ready")
        h_ready = st.sem("h_ready")
        h_items = h[:].rearrange("p j (b n) -> p j b n", n=N)

        def run(engine, body):
            body(0, True, False)
            with engine.Fori(1, STEPS - 1) as s:
                body(s, False, False)
            body(STEPS - 1, False, True)

        with st.block() as block:
            @block.sync
            def _(sp):
                for j in range(2):
                    sp.dma_start(x[:, j, :, PAD:PAD + PATCHES], dram["x"][:, j]).then_inc(x_loaded, 16)
                sp.dma_start(taps[:], dram["embed_taps"]).then_inc(weights_loaded, 16)
                sp.dma_start(point_w[:], dram["embed_point_w"]).then_inc(weights_loaded, 16)
                sp.dma_start(cols[:], dram["embed_cols"]).then_inc(weights_loaded, 16)

            @block.gpsimd
            def _(pool):
                pool.memset(x[:, :, :, 0:PAD], 0.0).then_inc(padded, 1)
                pool.memset(x[:, :, :, PAD + PATCHES:], 0.0).then_inc(padded, 1)
                pool.memset(ones[:], 1.0).then_inc(consts, 1)
                pool.memset(averager[:], 1.0 / D).then_inc(consts, 1)
                pool.memset(eps[:], 1e-6).then_inc(consts, 1)
                for j in range(2):
                    pool.wait_ge(rows_ready, (j + 1) * TAPS)
                    pool.affine_select(out=diag[:, j], in_=diag[:, j], compare_op=ALU.is_equal, fill=0.0,
                                       base=0, pattern=[[0, TAPS], [-1, HALF]],
                                       channel_multiplier=1).then_inc(diag_ready, 1)

            @block.tensor
            def _(pe):
                pe.wait_ge(diag_ready, 2)
                pe.wait_ge(padded, 2)
                pe.wait_ge(x_loaded, 32)
                pe.wait_ge(weights_loaded, 48)

                def convolve(s):
                    for j in range(2):
                        for k in range(TAPS):
                            mm = pe.matmul(conv_ps[:, j, :].rearrange("p (b n) -> p b n", b=G), diag[:, j, k, :],
                                           x[:, j, ds(s * G, G), k:k + PATCHES],
                                           start=(k == 0), stop=(k == TAPS - 1))
                    mm.then_inc(conv_done, 1)

                def project(s):
                    pe.wait_ge(conv_ready, s + 1)
                    for m in range(2):
                        for j in range(2):
                            mm = pe.matmul(y_ps[:, m, :], point_w[:, j, m * HALF:(m + 1) * HALF], conv[:, j, :],
                                           start=(j == 0), stop=(j == 1))
                    mm.then_inc(y_done, 1)

                convolve(0)
                project(0)

                def step(s, first, last):
                    pe.wait_ge(y_ready, 2 * s + 2)
                    for j in range(2):
                        mm = pe.matmul(mean_ps[:], averager[:], y[:, j, :], start=(j == 0), stop=(j == 1))
                    mm.then_inc(mean_ready, 1)
                    if not last:
                        convolve(s + 1)
                    pe.wait_ge(squared_ready, s + 1)
                    if not first:
                        pe.wait_ge(std_ready, s)
                    for j in range(2):
                        mm = pe.matmul(var_ps[:], averager[:], squared[:, j, :], start=(j == 0), stop=(j == 1))
                    mm.then_inc(var_ready, 1)
                    if not last:
                        project(s + 1)

                run(pe, step)

            @block.scalar
            def _(act):
                act.wait_ge(weights_loaded, 48)
                act.wait_ge(consts, 3)

                def copy_conv(s):
                    act.wait_ge(conv_done, s + 1)
                    act.activation(conv[:], conv_ps[:], ACT.Copy).then_inc(conv_ready, 1)

                def copy_y(s):
                    act.wait_ge(y_done, s + 1)
                    for m in range(2):
                        act.activation(y[:, m, :], y_ps[:, m, :], ACT.Identity,
                                       bias=cols[:, 0, m:m + 1]).then_inc(y_ready, 1)

                copy_conv(0)
                copy_y(0)

                def step(s, first, last):
                    act.wait_ge(centred_ready, s + 1)
                    act.activation(squared[:], centred[:], ACT.Square).then_inc(squared_ready, 1)
                    if not last:
                        copy_conv(s + 1)
                    act.wait_ge(var_ready, s + 1)
                    if not first:
                        act.wait_ge(rstd_ready, s)
                    act.activation(std[:], var_ps[:], ACT.Sqrt, bias=eps[:]).then_inc(std_ready, 1)
                    if not last:
                        copy_y(s + 1)
                    act.wait_ge(normed_ready, s + 1)
                    for m in range(2):
                        act.activation(h_items[:, m, ds(s * G, G), 1:N],
                                       normed[:, m, :].rearrange("p (b n) -> p b n", b=G), ACT.Relu,
                                       bias=cols[:, 2, m:m + 1], scale=cols[:, 1, m:m + 1]).then_inc(h_ready, 1)

                run(act, step)

            @block.vector
            def _(dve):
                dve.wait_ge(weights_loaded, 48)
                dve.wait_ge(consts, 3)
                for j in range(2):
                    for k in range(TAPS):
                        dve.tensor_scalar(diag[:, j, k, :], ones[:], taps[:, j, k:k + 1], None,
                                          ALU.mult).then_inc(rows_ready, 1)
                for m in range(2):
                    dve.tensor_copy(h_items[:, m, :, 0], cols[:, 3, m:m + 1].broadcast_to([HALF, ITEMS]))

                def step(s, first):
                    dve.wait_ge(mean_ready, s + 1)
                    if not first:
                        dve.wait_ge(normed_ready, s)
                    dve.tensor_tensor(centred[:], y[:], mean_ps[:].unsqueeze(1).broadcast_to([HALF, 2, COLS]),
                                      ALU.subtract).then_inc(centred_ready, 1)
                    dve.wait_ge(std_ready, s + 1)
                    dve.reciprocal(rstd[:], std[:]).then_inc(rstd_ready, 1)
                    dve.wait_ge(rstd_ready, s + 1)
                    if not first:
                        dve.wait_ge(h_ready, 2 * s)
                    dve.tensor_tensor(normed[:], centred[:], rstd[:].unsqueeze(1).broadcast_to([HALF, 2, COLS]),
                                      ALU.mult).then_inc(normed_ready, 1)

                steps(dve, STEPS, step)


def linear_attention(nc, dram, h, xn):
    HEAD = 16
    SCALE = HEAD ** -0.5
    PT = PAIR * N
    with Stage(nc, "linattn") as st:
        w_qkv = st.sb("w_qkv", [HALF, 2, 3 * D])
        w_proj = st.sb("w_proj", [HALF, 2, D])
        b_proj = st.sb("b_proj", [HALF, 1, 2])
        mask = st.sb("mask", [HALF, 2, HALF])
        x = st.sb("x", [HALF, 2, PT])
        q = st.sb("q", [HALF, 2, PT])
        k = st.sb("k", [65, PAIR, 2, D])
        v1 = st.sb("v1", [65, PAIR, 2, 2, 2, HALF])
        kv = st.sb("kv", [HALF, PAIR, 2, 2, HALF])
        den = st.sb("den", [HALF, 2, PT])
        rden = st.sb("rden", [HALF, 2, PT])
        heads = st.sb("heads", [HALF, 2, PT])
        loaded = st.sem("loaded")

        def loads(sp):
            sp.dma_start(w_qkv[:], dram["linattn_qkv"]).then_inc(loaded, 16)
            sp.dma_start(w_proj[:], dram["linattn_proj"]).then_inc(loaded, 16)
            sp.dma_start(b_proj[:], dram["linattn_cols"]).then_inc(loaded, 16)
            sp.dma_start(mask[:], dram["head_mask"]).then_inc(loaded, 16)

        layer_norm(nc, dram, h, xn, "linattn_norm", loads)
        q_banks = st.ps("q_banks", [HALF, 2, 512])
        k_v_banks = st.ps("k_v_banks", [65, 4, 512])
        kv_banks = st.ps("kv_banks", [HALF, 2, 512])
        q_ps = num_ps = o_ps = q_banks[:, :, 0:PT]
        den_ps = kv_banks[:, :, 0:PT]
        kv_ps = kv_banks[:, :, 0:4 * HALF]
        ones_ready = st.sem("ones_ready")
        x_ready = st.sem("x_ready")
        k_v_done = st.sem("k_v_done")
        q_done = st.sem("q_done")
        v_ready = st.sem("v_ready")
        k_ready = st.sem("k_ready")
        q_ready = st.sem("q_ready")
        kv_done = st.sem("kv_done")
        kv_ready = st.sem("kv_ready")
        den_done = st.sem("den_done")
        num_done = st.sem("num_done")
        den_ready = st.sem("den_ready")
        rden_ready = st.sem("rden_ready")
        heads_ready = st.sem("heads_ready")
        proj_done = st.sem("proj_done")
        h_ready = st.sem("h_ready")

        def run(engine, body):
            body(0, True, False)
            with engine.Fori(1, PAIRS - 1) as s:
                body(s, False, False)
            body(PAIRS - 1, False, True)

        with st.block() as block:
            @block.gpsimd
            def _(pool):
                pool.memset(v1[:, :, :, :, 1, :], 1.0).then_inc(ones_ready, 1)

                def step(s, first):
                    if not first:
                        pool.wait_ge(k_v_done, 2 * s)
                    pool.tensor_copy(x[:], xn[:, :, ds(s * PT, PT)]).then_inc(x_ready, 1)

                steps(pool, PAIRS, step)

            @block.tensor
            def _(pe):
                pe.wait_ge(loaded, 64)
                pe.wait_ge(ones_ready, 1)

                def project_k_v(s):
                    pe.wait_ge(x_ready, s + 1)
                    for i in range(PAIR):
                        for c, (c0, n) in enumerate(QCUT):
                            for j in range(2):
                                mm = pe.matmul(k_v_banks[0:n, 2 * i + c, 0:2 * D],
                                               x[:, j, i * N + c0:i * N + c0 + n], w_qkv[:, j, D:3 * D],
                                               start=(j == 0), stop=(j == 1))
                        mm.then_inc(k_v_done, 1)

                project_k_v(0)

                def step(s, first, last):
                    if not first:
                        pe.wait_ge(h_ready, 2 * s)
                    for m in range(2):
                        for j in range(2):
                            mm = pe.matmul(q_ps[:, m, :], w_qkv[:, j, m * HALF:(m + 1) * HALF],
                                           xn[:, j, ds(s * PT, PT)], start=(j == 0), stop=(j == 1))
                    mm.then_inc(q_done, 1)
                    for i in range(PAIR):
                        pe.wait_ge(v_ready, 2 * s + i + 1)
                        pe.wait_ge(k_ready, 2 * s + i + 1)
                        for j in range(2):
                            for c, n in enumerate(KEYS):
                                mm = pe.matmul(kv_ps[:, i, 2 * j * HALF:2 * (j + 1) * HALF],
                                               k[0:n, i, c, j * HALF:(j + 1) * HALF],
                                               v1[0:n, i, c, j], start=(c == 0), stop=(c == 1))
                        mm.then_inc(kv_done, 1)
                    pe.wait_ge(q_ready, s + 1)
                    pe.wait_ge(kv_ready, 2 * s + 2)
                    for ps, part, done in ((den_ps, 1, den_done), (num_ps, 0, num_done)):
                        for j in range(2):
                            for i in range(PAIR):
                                mm = pe.matmul(ps[:, j, i * N:(i + 1) * N], kv[:, i, j, part, :],
                                               q[:, j, i * N:(i + 1) * N], start=True, stop=True)
                            mm.then_inc(done, 1)
                    if not last:
                        project_k_v(s + 1)
                    pe.wait_ge(heads_ready, 2 * s + 2)
                    for m in range(2):
                        for j in range(2):
                            mm = pe.matmul(o_ps[:, m, :], w_proj[:, j, m * HALF:(m + 1) * HALF], heads[:, j, :],
                                           start=(j == 0), stop=(j == 1))
                        mm.then_inc(proj_done, 1)

                run(pe, step)

            @block.scalar
            def _(act):
                def step(s, first):
                    for i in range(PAIR):
                        act.wait_ge(k_v_done, 2 * s + i + 1)
                        if not first:
                            act.wait_ge(kv_done, 2 * s)
                        act.activation(v1[:, i, :, :, 0, :],
                                       k_v_banks[:, 2 * i:2 * i + 2, D:2 * D].rearrange("p c (j f) -> p c j f", j=2),
                                       ACT.Copy).then_inc(v_ready, 1)

                steps(act, PAIRS, step)

            @block.vector
            def _(dve):
                dve.wait_ge(loaded, 64)

                def read_k(s, first):
                    for i in range(PAIR):
                        dve.wait_ge(v_ready, 2 * s + i + 1)
                        if not first:
                            dve.wait_ge(kv_done, 2 * s)
                        dve.tensor_scalar(k[:, i], k_v_banks[:, 2 * i:2 * i + 2, 0:D], 0.0, SCALE, ALU.max,
                                          ALU.add).then_inc(k_ready, 1)

                read_k(0, True)

                def step(s, first, last):
                    dve.wait_ge(q_done, s + 1)
                    dve.tensor_scalar(q[:], q_ps, 0.0, SCALE, ALU.max, ALU.add).then_inc(q_ready, 1)
                    for i in range(PAIR):
                        dve.wait_ge(kv_done, 2 * s + i + 1)
                        dve.tensor_tensor(kv[:, i], kv_ps[:, i, :].rearrange("p (j r f) -> p j r f", j=2, r=2),
                                          mask[:].unsqueeze(1).broadcast_to([HALF, 2, 2, HALF]),
                                          ALU.mult).then_inc(kv_ready, 1)
                    for j in range(2):
                        dve.wait_ge(den_done, 2 * s + j + 1)
                        dve.tensor_scalar(den[:, j, :], den_ps[:, j, :], 1e-6, None, ALU.add).then_inc(den_ready, 1)
                    for j in range(2):
                        dve.wait_ge(den_ready, 2 * s + j + 1)
                        dve.reciprocal(rden[:, j, :], den[:, j, :]).then_inc(rden_ready, 1)
                    for j in range(2):
                        dve.wait_ge(rden_ready, 2 * s + j + 1)
                        dve.wait_ge(num_done, 2 * s + j + 1)
                        if not first:
                            dve.wait_ge(proj_done, 2 * s)
                        dve.tensor_tensor(heads[:, j, :], num_ps[:, j, :], rden[:, j, :],
                                          ALU.mult).then_inc(heads_ready, 1)
                    if not last:
                        read_k(s + 1, False)
                    for m in range(2):
                        dve.wait_ge(proj_done, 2 * s + m + 1)
                        tile = h[:, m, ds(s * PT, PT)]
                        dve.scalar_tensor_tensor(out=tile, in0=o_ps[:, m, :], scalar=b_proj[:, 0, m:m + 1], in1=tile,
                                                 op0=ALU.add, op1=ALU.add).then_inc(h_ready, 1)

                run(dve, step)


CHUNKS = T // RT
SPLIT = 96
assert CHUNKS * RT == T and TILE % RT == 0


def router(nc, dram, h, xn, gates, name, experts, choose, prefetch, extra=0):
    E = experts + extra
    with Stage(nc, name + "_router") as st:
        w = st.sb("w", [HALF, 2, E])
        ident = st.sb("ident", [RT, RT])
        b = {k: st.sb(k, [RT, E]) for k in ("logit_bias", "score_bias")}
        before = st.sb("before", [RT, CHUNKS, experts, experts], BF16)
        f = {k: st.sb(k, [RT, CHUNKS, E]) for k in ("logits", "exps", "probs", "scores", "rank", "mask", "weight")}
        g = {k: st.sb(k, [RT, CHUNKS, 8]) for k in ("group", "group_rank", "group_mask")}
        c = {k: st.sb(k, [RT, CHUNKS]) for k in ("top", "total", "recip", "u", "v")}
        wide = st.sb("wide", [RT, CHUNKS, SPLIT])
        full = st.sb("full", [SPLIT, T])
        rest = st.sb("rest", [SPLIT, T])
        part = st.sb("part", [SPLIT, T], BF16)
        loaded = st.sem("loaded")
        prefetched = st.sem("prefetched")

        def loads(sp):
            sp.dma_start(w[:], dram[name + "_router_w"]).then_inc(loaded, 16)
            sp.dma_start(b["logit_bias"][:], dram[name + "_router_b"][0:1].broadcast_to([RT, E])).then_inc(loaded, 16)
            sp.dma_start(b["score_bias"][:], dram[name + "_router_b"][1:2].broadcast_to([RT, E])).then_inc(loaded, 16)
            sp.dma_start(ident[:], dram["ident"][0:RT, 0:RT]).then_inc(loaded, 16)
            for dst, src in prefetch:
                sp.dma_start(dst, src).then_inc(prefetched, 16)

        layer_norm(nc, dram, h, xn, name + "_norm", loads)
        logits_ps = st.ps("logits_ps", [RT, CHUNKS, E])
        turned_ps = st.ps("turned_ps", [SPLIT, TILES, 512])
        logits_done = st.sem("logits_done")
        exp_in_ready = st.sem("exp_in_ready")
        exp_ready = st.sem("exp_ready")
        wide_ready = st.sem("wide_ready")
        turned_done = st.sem("turned_done")
        full_ready = st.sem("full_ready")
        chain = st.sem("chain")
        with st.block() as block:
            @block.sync
            def _(sp):
                sp.wait_ge(prefetched, 16 * len(prefetch))

            @block.tensor
            def _(pe):
                pe.wait_ge(loaded, 64)
                for t in range(CHUNKS):
                    for j in range(2):
                        mm = pe.matmul(logits_ps[:, t, :], xn[:, j, t * RT:(t + 1) * RT], w[:, j, :],
                                       start=(j == 0), stop=(j == 1))
                mm.then_inc(logits_done, 1)
                pe.wait_ge(wide_ready, 1)
                per = TILE // RT
                for t in range(CHUNKS):
                    mm = pe.transpose(turned_ps[:, t // per, (t % per) * RT:(t % per + 1) * RT],
                                      wide[:, t, :], ident[:])
                mm.then_inc(turned_done, 1)

            @block.scalar
            def _(act):
                act.wait_ge(exp_in_ready, 1)
                act.activation(f["exps"][:], f["logits"][:], ACT.Exp).then_inc(exp_ready, 1)
                act.wait_ge(turned_done, 1)
                act.activation(full[:].rearrange("p (t n) -> p t n", n=TILE), turned_ps[:, :, 0:TILE],
                               ACT.Copy).then_inc(full_ready, 1)

            @block.vector
            def _(dve):
                count = [0]

                def link(ins):
                    count[0] += 1
                    ins.then_inc(chain, 1)
                    dve.wait_ge(chain, count[0])

                def over(ap, n):
                    return ap.unsqueeze(1).broadcast_to([RT, CHUNKS, n])

                def last(ap, n):
                    return ap.unsqueeze(2).broadcast_to([RT, CHUNKS, n])

                def rank(out, score, n):
                    first = before[:].rearrange("p c a b -> p c (a b)")[:, :, 0:n * n].rearrange("p c (a b) -> p c a b", a=n)
                    for e in range(n):
                        this = score[:, :, e:e + 1]
                        if e:
                            count[0] += 1
                            dve.tensor_tensor(first[:, :, e, 0:e], score[:, :, 0:e], this.broadcast_to([RT, CHUNKS, e]),
                                              ALU.is_ge).then_inc(chain, 1)
                        count[0] += 1
                        dve.tensor_tensor(first[:, :, e, e:n], score[:, :, e:n], this.broadcast_to([RT, CHUNKS, n - e]),
                                          ALU.is_gt).then_inc(chain, 1)
                    dve.wait_ge(chain, count[0])
                    link(dve.tensor_reduce(out, first, AX.X, ALU.add))

                link(dve.memset(wide[:], 0.0))
                dve.wait_ge(loaded, 64)
                dve.wait_ge(logits_done, 1)
                L = f["logits"]
                n = experts
                link(dve.tensor_tensor(L[:], logits_ps[:], over(b["logit_bias"][:], E), ALU.add))
                link(dve.tensor_reduce(c["top"][:], L[:, :, 0:n], AX.X, ALU.max))
                link(dve.tensor_tensor(L[:, :, 0:n], L[:, :, 0:n], last(c["top"][:], n), ALU.subtract))
                if extra:
                    link(dve.tensor_scalar(L[:, :, n:E], L[:, :, n:E], -1.0, None, ALU.mult))
                dve.nop().then_inc(exp_in_ready, 1)
                dve.wait_ge(exp_ready, 1)
                link(dve.tensor_reduce(c["total"][:], f["exps"][:, :, 0:n], AX.X, ALU.add))
                link(dve.reciprocal(c["recip"][:], c["total"][:]))
                link(dve.tensor_tensor(f["probs"][:, :, 0:n], f["exps"][:, :, 0:n], last(c["recip"][:], n), ALU.mult))
                choose(dve, link, rank, over, last, b, f, g, c)
                for r in range(3):
                    ins = dve.tensor_copy(wide[:, :, 32 * r:32 * r + E], f["weight"][:])
                ins.then_inc(wide_ready, 1)
                dve.wait_ge(full_ready, 1)
                link(dve.tensor_copy(part[:], full[:]))
                link(dve.tensor_copy(gates[0:32, :], part[0:32, :]))
                link(dve.tensor_tensor(rest[:], full[:], part[:], ALU.subtract))
                link(dve.tensor_copy(part[:], rest[:]))
                link(dve.tensor_copy(gates[32:64, :], part[32:64, :]))
                link(dve.tensor_tensor(rest[:], rest[:], part[:], ALU.subtract))
                link(dve.tensor_copy(gates[64:96, :], rest[64:96, :]))


def expert_mlps(nc, h, xn, gates, sel, name, units, act_fn, bias, y_bias, extra_down):
    U = len(units)
    with Stage(nc, name + "_mlp") as st:
        s = st.sb("s", [128, 2, TILE])
        prod = st.sb("prod", [128, 2, TILE])
        hid = st.sb("hid", [128, 2, TILE])
        up_ps = st.ps("up_ps", [128, 2, 512])
        gate_ps = st.ps("gate_ps", [128, 2, 512])
        wide_ps = st.ps("wide_ps", [128, 2, 512])
        y_ps = st.ps("y_ps", [HALF, 2, 512])
        up_done = st.sem("up_done")
        side_done = st.sem("side_done")
        s_ready = st.sem("s_ready")
        prod_ready = st.sem("prod_ready")
        hid_ready = st.sem("hid_ready")
        down_done = st.sem("down_done")
        h_ready = st.sem("h_ready")
        gated = [k for k, u in enumerate(units) if u["row"] is not None and u["gate"] is not None]
        prods = len(gated)
        with st.block() as block:
            @block.tensor
            def _(pe):
                def down(t, first, k):
                    u = units[k]
                    pe.wait_ge(hid_ready, t * U + k + 1)
                    if k == 0 and not first:
                        pe.wait_ge(h_ready, 2 * t)
                    if k == 0:
                        for i, w in enumerate(extra_down):
                            for m in range(2):
                                pe.matmul(y_ps[:, m, 0:TILE], w[:, m * HALF:(m + 1) * HALF],
                                          gates[:, ds(t * TILE, TILE)], start=(i == 0), stop=False)
                    for m in range(2):
                        mm = pe.matmul(y_ps[:, m, 0:TILE], u["down"][:, m * HALF:(m + 1) * HALF],
                                       hid[0:u["n"], k % 2, :], start=(k == 0 and not extra_down),
                                       stop=(k == U - 1))
                    mm.then_inc(down_done, 1)

                def step(t, first):
                    x = [xn[:, j, ds(t * TILE, TILE)] for j in range(2)]
                    for k, u in enumerate(units):
                        n = u["n"]
                        for j in range(2):
                            mm = pe.matmul(up_ps[0:n, k % 2, 0:TILE], u["up"][:, j, :], x[j],
                                           start=(j == 0), stop=(j == 1))
                        mm.then_inc(up_done, 1)
                        if u["gate"] is not None:
                            for j in range(2):
                                mm = pe.matmul(gate_ps[0:n, k % 2, 0:TILE], u["gate"][:, j, :], x[j],
                                               start=(j == 0), stop=(j == 1))
                        if u["row"] is not None:
                            mm = pe.matmul(wide_ps[0:n, k % 2, 0:TILE], sel[:, u["row"], 0:n],
                                           gates[:, ds(t * TILE, TILE)], start=True, stop=True)
                        mm.then_inc(side_done, 1)
                        if k:
                            down(t, first, k - 1)
                    down(t, first, U - 1)

                steps(pe, TILES, step)

            @block.scalar
            def _(act):
                def step(t, first):
                    for k, u in enumerate(units):
                        n = u["n"]
                        act.wait_ge(up_done, t * U + k + 1)
                        if not first or k >= 2:
                            act.wait_ge(hid_ready, t * U + k - 1)
                        act.activation(s[0:n, k % 2, :], up_ps[0:n, k % 2, 0:TILE], act_fn,
                                       bias=0.0 if bias is None else bias[0:n, 0, k:k + 1]).then_inc(s_ready, 1)

                steps(act, TILES, step)

            @block.vector
            def _(dve):
                def step(t, first):
                    done = 0
                    for k, u in enumerate(units):
                        n = u["n"]
                        g_bias = 0.0 if bias is None else bias[0:n, 1, k:k + 1]
                        dve.wait_ge(s_ready, t * U + k + 1)
                        dve.wait_ge(side_done, t * U + k + 1)
                        if not first or k >= 2:
                            dve.wait_ge(down_done, t * U + k - 1)
                        if u["gate"] is not None and u["row"] is not None:
                            done += 1
                            dve.scalar_tensor_tensor(out=prod[0:n, k % 2, :], in0=gate_ps[0:n, k % 2, 0:TILE],
                                                     scalar=g_bias, in1=s[0:n, k % 2, :], op0=ALU.add,
                                                     op1=ALU.mult).then_inc(prod_ready, 1)
                            dve.wait_ge(prod_ready, t * prods + done)
                            dve.tensor_tensor(hid[0:n, k % 2, :], prod[0:n, k % 2, :], wide_ps[0:n, k % 2, 0:TILE],
                                              ALU.mult).then_inc(hid_ready, 1)
                        elif u["gate"] is not None:
                            dve.scalar_tensor_tensor(out=hid[0:n, k % 2, :], in0=gate_ps[0:n, k % 2, 0:TILE],
                                                     scalar=g_bias, in1=s[0:n, k % 2, :], op0=ALU.add,
                                                     op1=ALU.mult).then_inc(hid_ready, 1)
                        else:
                            dve.tensor_tensor(hid[0:n, k % 2, :], s[0:n, k % 2, :], wide_ps[0:n, k % 2, 0:TILE],
                                              ALU.mult).then_inc(hid_ready, 1)
                    dve.wait_ge(down_done, (t + 1) * U)
                    for m in range(2):
                        tile = h[:, m, ds(t * TILE, TILE)]
                        dve.scalar_tensor_tensor(out=tile, in0=y_ps[:, m, 0:TILE],
                                                 scalar=0.0 if y_bias is None else y_bias[:, 0, m:m + 1],
                                                 in1=tile, op0=ALU.add, op1=ALU.add).then_inc(h_ready, 1)

                steps(dve, TILES, step)


def split_weights(nc, name, w, rest, parts):
    with Stage(nc, name) as st:
        chain = st.sem("chain")
        with st.block() as block:
            @block.vector
            def _(dve):
                source = w
                for i in range(3):
                    dve.tensor_copy(parts[:, i], source[:]).then_inc(chain, 1)
                    dve.wait_ge(chain, 2 * i + 1)
                    if i < 2:
                        dve.tensor_tensor(rest[:], source[:], parts[:, i], ALU.subtract).then_inc(chain, 1)
                        dve.wait_ge(chain, 2 * i + 2)
                        source = rest


def grouped_experts(nc, dram, h, xn):
    E, HID, BIG = 16, 128, 1e30

    def choose(dve, link, rank, over, last, b, f, g, c):
        link(dve.tensor_tensor(f["scores"][:], f["probs"][:], over(b["score_bias"][:], E), ALU.add))
        pairs = f["scores"][:].rearrange("p c (g i) -> p c g i", i=2)
        link(dve.tensor_tensor(g["group"][:], pairs[:, :, :, 0], pairs[:, :, :, 1], ALU.add))
        rank(g["group_rank"][:], g["group"][:], 8)
        link(dve.tensor_scalar(g["group_mask"][:], g["group_rank"][:], 3.5, None, ALU.is_lt))
        gm = g["group_mask"][:].unsqueeze(3).broadcast_to([RT, CHUNKS, 8, 2])
        link(dve.tensor_tensor(pairs, pairs, gm, ALU.mult))
        link(dve.tensor_scalar(g["group_mask"][:], g["group_mask"][:], BIG, -BIG, ALU.mult, ALU.add))
        link(dve.tensor_tensor(pairs, pairs, gm, ALU.add))
        rank(f["rank"][:], f["scores"][:], E)
        link(dve.tensor_scalar(f["mask"][:], f["rank"][:], 3.5, 2.5, ALU.is_lt, ALU.mult))
        link(dve.tensor_tensor(f["weight"][:], f["probs"][:], f["mask"][:], ALU.mult))

    with Stage(nc, "grouped") as st:
        gates = st.sb("gates", [SPLIT, T], BF16)
        sel = st.sb("sel", [SPLIT, E, 128], BF16)
        up = st.sb("up", [HALF, 2, E + 1, HID])
        gate = st.sb("gate", [HALF, 2, E + 1, HID])
        down = st.sb("down", [HID, E + 1, D])
        bias = st.sb("bias", [HID, 2, E + 1])
        bd = st.sb("bd", [SPLIT, D])
        bd_rest = st.sb("bd_rest", [SPLIT, D])
        bd_parts = st.sb("bd_parts", [SPLIT, 3, D], BF16)
        y_bias = st.sb("y_bias", [HALF, 1, 2])
        router(nc, dram, h, xn, gates, "grouped", E, choose,
               [(up[:], dram["grouped_up"]), (gate[:], dram["grouped_gate"]), (down[:], dram["grouped_down"]),
                (bias[:], dram["grouped_bias"]), (bd[:], dram["grouped_bd"]), (y_bias[:], dram["grouped_cols"]),
                (sel[:], dram["sel"][:, 0:E])])
        split_weights(nc, "grouped_bd_split", bd, bd_rest, bd_parts)
        units = [dict(up=up[:, :, e], gate=gate[:, :, e], down=down[:, e], n=HID, row=e if e < E else None)
                 for e in range(E + 1)]
        expert_mlps(nc, h, xn, gates, sel, "grouped", units, ACT.Silu, bias, y_bias,
                    [bd_parts[:, i] for i in range(3)])


def top2(n):
    def choose(dve, link, rank, over, last, b, f, g, c):
        rank(f["rank"][:, :, 0:n], f["probs"][:, :, 0:n], n)
        link(dve.tensor_scalar(f["mask"][:, :, 0:n], f["rank"][:, :, 0:n], 1.5, None, ALU.is_lt))
        link(dve.tensor_tensor(f["weight"][:, :, 0:n], f["probs"][:, :, 0:n], f["mask"][:, :, 0:n], ALU.mult))
    return choose


def shared_experts(nc, dram, h, xn):
    E, HID, SHARED = 8, 192, 768

    def choose(dve, link, rank, over, last, b, f, g, c):
        top2(E)(dve, link, rank, over, last, b, f, g, c)
        w, alpha = f["weight"][:, :, 0:E], f["weight"][:, :, E]
        link(dve.tensor_reduce(c["total"][:], w, AX.X, ALU.add))
        link(dve.reciprocal(c["recip"][:], c["total"][:]))
        link(dve.tensor_tensor(w, w, last(c["recip"][:], E), ALU.mult))
        link(dve.tensor_scalar(c["u"][:], f["exps"][:, :, E], 1.0, None, ALU.add))
        link(dve.reciprocal(c["v"][:], c["u"][:]))
        link(dve.tensor_copy(alpha, c["v"][:]))
        link(dve.tensor_scalar(c["u"][:], c["v"][:], -1.0, 1.0, ALU.mult, ALU.add))
        link(dve.tensor_tensor(w, w, last(c["u"][:], E), ALU.mult))

    with Stage(nc, "shared") as st:
        gates = st.sb("gates", [SPLIT, T], BF16)
        sel = st.sb("sel", [SPLIT, E + 1, 128], BF16)
        W = E * HID + SHARED
        up = st.sb("up", [HALF, 2, W])
        gate = st.sb("gate", [HALF, 2, W])
        down_r = st.sb("down_r", [HALF, E * 2, D])
        down_s = st.sb("down_s", [128, SHARED // 128, D])
        router(nc, dram, h, xn, gates, "shared", E, choose,
               [(up[:], dram["shared_up"]), (gate[:], dram["shared_gate"]), (down_r[:], dram["shared_down_r"]),
                (down_s[:], dram["shared_down_s"]), (sel[:], dram["sel"][:, 0:E + 1])], extra=1)
        units = [dict(up=up[:, :, k * HALF:(k + 1) * HALF], gate=gate[:, :, k * HALF:(k + 1) * HALF],
                      down=down_r[:, k], n=HALF, row=k // 2) for k in range(2 * E)]
        for k in range(SHARED // 128):
            cols = slice(E * HID + k * 128, E * HID + (k + 1) * 128)
            units.append(dict(up=up[:, :, cols], gate=gate[:, :, cols], down=down_s[:, k], n=128, row=E))
        expert_mlps(nc, h, xn, gates, sel, "shared", units, ACT.Silu, None, None, [])


def gelu_experts(nc, dram, h, xn):
    E, HID = 8, 768
    with Stage(nc, "geluexp") as st:
        gates = st.sb("gates", [SPLIT, T], BF16)
        sel = st.sb("sel", [SPLIT, E, 128], BF16)
        up = st.sb("up", [HALF, 2, E * HID])
        down = st.sb("down", [128, E * HID // 128, D])
        router(nc, dram, h, xn, gates, "geluexp", E, top2(E),
               [(up[:], dram["geluexp_up"]), (down[:], dram["geluexp_down"]), (sel[:], dram["sel"][:, 0:E])])
        units = [dict(up=up[:, :, k * 128:(k + 1) * 128], gate=None, down=down[:, k], n=128,
                      row=k // (HID // 128)) for k in range(E * HID // 128)]
        expert_mlps(nc, h, xn, gates, sel, "geluexp", units, ACT.Gelu_apprx_tanh, None, None, [])


INNER = 2 * D
IC = INNER // 128
STATES = 16
DCONV = 4
RANK = 12
MG = 2
MT = MG * N
MTILES = ITEMS // MG
AHEAD = 2
SILU_AT = 3
FLAGS_AT = 9
COLLECT_AT = 12
SMALL = 1 / 32


def mamba(nc, xn, mout, w, which):
    back = which == "b"
    PREP = [("u", 0), ("u", 1), ("u", 2), ("conv", 0), ("conv", 1), ("conv", 2), ("xd", 0),
            ("dt", 0), ("dt", 1), ("dt", 2), ("z", 0), ("z", 1), ("z", 2)]
    SLOTS = [("conv", 0), ("conv", 1), ("conv", 2), None, ("out", 0), ("xd", 0), ("dt", 0), ("dt", 1),
             ("dt", 2), ("out", 1), ("z", 0), ("z", 1), ("z", 2), ("u", 0), ("u", 1), ("u", 2)]
    PER_STEP = len(PREP) + 2
    LAST = MTILES - 1
    LOADED = 16 * 14

    def slots(first, last):
        count, out = 0, []
        for piece in SLOTS:
            kept = [] if piece is None or (first and piece[0] == "out") or (last and piece[0] != "out") else [piece]
            out.append([(count + i, k, c) for i, (k, c) in enumerate(kept)])
            count += len(kept)
        return out

    def pieces_before(t, first):
        return len(PREP) + IC if first else 2 * len(PREP) + IC + PER_STEP * (t - 1)

    def run(engine, body):
        body(0, 0, True, False)
        with engine.Fori(0, (MTILES - 2) // 2) as i:
            body(2 * i + 1, 1, False, False)
            body(2 * i + 2, 0, False, False)
        body(LAST, LAST % 2, False, True)

    in_w, x_w, dt_w, out_w, cols, A_log = (w[k] for k in ("in_w", "x_w", "dt_w", "out_w", "cols", "A_log"))
    ident, sel, loaded = w["ident"], w["sel"], w["loaded"]
    with Stage(nc, "mamba_" + which) as st:
        A = st.sb("A", [128, IC, STATES])
        diag = st.sb("diag", [128, IC, DCONV, 128])
        upad = st.sb("upad", [128, IC, MG, N + 2 * (DCONV - 1)])
        uc = st.sb("uc", [128, 2, IC, MT])
        sz = st.sb("sz", [128, 2, IC, MT])
        xd = st.sb("xd", [128, MT])
        xd_rest = st.sb("xd_rest", [128, MT])
        xd_part = st.sb("xd_part", [128, MT], BF16)
        zeros = st.sb("zeros", [128, MT])
        parts = st.sb("parts", [128, 2, MT], BF16)
        pre = st.sb("pre", [128, IC, MT])
        soft = st.sb("soft", [128, IC, MT])
        log = st.sb("log", [128, IC, MT])
        series = st.sb("series", [128, IC, MT])
        small = st.sb("small", [128, 2, IC, MT])
        dt = st.sb("dt", [128, 2, IC, MT])
        dtu = st.sb("dtu", [128, 2, IC, MT])
        decay = st.sb("decay", [128, AHEAD + 2, IC, MG, N])
        inject = st.sb("inject", [128, 2, IC, MT])
        state = st.sb("state", [128, 2, IC, MT])
        seen = st.sb("seen", [128, 2, IC, MT])
        yd = st.sb("yd", [128, IC, MT])
        gated = st.sb("gated", [128, IC, MT])
        o = st.sb("o", [HALF, 2, MT])
        work_ps = st.ps("work_ps", [128, 512])
        y_ps = st.ps("y_ps", [128, IC, 512])
        b_ps = st.ps("b_ps", [128, 2, 512])
        c_ps = st.ps("c_ps", [128, 2, 512])
        names = ("zeroed consts a_ready work_done work_read uc_ready sz_ready parts_ready soft_step small_ready "
                 "own_step dt_ready dtu_ready bc_done decay_ready inject_ready scanned seen_ready summed yd_ready "
                 "gated_ready mout_ready").split()
        sem = {n: st.sem(n) for n in names}

        def tile(t):
            return ds(t * MT, MT)

        with st.block() as block:
            @block.gpsimd
            def _(pool):
                pool.memset(upad[:], 0.0).then_inc(sem["zeroed"], 1)
                pool.memset(zeros[:], 0.0).then_inc(sem["zeroed"], 1)
                pool.memset(decay[:], 0.0).then_inc(sem["zeroed"], 1)

                def copy(out, in_):
                    return pool.tensor_scalar(out, in_, 1.0, 0.0, ALU.mult, ALU.add)

                def prepare(t, q, read, fresh):
                    count = [0]

                    def then(ins):
                        count[0] += 1
                        ins.then_inc(sem["own_step"], 1)
                        pool.wait_ge(sem["own_step"], count[0])

                    pool.sem_clear(sem["own_step"])
                    pool.wait_ge(sem["work_read"], read)
                    if not fresh:
                        pool.wait_ge(sem["bc_done"], STATES * (t - 1))
                    then(pool.tensor_tensor(xd_part[:], xd[:], zeros[:], ALU.add))
                    then(copy(parts[0:64, q, :], xd_part[0:64, :]))
                    then(pool.tensor_tensor(xd_rest[:], xd[:], xd_part[:], ALU.subtract))
                    then(copy(xd_part[:], xd_rest[:]))
                    then(copy(parts[64:96, q, :], xd_part[64:96, :]))
                    pool.wait_ge(sem["soft_step"], 4 * t + 2)
                    if not fresh:
                        pool.wait_ge(sem["decay_ready"], STATES * (t - 1))
                        pool.wait_ge(sem["inject_ready"], STATES * (t - 1))
                    then(pool.tensor_tensor(xd_rest[:], xd_rest[:], xd_part[:], ALU.subtract))
                    then(pool.tensor_scalar(series[:], soft[:], -1 / 4, 1 / 3, ALU.mult, ALU.add))
                    copy(parts[96:128, q, :], xd_rest[96:128, :]).then_inc(sem["parts_ready"], 1)
                    pool.wait_ge(sem["parts_ready"], t + 1)
                    then(pool.tensor_tensor(series[:], series[:], soft[:], ALU.mult))
                    then(pool.tensor_scalar(series[:], series[:], 1.0, -1 / 2, ALU.mult, ALU.add))
                    then(pool.tensor_tensor(series[:], series[:], soft[:], ALU.mult))
                    then(pool.tensor_scalar(series[:], series[:], 1.0, 1.0, ALU.mult, ALU.add))
                    then(pool.tensor_tensor(series[:], series[:], soft[:], ALU.mult))
                    pool.wait_ge(sem["small_ready"], 2 * t + 2)
                    then(pool.tensor_tensor(series[:], series[:], small[:, 0], ALU.mult))
                    pool.wait_ge(sem["soft_step"], 4 * t + 3)
                    then(pool.tensor_tensor(log[:], log[:], small[:, 1], ALU.mult))
                    then(pool.tensor_tensor(log[:], log[:], series[:], ALU.add))
                    pool.wait_ge(sem["soft_step"], 4 * t + 4)
                    pool.tensor_tensor(dt[:, q], pre[:], log[:], ALU.add).then_inc(sem["dt_ready"], 1)
                    pool.wait_ge(sem["dt_ready"], t + 1)
                    pool.wait_ge(sem["uc_ready"], t + 1)
                    pool.tensor_tensor(dtu[:, q], dt[:, q], uc[:, q], ALU.mult).then_inc(sem["dtu_ready"], 1)

                pool.wait_ge(sem["zeroed"], 3)
                prepare(0, 0, 7, True)

                def body(t, p, first, last):
                    at = {(k, c): i for slot in slots(first, last) for i, k, c in slot}
                    w0 = pieces_before(t, first)
                    if not last:
                        prepare(t + 1, 1 - p, w0 + at["xd", 0] + 1, first)

                run(pool, body)

            @block.tensor
            def _(pe):
                pe.wait_ge(loaded, LOADED)

                def piece(t, q, kind, c, w, none_before=False):
                    if not none_before:
                        pe.wait_ge(sem["work_read"], w)
                    if kind in ("u", "z"):
                        col = (c if kind == "u" else IC + c) * 128
                        for j in range(2):
                            mm = pe.matmul(work_ps[:, 0:MT], in_w[:, j, col:col + 128], xn[:, j, tile(t)],
                                           start=(j == 0), stop=(j == 1))
                    elif kind == "conv":
                        for k in range(DCONV):
                            shift = 2 * (DCONV - 1) - k if back else k
                            mm = pe.matmul(work_ps[:, 0:MT].rearrange("p (b n) -> p b n", b=MG), diag[:, c, k, :],
                                           upad[:, c, :, shift:shift + N], start=(k == 0), stop=(k == DCONV - 1))
                    elif kind == "xd":
                        pe.wait_ge(sem["uc_ready"], t + 1)
                        for k in range(IC):
                            mm = pe.matmul(work_ps[:, 0:MT], x_w[:, k, :], uc[:, q, k, :], start=(k == 0),
                                           stop=(k == IC - 1))
                    elif kind == "dt":
                        mm = pe.matmul(work_ps[:, 0:MT], dt_w[:, c * 128:(c + 1) * 128], xd[0:RANK, :], start=True,
                                       stop=True)
                    else:
                        pe.wait_ge(sem["gated_ready"], t + 1)
                        for k in range(IC):
                            mm = pe.matmul(work_ps[0:HALF, 0:MT], out_w[:, k, c * HALF:(c + 1) * HALF], gated[:, k, :],
                                           start=(k == 0), stop=(k == IC - 1))
                    mm.then_inc(sem["work_done"], 1)

                def broadcast(n, q):
                    pe.matmul(b_ps[:, n % 2, 0:MT], sel[:, n, :], parts[:, q, :], start=True, stop=True)
                    pe.matmul(c_ps[:, n % 2, 0:MT], sel[:, STATES + n, :], parts[:, q, :], start=True,
                              stop=True).then_inc(sem["bc_done"], 1)

                for i, (kind, c) in enumerate(PREP):
                    if i == IC:
                        pe.wait_ge(sem["consts"], IC * DCONV)
                    piece(0, 0, kind, c, i, i == 0)
                for c in range(IC):
                    piece(1, 1, "u", c, len(PREP) + c)
                pe.wait_ge(sem["parts_ready"], 1)
                for n in range(AHEAD):
                    broadcast(n, 0)

                def body(t, p, first, last):
                    w0 = pieces_before(t, first)

                    for n, slot in enumerate(slots(first, last)):
                        pe.wait_ge(sem["seen_ready"], t * STATES + n + 1)
                        if n + AHEAD < STATES:
                            broadcast(n + AHEAD, p)
                        elif not last:
                            pe.wait_ge(sem["parts_ready"], t + 2)
                            broadcast(n + AHEAD - STATES, 1 - p)

                        def add_seen():
                            for c in range(IC):
                                mm = pe.matmul(y_ps[:, c, 0:MT], ident[:], seen[:, n % 2, c, :], start=(n == 0),
                                               stop=(n == STATES - 1))
                            mm.then_inc(sem["summed"], 1)

                        if n:
                            add_seen()
                        for i, kind, c in slot:
                            if kind == "out":
                                piece(t - 1, 1 - p, kind, c, w0 + i)
                            elif kind == "u":
                                piece((t + 2) % MTILES, p, kind, c, w0 + i)
                            else:
                                piece(t + 1, 1 - p, kind, c, w0 + i)
                        if n == 0:
                            if not first:
                                pe.wait_ge(sem["yd_ready"], IC * t)
                            add_seen()

                run(pe, body)
                for m in range(2):
                    piece(LAST, LAST % 2, "out", m, pieces_before(LAST, False) + 2 + m)

            @block.scalar
            def _(act):
                act.wait_ge(loaded, LOADED)
                act.wait_ge(sem["zeroed"], 1)
                act.activation(A[:], A_log[:], ACT.Exp).then_inc(sem["a_ready"], 1)
                act.wait_ge(sem["a_ready"], 2)

                def piece(t, q, kind, c, w, fresh):
                    def empty(out, func, src=work_ps[:, 0:MT], **kw):
                        act.wait_ge(sem["work_done"], w + 1)
                        act.activation(out, src, func, **kw).then_inc(sem["work_read"], 1)

                    if kind == "u":
                        empty(upad[:, c, :, DCONV - 1:DCONV - 1 + N], ACT.Copy,
                              src=work_ps[:, 0:MT].rearrange("p (b n) -> p b n", b=MG))
                    elif kind == "conv":
                        if c == 0 and not fresh:
                            act.wait_ge(sem["yd_ready"], IC * (t - 1))
                        empty(uc[:, q, c, :], ACT.Identity, bias=cols[:, c, DCONV:DCONV + 1])
                    elif kind == "xd":
                        empty(xd[:], ACT.Copy)
                    elif kind == "dt":
                        empty(pre[:, c, :], ACT.Identity, bias=cols[:, c, DCONV + 1:DCONV + 2])
                        if c == IC - 1:
                            act.wait_ge(sem["work_read"], w + 1)
                            act.activation(soft[:], pre[:], ACT.Abs).then_inc(sem["soft_step"], 1)
                            act.wait_ge(sem["soft_step"], 4 * t + 1)
                            act.activation(soft[:], soft[:], ACT.Exp, scale=-1.0).then_inc(sem["soft_step"], 1)
                            act.wait_ge(sem["soft_step"], 4 * t + 2)
                            act.activation(log[:], soft[:], ACT.Ln, bias=1.0).then_inc(sem["soft_step"], 1)
                            act.activation(pre[:], pre[:], ACT.Relu).then_inc(sem["soft_step"], 1)
                    elif kind == "z":
                        if c == 0 and not fresh:
                            act.wait_ge(sem["gated_ready"], t - 1)
                        empty(sz[:, q, c, :], ACT.Copy)
                    else:
                        empty(o[:, c, :], ACT.Copy, src=work_ps[0:HALF, 0:MT])

                a, b = (0, N - 1) if back else (1, N)

                def decays(n, q):
                    for c in range(IC):
                        ins = act.activation(decay[:, n % (AHEAD + 2), c, :, a:b],
                                             dt[:, q, c, :].rearrange("p (b n) -> p b n", b=MG)[:, :, a:b],
                                             ACT.Exp, scale=A[:, c, n:n + 1])
                    ins.then_inc(sem["decay_ready"], 1)

                def silu_u(q, read):
                    act.wait_ge(sem["work_read"], read)
                    act.activation(uc[:, q], uc[:, q], ACT.Silu).then_inc(sem["uc_ready"], 1)

                for i, (kind, c) in enumerate(PREP):
                    piece(0, 0, kind, c, i, True)
                    if (kind, c) == ("conv", IC - 1):
                        silu_u(0, i + 1)
                for c in range(IC):
                    piece(1, 1, "u", c, len(PREP) + c, True)
                act.wait_ge(sem["zeroed"], 3)
                act.wait_ge(sem["dt_ready"], 1)
                for n in range(AHEAD):
                    decays(n, 0)

                def body(t, p, first, last):
                    w0 = pieces_before(t, first)
                    def silu_z():
                        act.wait_ge(sem["work_read"], w0)
                        act.activation(sz[:, p], sz[:, p], ACT.Silu).then_inc(sem["sz_ready"], 1)

                    for n, slot in enumerate(slots(first, last)):
                        if not first or n >= 2:
                            act.wait_ge(sem["scanned"], t * STATES + n - 1)
                        if n + AHEAD < STATES:
                            decays(n + AHEAD, p)
                        elif not last:
                            act.wait_ge(sem["dt_ready"], t + 2)
                            decays(n + AHEAD - STATES, 1 - p)
                        for i, kind, c in slot:
                            if kind == "out":
                                piece(t - 1, 1 - p, kind, c, w0 + i, False)
                            else:
                                piece(t + 1, 1 - p, kind, c, w0 + i, first)
                        if n == SILU_AT and not last:
                            silu_u(1 - p, w0 + IC)
                            silu_z()
                    if last:
                        silu_z()

                run(act, body)
                act.wait_ge(sem["mout_ready"], LAST)
                for m in range(2):
                    piece(LAST, LAST % 2, "out", m, pieces_before(LAST, False) + 2 + m, False)

            @block.vector
            def _(dve):
                dve.wait_ge(loaded, LOADED)
                for c in range(IC):
                    for k in range(DCONV):
                        dve.tensor_scalar(diag[:, c, k, :], ident[:], cols[:, c, k:k + 1], None,
                                          ALU.mult).then_inc(sem["consts"], 1)
                dve.wait_ge(sem["a_ready"], 1)
                dve.tensor_scalar(A[:], A[:], -1.0, None, ALU.mult).then_inc(sem["a_ready"], 1)

                def flags(t, fresh):
                    dve.wait_ge(sem["soft_step"], 4 * t + 2)
                    if not fresh:
                        dve.wait_ge(sem["dt_ready"], t)
                    dve.tensor_scalar(small[:, 0], soft[:], SMALL, None, ALU.is_lt).then_inc(sem["small_ready"], 1)
                    dve.tensor_scalar(small[:, 1], soft[:], SMALL, None, ALU.is_ge).then_inc(sem["small_ready"], 1)

                def gate(t, p):
                    dve.wait_ge(sem["summed"], STATES * (t + 1))
                    for c in range(IC):
                        dve.scalar_tensor_tensor(out=yd[:, c, :], in0=uc[:, p, c, :], scalar=cols[:, c, DCONV + 2:DCONV + 3],
                                                 in1=y_ps[:, c, 0:MT], op0=ALU.mult,
                                                 op1=ALU.add).then_inc(sem["yd_ready"], 1)
                    dve.wait_ge(sem["yd_ready"], IC * (t + 1))
                    dve.wait_ge(sem["sz_ready"], t + 1)
                    dve.tensor_tensor(gated[:], yd[:], sz[:, p], ALU.mult).then_inc(sem["gated_ready"], 1)

                def collect(t, read):
                    dve.wait_ge(sem["work_read"], read)
                    base = mout if back else xn
                    dve.tensor_tensor(mout[:, :, tile(t)], o[:], base[:, :, tile(t)],
                                      ALU.add).then_inc(sem["mout_ready"], 1)

                flags(0, True)

                def body(t, p, first, last):
                    s0 = t * STATES

                    def inject_(n):
                        dve.wait_ge(sem["bc_done"], s0 + n + 1)
                        dve.tensor_tensor(inject[:, n % 2], dtu[:, p],
                                          b_ps[:, n % 2, 0:MT].unsqueeze(1).broadcast_to([128, IC, MT]),
                                          ALU.mult).then_inc(sem["inject_ready"], 1)

                    dve.wait_ge(sem["dtu_ready"], t + 1)
                    inject_(0)
                    for n in range(STATES):
                        flat = [state[:, n % 2].rearrange("p c n -> p (c n)"),
                                decay[:, n % (AHEAD + 2)].rearrange("p c b n -> p (c b n)"),
                                inject[:, n % 2].rearrange("p c n -> p (c n)")]
                        if back:
                            flat = [x[:, ::-1] for x in flat]
                        dve.wait_ge(sem["decay_ready"], s0 + n + 1)
                        dve.wait_ge(sem["inject_ready"], s0 + n + 1)
                        dve.tensor_tensor_scan(flat[0], flat[1], flat[2], 0.0, ALU.mult,
                                               ALU.add).then_inc(sem["scanned"], 1)
                        if n + 1 < STATES:
                            inject_(n + 1)
                        dve.wait_ge(sem["scanned"], s0 + n + 1)
                        if not first or n >= 2:
                            dve.wait_ge(sem["summed"], s0 + n - 1)
                        dve.tensor_tensor(seen[:, n % 2], state[:, n % 2],
                                          c_ps[:, n % 2, 0:MT].unsqueeze(1).broadcast_to([128, IC, MT]),
                                          ALU.mult).then_inc(sem["seen_ready"], 1)
                        if n == 0 and not first:
                            gate(t - 1, 1 - p)
                        if n == FLAGS_AT and not last:
                            flags(t + 1, False)
                        if n == COLLECT_AT and not first:
                            at = {(k, c): i for slot in slots(first, last) for i, k, c in slot}
                            collect(t - 1, pieces_before(t, first) + at["out", 1] + 1)

                run(dve, body)
                gate(LAST, LAST % 2)
                collect(LAST, pieces_before(LAST, False) + 4)


def add_scaled(nc, h, normed, cols, loaded, count):
    with Stage(nc, "addscaled") as st:
        scaled = st.sb("scaled", [HALF, 2, T])
        scaled_ready = st.sem("scaled_ready")
        with st.block() as block:
            @block.scalar
            def _(act):
                act.wait_ge(loaded, count)
                for t in range(0, TILES, 2):
                    for m in range(2):
                        part = slice(t * TILE, (t + 2) * TILE)
                        act.activation(scaled[:, m, part], normed[:, m, part], ACT.Identity, bias=cols[:, 1, m:m + 1],
                                       scale=cols[:, 0, m:m + 1]).then_inc(scaled_ready, 1)

            @block.vector
            def _(dve):
                for t in range(0, TILES, 2):
                    part = slice(t * TILE, (t + 2) * TILE)
                    dve.wait_ge(scaled_ready, t + 2)
                    dve.tensor_tensor(h[:, :, part], h[:, :, part], scaled[:, :, part], ALU.add)


def bidirectional_mamba(nc, dram, h, xn):
    with Stage(nc, "mamba") as st:
        mout = st.sb("mout", [HALF, 2, T])
        ident = st.sb("ident", [128, 128])
        sel = st.sb("sel", [128, 2 * STATES, 128], BF16)
        norm_cols = st.sb("norm_cols", [HALF, 2, 2])
        loaded = st.sem("loaded")
        weights = {}
        for which in ("f", "b"):
            weights[which] = dict(
                in_w=st.sb("in_w_" + which, [HALF, 2, 2 * INNER]),
                x_w=st.sb("x_w_" + which, [128, IC, 128]),
                dt_w=st.sb("dt_w_" + which, [RANK, INNER]),
                out_w=st.sb("out_w_" + which, [128, IC, D]),
                cols=st.sb("cols_" + which, [128, IC, DCONV + 3]),
                A_log=st.sb("A_log_" + which, [128, IC, STATES]))

        def loads(sp):
            for which, w in weights.items():
                for k, name in (("in_w", "in"), ("x_w", "x"), ("dt_w", "dt"), ("out_w", "out"), ("cols", "cols"),
                                ("A_log", "A_log")):
                    sp.dma_start(w[k][:], dram[f"mamba_{which}_{name}"]).then_inc(loaded, 16)
            sp.dma_start(ident[:], dram["ident"]).then_inc(loaded, 16)
            sp.dma_start(sel[:], dram["state_sel"]).then_inc(loaded, 16)
            sp.dma_start(norm_cols[:], dram["mamba_norm_cols"]).then_inc(norm_loaded, 16)

        norm_loaded = st.sem("gain_loaded")
        layer_norm(nc, dram, h, xn, "mamba_norm", loads)
        for which in ("f", "b"):
            mamba(nc, xn, mout, dict(weights[which], ident=ident, sel=sel, loaded=loaded), which)
        layer_norm(nc, dram, mout, xn, "mamba_out_norm", epsilon=1e-12)
        add_scaled(nc, h, xn, norm_cols, norm_loaded, 16)


def quantised_mlp(nc, dram, h, xn):
    HID = 768
    K = HID // 128
    LOW, HIGH = -8.0, 7.0
    ROUND = 1.5 * 2.0 ** 23
    with Stage(nc, "quant") as st:
        w1 = st.sb("w1", [HALF, 2, HID])
        w2 = st.sb("w2", [128, K, D])
        step_w1 = st.sb("step_w1", [HALF, HID])
        step_w2 = st.sb("step_w2", [128, D])
        inv_w1 = st.sb("inv_w1", [HALF, HID])
        inv_w2 = st.sb("inv_w2", [128, D])
        w1q = st.sb("w1q", [HALF, 2, HID], BF16)
        w2q = st.sb("w2q", [128, K, D], BF16)
        step_a1 = st.sb("step_a1", [HALF, 2])
        step_a2 = st.sb("step_a2", [HALF, HID // HALF])
        hid_cols = st.sb("hid_cols", [128, 2, K])
        out_cols = st.sb("out_cols", [HALF, 2, 2])
        ones = st.sb("ones", [HALF, 128])
        step_a = st.sb("step_a", [128, 2])
        inv_a = st.sb("inv_a", [128, 2])
        scale1 = st.sb("scale1", [128, K])
        scale2 = st.sb("scale2", [HALF, 2])
        xs = st.sb("xs", [HALF, 2, T])
        xq = st.sb("xq", [HALF, 2, T], BF16)
        g = st.sb("g", [128, K, TILE])
        gs = st.sb("gs", [128, K, TILE])
        gq = st.sb("gq", [128, K, TILE], BF16)
        y = st.sb("y", [HALF, 2, TILE])
        loaded = st.sem("loaded")

        def loads(sp):
            for dst, src in ((step_a1, "quant_a1"), (step_a2, "quant_a2"), (w1, "quant_w1"), (w2, "quant_w2"),
                             (hid_cols, "quant_hid"), (out_cols, "quant_out")):
                sp.dma_start(dst[:], dram[src]).then_inc(loaded, 16)
            sp.dma_start(step_w1[:], dram["quant_step_w1"].broadcast_to([HALF, HID])).then_inc(loaded, 16)
            sp.dma_start(step_w2[:], dram["quant_step_w2"].broadcast_to([128, D])).then_inc(loaded, 16)

        layer_norm(nc, dram, h, xn, "quant_norm", loads)
        mean_ps = st.ps("mean_ps", [128, 2])
        up_ps = st.ps("up_ps", [128, 2, 512])
        y_ps = st.ps("y_ps", [HALF, 2, 512])
        ones_ready = st.sem("ones_ready")
        mean_done = st.sem("mean_done")
        chain = st.sem("chain")
        ready = st.sem("ready")
        up_done = st.sem("up_done")
        g_ready = st.sem("g_ready")
        gq_step = st.sem("gq_step")
        gq_ready = st.sem("gq_ready")
        down_done = st.sem("down_done")
        y_ready = st.sem("y_ready")
        h_ready = st.sem("h_ready")
        with st.block() as block:
            @block.gpsimd
            def _(pool):
                pool.memset(ones[:], 1.0).then_inc(ones_ready, 1)

            @block.tensor
            def _(pe):
                pe.wait_ge(loaded, 128)
                pe.wait_ge(ones_ready, 1)
                for i, steps_in in enumerate((step_a1, step_a2)):
                    n = steps_in[:].shape[1]
                    for j in range(n):
                        mm = pe.matmul(mean_ps[:, i:i + 1], ones[:], steps_in[:, j:j + 1],
                                       start=(j == 0), stop=(j == n - 1))
                mm.then_inc(mean_done, 1)
                pe.wait_ge(ready, 1)

                def step(t, first):
                    for k in range(K):
                        if not first or k >= 2:
                            pe.wait_ge(g_ready, t * K + k - 1)
                        for j in range(2):
                            mm = pe.matmul(up_ps[:, k % 2, 0:TILE], w1q[:, j, k * 128:(k + 1) * 128],
                                           xq[:, j, ds(t * TILE, TILE)], start=(j == 0), stop=(j == 1))
                        mm.then_inc(up_done, 1)
                    pe.wait_ge(gq_ready, t + 1)
                    if not first:
                        pe.wait_ge(y_ready, 2 * t)
                    for m in range(2):
                        for k in range(K):
                            mm = pe.matmul(y_ps[:, m, 0:TILE], w2q[:, k, m * HALF:(m + 1) * HALF], gq[:, k, :],
                                           start=(k == 0), stop=(k == K - 1))
                    mm.then_inc(down_done, 1)

                steps(pe, TILES, step)

            @block.scalar
            def _(act):
                act.wait_ge(ready, 1)

                def step(t, first):
                    if not first:
                        act.wait_ge(gq_step, 3 * t)
                    for k in range(K):
                        act.wait_ge(up_done, t * K + k + 1)
                        act.activation(g[:, k, :], up_ps[:, k % 2, 0:TILE], ACT.Gelu, bias=hid_cols[:, 1, k:k + 1],
                                       scale=scale1[:, k:k + 1]).then_inc(g_ready, 1)
                    act.wait_ge(down_done, t + 1)
                    if not first:
                        act.wait_ge(h_ready, t)
                    for m in range(2):
                        act.activation(y[:, m, :], y_ps[:, m, 0:TILE], ACT.Identity, bias=out_cols[:, 1, m:m + 1],
                                       scale=scale2[:, m:m + 1]).then_inc(y_ready, 1)

                steps(act, TILES, step)

            @block.vector
            def _(dve):
                count = [0]

                def link(ins):
                    count[0] += 1
                    ins.then_inc(chain, 1)
                    dve.wait_ge(chain, count[0])

                def quantise(out, scaled):
                    link(dve.tensor_scalar(scaled, scaled, HIGH, LOW, ALU.min, ALU.max))
                    link(dve.tensor_scalar(out, scaled, ROUND, ROUND, ALU.add, ALU.subtract))

                dve.wait_ge(loaded, 128)
                link(dve.reciprocal(inv_w1[:], step_w1[:]))
                link(dve.reciprocal(inv_w2[:], step_w2[:]))
                link(dve.tensor_tensor(w1[:], w1[:], inv_w1[:].unsqueeze(1).broadcast_to([HALF, 2, HID]), ALU.mult))
                quantise(w1q[:], w1[:])
                link(dve.tensor_tensor(w2[:], w2[:], inv_w2[:].unsqueeze(1).broadcast_to([128, K, D]), ALU.mult))
                quantise(w2q[:], w2[:])
                dve.wait_ge(mean_done, 1)
                link(dve.tensor_scalar(step_a[:, 0:1], mean_ps[:, 0:1], 1.0 / D, None, ALU.mult))
                link(dve.tensor_scalar(step_a[:, 1:2], mean_ps[:, 1:2], 1.0 / HID, None, ALU.mult))
                link(dve.reciprocal(inv_a[:], step_a[:]))
                link(dve.tensor_scalar(scale1[:], hid_cols[:, 0], step_a[:, 0:1], None, ALU.mult))
                link(dve.tensor_scalar(scale2[:], out_cols[:, 0], step_a[0:HALF, 1:2], None, ALU.mult))
                link(dve.tensor_scalar(xs[:], xn[:], inv_a[0:HALF, 0:1], None, ALU.mult))
                quantise(xq[:], xs[:])
                dve.nop().then_inc(ready, 1)

                def step(t, first):
                    dve.wait_ge(g_ready, (t + 1) * K)
                    dve.tensor_scalar(g[:], g[:], 10.0, -10.0, ALU.min, ALU.max).then_inc(gq_step, 1)
                    dve.wait_ge(gq_step, 3 * t + 1)
                    dve.tensor_scalar(gs[:], g[:], inv_a[:, 1:2], HIGH, ALU.mult, ALU.min).then_inc(gq_step, 1)
                    dve.wait_ge(gq_step, 3 * t + 2)
                    dve.tensor_scalar(gs[:], gs[:], LOW, ROUND, ALU.max, ALU.add).then_inc(gq_step, 1)
                    dve.wait_ge(gq_step, 3 * t + 3)
                    if not first:
                        dve.wait_ge(down_done, t)
                    dve.tensor_scalar(gq[:], gs[:], ROUND, None, ALU.subtract).then_inc(gq_ready, 1)
                    dve.wait_ge(y_ready, 2 * t + 2)
                    tile = h[:, :, ds(t * TILE, TILE)]
                    dve.tensor_tensor(tile, tile, y[:], ALU.add).then_inc(h_ready, 1)

                steps(dve, TILES, step)




def group_attention(nc, dram, h, xn):
    GP = 49
    SCALE = D ** -0.5
    P = 65
    with Stage(nc, "groupattn") as st:
        w_qkv = st.sb("w_qkv", [HALF, 2, 3 * D])
        w_proj = st.sb("w_proj", [HALF, 2, D])
        w_gp = st.sb("w_gp", [HALF, 2, GP])
        cols = st.sb("cols", [HALF, 3, 2])
        v_bias = st.sb("v_bias", [P, D])
        ident = st.sb("ident", [P, P])
        a = st.sb("a", [P, 4])
        x = st.sb("x", [HALF, PAIR, 2, N])
        q = st.sb("q", [HALF, PAIR, 2, N])
        k = st.sb("k", [HALF, PAIR, 2, N])
        v = st.sb("v", [P, PAIR, 2, D])
        g_in = st.sb("g_in", [P, PAIR, 2, GP])
        g_exp = st.sb("g_exp", [P, PAIR, 2, GP])
        g_top = st.sb("g_top", [P, PAIR, 2])
        g_sum = st.sb("g_sum", [P, PAIR, 2])
        g_inv = st.sb("g_inv", [P, PAIR, 2])
        gw = st.sb("gw", [P, PAIR, 2, GP])
        gwt = st.sb("gwt", [GP, PAIR, N])
        top = st.sb("top", [P, PAIR, 2])
        bias = st.sb("bias", [P, PAIR, 2])
        total = st.sb("total", [P, PAIR, 2])
        inv = st.sb("inv", [P, PAIR, 2])
        e = st.sb("e", [P, PAIR, 2, N])
        mix = st.sb("mix", [P, PAIR, 2, N])
        wt = st.sb("wt", [P, PAIR, 2, N])
        wtt = st.sb("wtt", [P, PAIR, 2, N])
        heads = st.sb("heads", [HALF, PAIR, 2, N])
        loaded = st.sem("loaded")

        def loads(sp):
            for dst, src in ((w_qkv, "groupattn_qkv"), (w_proj, "groupattn_proj"), (w_gp, "groupattn_gp"),
                             (cols, "groupattn_cols")):
                sp.dma_start(dst[:], dram[src]).then_inc(loaded, 16)
            sp.dma_start(v_bias[:], dram["groupattn_v_bias"].broadcast_to([P, D])).then_inc(loaded, 16)
            sp.dma_start(a[:, 0:1], dram["groupattn_alpha"].broadcast_to([P, 1])).then_inc(loaded, 16)
            sp.dma_start(ident[:], dram["ident"][0:P, 0:P]).then_inc(loaded, 16)

        layer_norm(nc, dram, h, xn, "groupattn_norm", loads)
        banks = [[st.ps(f"bank_{b}{i}", [128, 512]) for b in "abcd"] for i in range(PAIR)]

        def view(b, p, n):
            return [banks[i][b][0:p, 0:2 * n].rearrange("p (a b) -> p a b", a=2) for i in range(PAIR)]

        q_ps, s_ps, wtt_ps = view(0, HALF, N), view(0, P, N), view(0, P, N)
        k_ps, group_ps, o_ps = view(1, HALF, N), view(1, P, N), view(1, HALF, N)
        v_ps, out_ps = view(2, P, D), view(2, HALF, N)
        g_ps, gwt_ps = view(3, P, GP), [banks[i][3][0:GP, 0:N] for i in range(PAIR)]
        names = ("x_ready qkv_done q_ready k_ready v_ready g_done g_top g_in g_exp g_inv gw_ready "
                 "gwt_done gwt_ready s_done top_ready bias_ready e_ready inv_ready group_done mix_ready wt_ready "
                 "wtt_done wtt_ready out_done heads_ready proj_done h_ready a_step").split()
        sem = {n: st.sem(n) for n in names}
        with st.block() as block:
            @block.gpsimd
            def _(pool):
                def step(s, first):
                    for i in range(PAIR):
                        if not first:
                            pool.wait_ge(sem["qkv_done"], 2 * s + i - 1)
                        pool.tensor_copy(x[:, i], xn[:, :, ds((2 * s + i) * N, N)]).then_inc(sem["x_ready"], 1)

                steps(pool, PAIRS, step)

            @block.tensor
            def _(pe):
                pe.wait_ge(loaded, 112)

                def step(s, first):
                    for i in range(PAIR):
                        b = 2 * s + i
                        pe.wait_ge(sem["x_ready"], b + 1)
                        if not first:
                            pe.wait_ge(sem["h_ready"], 2 * (b - 1))
                        for ps, w0 in ((q_ps, 0), (k_ps, D)):
                            for m in range(2):
                                for j in range(2):
                                    pe.matmul(ps[i][:, m, :], w_qkv[:, j, w0 + m * HALF:w0 + (m + 1) * HALF],
                                              x[:, i, j, :], start=(j == 0), stop=(j == 1))
                        for c, (c0, n) in enumerate(QCUT):
                            for j in range(2):
                                mm = pe.matmul(v_ps[i][:, c, :], x[:, i, j, c0:c0 + n], w_qkv[:, j, 2 * D:],
                                               start=(j == 0), stop=(j == 1))
                        mm.then_inc(sem["qkv_done"], 1)
                    for i in range(PAIR):
                        b = 2 * s + i
                        pe.wait_ge(sem["q_ready"], 2 * b + 2)
                        for c, (c0, n) in enumerate(QCUT):
                            for j in range(2):
                                mm = pe.matmul(g_ps[i][:, c, :], q[:, i, j, c0:c0 + n], w_gp[:, j, :],
                                               start=(j == 0), stop=(j == 1))
                        mm.then_inc(sem["g_done"], 1)
                        pe.wait_ge(sem["k_ready"], 2 * b + 2)
                        for c, (c0, n) in enumerate(QCUT):
                            for j in range(2):
                                mm = pe.matmul(s_ps[i][:, c, :], q[:, i, j, c0:c0 + n], k[:, i, j, :],
                                               start=(j == 0), stop=(j == 1))
                        mm.then_inc(sem["s_done"], 1)
                    for i in range(PAIR):
                        b = 2 * s + i
                        pe.wait_ge(loaded, 112)
                        pe.wait_ge(sem["gw_ready"], b + 1)
                        for c, (c0, n) in enumerate(QCUT):
                            mm = pe.transpose(gwt_ps[i][:, c0:c0 + n], gw[:, i, c, :], ident[:])
                        mm.then_inc(sem["gwt_done"], 1)
                    for i in range(PAIR):
                        b = 2 * s + i
                        pe.wait_ge(sem["gwt_ready"], b + 1)
                        for c, (c0, n) in enumerate(QCUT):
                            mm = pe.matmul(group_ps[i][:, c, :], gwt[:, i, c0:c0 + n], gwt[:, i], start=True, stop=True)
                        mm.then_inc(sem["group_done"], 1)
                    for i in range(PAIR):
                        b = 2 * s + i
                        pe.wait_ge(loaded, 112)
                        pe.wait_ge(sem["wt_ready"], 2 * b + 2)
                        for c, (c0, n) in enumerate(QCUT):
                            for d, (d0, l) in enumerate(QCUT):
                                mm = pe.transpose(wtt_ps[i][:, d, c0:c0 + n], wt[:, i, c, d0:d0 + l], ident[:])
                        mm.then_inc(sem["wtt_done"], 1)
                    for i in range(PAIR):
                        b = 2 * s + i
                        pe.wait_ge(sem["v_ready"], b + 1)
                        pe.wait_ge(sem["wtt_ready"], b + 1)
                        for m in range(2):
                            for d, l in enumerate(KEYS):
                                mm = pe.matmul(out_ps[i][:, m, :], v[0:l, i, d, m * HALF:(m + 1) * HALF],
                                               wtt[0:l, i, d, :], start=(d == 0), stop=(d == 1))
                        mm.then_inc(sem["out_done"], 1)
                    for i in range(PAIR):
                        b = 2 * s + i
                        pe.wait_ge(sem["heads_ready"], b + 1)
                        for m in range(2):
                            for j in range(2):
                                mm = pe.matmul(o_ps[i][:, m, :], w_proj[:, j, m * HALF:(m + 1) * HALF],
                                               heads[:, i, j, :], start=(j == 0), stop=(j == 1))
                        mm.then_inc(sem["proj_done"], 1)

                steps(pe, PAIRS, step)

            @block.scalar
            def _(act):
                act.wait_ge(loaded, 112)
                act.activation(a[:, 1:2], a[:, 0:1], ACT.Exp, scale=-1.0).then_inc(sem["a_step"], 1)

                def step(s, first):
                    for i in range(PAIR):
                        b = 2 * s + i
                        act.wait_ge(sem["qkv_done"], b + 1)
                        for m in range(2):
                            act.activation(q[:, i, m, :], q_ps[i][:, m, :], ACT.Identity,
                                           bias=cols[:, 0, m:m + 1]).then_inc(sem["q_ready"], 1)
                    for i in range(PAIR):
                        b = 2 * s + i
                        act.wait_ge(sem["g_in"], b + 1)
                        for c in range(2):
                            act.activation(g_exp[:, i, c, :], g_in[:, i, c, :], ACT.Exp,
                                           accum_out=g_sum[:, i, c:c + 1]).then_inc(sem["g_exp"], 1)
                    for i in range(PAIR):
                        b = 2 * s + i
                        act.wait_ge(sem["bias_ready"], b + 1)
                        for c in range(2):
                            act.activation(e[:, i, c, :], s_ps[i][:, c, :], ACT.Exp, bias=bias[:, i, c:c + 1],
                                           scale=SCALE, accum_out=total[:, i, c:c + 1]).then_inc(sem["e_ready"], 1)
                        act.wait_ge(sem["gwt_done"], b + 1)
                        act.activation(gwt[:, i], gwt_ps[i], ACT.Copy).then_inc(sem["gwt_ready"], 1)
                    for i in range(PAIR):
                        b = 2 * s + i
                        act.wait_ge(sem["wtt_done"], b + 1)
                        act.activation(wtt[:, i], wtt_ps[i], ACT.Copy).then_inc(sem["wtt_ready"], 1)
                    for i in range(PAIR):
                        b = 2 * s + i
                        act.wait_ge(sem["out_done"], b + 1)
                        act.activation(heads[:, i], out_ps[i], ACT.Copy).then_inc(sem["heads_ready"], 1)

                steps(act, PAIRS, step)

            @block.vector
            def _(dve):
                dve.wait_ge(sem["a_step"], 1)
                dve.tensor_scalar(a[:, 3:4], a[:, 1:2], 1.0, None, ALU.add).then_inc(sem["a_step"], 1)
                dve.wait_ge(sem["a_step"], 2)
                dve.reciprocal(a[:, 2:3], a[:, 3:4]).then_inc(sem["a_step"], 1)
                dve.wait_ge(sem["a_step"], 3)
                dve.tensor_scalar(a[:, 3:4], a[:, 2:3], -1.0, 1.0, ALU.mult, ALU.add).then_inc(sem["a_step"], 1)
                dve.wait_ge(sem["a_step"], 4)

                def wide(ap, n):
                    return ap.unsqueeze(2).broadcast_to([P, 2, n])

                def step(s, first):
                    for i in range(PAIR):
                        b = 2 * s + i
                        dve.wait_ge(sem["qkv_done"], b + 1)
                        for m in range(2):
                            dve.tensor_scalar(k[:, i, m, :], k_ps[i][:, m, :], cols[:, 1, m:m + 1], None,
                                              ALU.add).then_inc(sem["k_ready"], 1)
                        dve.tensor_tensor(v[:, i], v_ps[i], v_bias[:].unsqueeze(1).broadcast_to([P, 2, D]),
                                          ALU.add).then_inc(sem["v_ready"], 1)
                    for i in range(PAIR):
                        b = 2 * s + i
                        dve.wait_ge(sem["g_done"], b + 1)
                        dve.tensor_reduce(g_top[:, i], g_ps[i], AX.X, ALU.max).then_inc(sem["g_top"], 1)
                        dve.wait_ge(sem["g_top"], b + 1)
                        dve.tensor_tensor(g_in[:, i], g_ps[i], wide(g_top[:, i], GP),
                                          ALU.subtract).then_inc(sem["g_in"], 1)
                    for i in range(PAIR):
                        b = 2 * s + i
                        dve.wait_ge(sem["s_done"], b + 1)
                        dve.tensor_reduce(top[:, i], s_ps[i], AX.X, ALU.max).then_inc(sem["top_ready"], 1)
                        dve.wait_ge(sem["top_ready"], b + 1)
                        dve.tensor_scalar(bias[:, i], top[:, i], -SCALE, None, ALU.mult).then_inc(sem["bias_ready"], 1)
                    for i in range(PAIR):
                        b = 2 * s + i
                        dve.wait_ge(sem["g_exp"], 2 * b + 2)
                        dve.reciprocal(g_inv[:, i], g_sum[:, i]).then_inc(sem["g_inv"], 1)
                        dve.wait_ge(sem["g_inv"], b + 1)
                        dve.tensor_tensor(gw[:, i], g_exp[:, i], wide(g_inv[:, i], GP),
                                          ALU.mult).then_inc(sem["gw_ready"], 1)
                    for i in range(PAIR):
                        b = 2 * s + i
                        dve.wait_ge(sem["e_ready"], 2 * b + 2)
                        dve.reciprocal(inv[:, i], total[:, i]).then_inc(sem["inv_ready"], 1)
                        dve.wait_ge(sem["group_done"], b + 1)
                        dve.tensor_scalar(mix[:, i], group_ps[i], a[:, 3:4], a[:, 2:3], ALU.mult,
                                          ALU.add).then_inc(sem["mix_ready"], 1)
                        dve.wait_ge(sem["inv_ready"], b + 1)
                        dve.wait_ge(sem["mix_ready"], b + 1)
                        for c in range(2):
                            dve.scalar_tensor_tensor(out=wt[:, i, c, :], in0=e[:, i, c, :], scalar=inv[:, i, c:c + 1],
                                                     in1=mix[:, i, c, :], op0=ALU.mult,
                                                     op1=ALU.mult).then_inc(sem["wt_ready"], 1)
                    for i in range(PAIR):
                        b = 2 * s + i
                        dve.wait_ge(sem["proj_done"], b + 1)
                        for m in range(2):
                            cols_b = h[:, m, ds(b * N, N)]
                            dve.scalar_tensor_tensor(out=cols_b, in0=o_ps[i][:, m, :], scalar=cols[:, 2, m:m + 1],
                                                     in1=cols_b, op0=ALU.add, op1=ALU.add).then_inc(sem["h_ready"], 1)

                steps(dve, PAIRS, step)


def collaborative_attention(nc, dram, h, xn):
    H, HEAD = 12, 16
    SCALE = HEAD ** -0.5
    R = (HALF + H, HALF)
    HG = 6
    ROUNDS = [(c, g) for c in range(2) for g in range(2)]
    LAST = ITEMS - 1
    with Stage(nc, "collab") as st:
        w_q = st.sb("w_q", [HALF, 2, D])
        w_k = st.sb("w_k", [HALF, 2, D + H])
        w_v = st.sb("w_v", [HALF, 2, D])
        w_proj = st.sb("w_proj", [HALF, 2, D])
        mixing = st.sb("mixing", [R[0], 2, H])
        cols = st.sb("cols", [HALF, 1, 2])
        v_bias = st.sb("v_bias", [65, D])
        ident = st.sb("ident", [65, 65])
        q_all = st.sb("q_all", [HALF, 2, T])
        k_all = st.sb("k_all", [R[0], 2, T])
        x = st.sb("x", [HALF, 2, N])
        q = st.sb("q", [R[0], 2, 2, N])
        keys = st.sb("keys", [R[0], 2, 2, H, N])
        v1 = st.sb("v1", [65, 2, 2, H, HEAD + 1])
        top = st.sb("top", [65, 2, HG])
        e = st.sb("e", [65, 2, HG, N])
        et = st.sb("et", [65, 2, HG, 65])
        inv = st.sb("inv", [65, 2, H])
        att = st.sb("att", [65, 2, H, HEAD])
        heads = st.sb("heads", [HALF, 2, N])
        loaded = st.sem("loaded")

        def loads(sp):
            for dst, src in ((w_q, "collab_q"), (w_k, "collab_k"), (w_v, "collab_v"), (w_proj, "collab_proj"),
                             (mixing, "collab_mixing"), (cols, "collab_cols")):
                sp.dma_start(dst[:], dram[src]).then_inc(loaded, 16)
            sp.dma_start(v_bias[:], dram["collab_v_bias"].broadcast_to([65, D])).then_inc(loaded, 16)
            sp.dma_start(ident[:], dram["ident"][0:65, 0:65]).then_inc(loaded, 16)

        layer_norm(nc, dram, h, xn, "collab_norm", loads)
        with Stage(nc, "collabproj") as pst:
            q_ps = pst.ps("q_ps", [HALF, 2, 512])
            k_ps = pst.ps("k_ps", [R[0], 2, 512])
            projected = pst.sem("projected")
            q_copied = pst.sem("q_copied")
            k_copied = pst.sem("k_copied")
            with pst.block() as block:
                @block.tensor
                def _(pe):
                    pe.wait_ge(loaded, 128)

                    def step(t, first):
                        if not first:
                            pe.wait_ge(q_copied, t)
                        for m in range(2):
                            for j in range(2):
                                pe.matmul(q_ps[:, m, 0:TILE], w_q[:, j, m * HALF:(m + 1) * HALF],
                                          xn[:, j, ds(t * TILE, TILE)], start=(j == 0), stop=(j == 1))
                        if not first:
                            pe.wait_ge(k_copied, 2 * t)
                        for m in range(2):
                            w = [w_k[:, j, 0:R[0]] if m == 0 else w_k[:, j, R[0]:] for j in range(2)]
                            for j in range(2):
                                mm = pe.matmul(k_ps[0:R[m], m, 0:TILE], w[j], xn[:, j, ds(t * TILE, TILE)],
                                               start=(j == 0), stop=(j == 1))
                        mm.then_inc(projected, 1)

                    steps(pe, TILES, step)

                @block.scalar
                def _(act):
                    def step(t, first):
                        act.wait_ge(projected, t + 1)
                        act.activation(q_all[:, :, ds(t * TILE, TILE)], q_ps[:, :, 0:TILE],
                                       ACT.Copy).then_inc(q_copied, 1)

                    steps(act, TILES, step)

                @block.vector
                def _(dve):
                    def step(t, first):
                        dve.wait_ge(projected, t + 1)
                        for m in range(2):
                            dve.tensor_copy(k_all[0:R[m], m, ds(t * TILE, TILE)],
                                            k_ps[0:R[m], m, 0:TILE]).then_inc(k_copied, 1)

                    steps(dve, TILES, step)

        s_ps = [st.ps(f"s_ps{i}", [65, 2, 512]) for i in range(2)]
        et_ps = st.ps("et_ps", [65, 2, 512])
        av_bank = st.ps("av_bank", [65, 512])
        bank_b = st.ps("bank_b", [128, 512])
        av_ps = av_bank[:, 0:2 * H * (HEAD + 1)].rearrange("p (c h d) -> p c h d", c=2, h=H)
        heads_ps = bank_b[0:HALF, 0:2 * N].rearrange("p (a b) -> p a b", a=2)
        o_ps = heads_ps
        v_ps = bank_b[0:65, 0:2 * D].rearrange("p (c f) -> p c f", c=2)
        names = ("ones_ready q_ready x_ready keys_ready v_done v_ready s_done top_ready shifted e_ready "
                 "et_done et_ready av_done inv_ready att_ready heads_done heads_ready proj_done h_ready").split()
        sem = {n: st.sem(n) for n in names}

        def run(engine, body):
            body(0, 0, True, False)
            with engine.Fori(0, (ITEMS - 2) // 2) as i:
                body(2 * i + 1, 1, False, False)
                body(2 * i + 2, 0, False, False)
            body(LAST, LAST % 2, False, True)

        with st.block() as block:
            @block.gpsimd
            def _(pool):
                pool.memset(v1[:, :, :, :, HEAD:], 1.0).then_inc(sem["ones_ready"], 1)
                pool.memset(q[HALF:R[0], :, 0, :], 1.0).then_inc(sem["ones_ready"], 1)
                pool.tensor_copy(q[0:HALF, 0], q_all[:, :, 0:N]).then_inc(sem["q_ready"], 1)
                pool.tensor_copy(x[:], xn[:, :, 0:N]).then_inc(sem["x_ready"], 1)

                def body(b, p, first, last):
                    if last:
                        return
                    if not first:
                        pool.wait_ge(sem["s_done"], 4 * b)
                    pool.wait_ge(sem["v_done"], b + 1)
                    pool.tensor_copy(q[0:HALF, 1 - p], q_all[:, :, ds((b + 1) * N, N)]).then_inc(sem["q_ready"], 1)
                    pool.tensor_copy(x[:], xn[:, :, ds((b + 1) * N, N)]).then_inc(sem["x_ready"], 1)

                run(pool, body)

            @block.tensor
            def _(pe):
                def scores(r, i, p):
                    c, g = ROUNDS[i]
                    c0, n = QCUT[c]
                    for u in range(2):
                        for j in range(2):
                            f = g * HG + 3 * u
                            mm = pe.matmul(s_ps[i % 2][0:n, u, 0:3 * N], q[0:R[j], p, j, c0:c0 + n],
                                           keys[0:R[j], p, j, f:f + 3, :].rearrange("p h n -> p (h n)"),
                                           start=(j == 0), stop=(j == 1))
                    mm.then_inc(sem["s_done"], 1)

                def values(b):
                    pe.wait_ge(sem["x_ready"], b + 1)
                    for c, (c0, n) in enumerate(CUT):
                        for j in range(2):
                            mm = pe.matmul(v_ps[0:n, c, :], x[:, j, c0:c0 + n], w_v[:, j, :],
                                           start=(j == 0), stop=(j == 1))
                    mm.then_inc(sem["v_done"], 1)

                def turn_heads(b):
                    pe.wait_ge(loaded, 128)
                    pe.wait_ge(sem["att_ready"], b + 1)
                    for c, (c0, n) in enumerate(QCUT):
                        flat = att[0:n, c].rearrange("p h d -> p (h d)")
                        for m in range(2):
                            mm = pe.transpose(heads_ps[:, m, c0:c0 + n], flat[:, m * HALF:(m + 1) * HALF],
                                              ident[0:n, 0:n])
                    mm.then_inc(sem["heads_done"], 1)

                def project(b):
                    pe.wait_ge(sem["heads_ready"], b + 1)
                    for m in range(2):
                        for j in range(2):
                            mm = pe.matmul(o_ps[:, m, :], w_proj[:, j, m * HALF:(m + 1) * HALF], heads[:, j, :],
                                           start=(j == 0), stop=(j == 1))
                    mm.then_inc(sem["proj_done"], 1)

                pe.wait_ge(sem["ones_ready"], 2)
                values(0)
                pe.wait_ge(sem["q_ready"], 1)
                pe.wait_ge(sem["keys_ready"], 2)
                scores(0, 0, 0)
                scores(1, 1, 0)

                def body(b, p, first, last):
                    for i, (c, g) in enumerate(ROUNDS):
                        r = 4 * b + i
                        n = QCUT[c][1]
                        pe.wait_ge(sem["e_ready"], r + 1)
                        for f in range(HG):
                            for d, (d0, l) in enumerate(CUT):
                                mm = pe.transpose(et_ps[0:l, d, f * 65:f * 65 + n], e[0:n, i % 2, f, d0:d0 + l],
                                                  ident[0:n, 0:n])
                        mm.then_inc(sem["et_done"], 1)
                        if i + 2 < 4:
                            scores(r + 2, i + 2, p)
                        elif not last:
                            if i == 2:
                                pe.wait_ge(sem["q_ready"], b + 2)
                                pe.wait_ge(sem["keys_ready"], 2 * b + 4)
                            scores(r + 2, i - 2, 1 - p)
                        if i == 0:
                            pe.wait_ge(sem["v_ready"], 2 * b + 2)
                            if not first:
                                pe.wait_ge(sem["att_ready"], b)
                        pe.wait_ge(sem["et_ready"], 2 * r + 2)
                        for f in range(HG):
                            for d, (d0, l) in enumerate(CUT):
                                mm = pe.matmul(av_ps[0:n, c, g * HG + f, :], et[0:l, d, f, 0:n],
                                               v1[0:l, p, d, g * HG + f, :], start=(d == 0), stop=(d == 1))
                        mm.then_inc(sem["av_done"], 1)
                        if i == 0 and not first:
                            turn_heads(b - 1)
                        if i == 1 and not first:
                            project(b - 1)
                        if i == 2 and not last:
                            if not first:
                                pe.wait_ge(sem["h_ready"], 2 * b)
                            values(b + 1)

                run(pe, body)
                turn_heads(LAST)
                project(LAST)

            @block.scalar
            def _(act):
                def copy_heads(b):
                    act.wait_ge(sem["heads_done"], b + 1)
                    act.activation(heads[:], heads_ps, ACT.Copy).then_inc(sem["heads_ready"], 1)

                def body(b, p, first, last):
                    for i, (c, g) in enumerate(ROUNDS):
                        r = 4 * b + i
                        n = QCUT[c][1]
                        act.wait_ge(sem["shifted"], r + 1)
                        act.activation(e[0:n, i % 2], e[0:n, i % 2], ACT.Exp, scale=SCALE).then_inc(sem["e_ready"], 1)
                        if i == 1 and not first:
                            copy_heads(b - 1)
                        act.wait_ge(sem["et_done"], r + 1)
                        if not first or i:
                            act.wait_ge(sem["av_done"], r)
                        for d, (d0, l) in enumerate(CUT):
                            act.activation(et[0:l, d, :, 0:n],
                                           et_ps[0:l, d, 0:HG * 65].rearrange("p (f n) -> p f n", f=HG)[:, :, 0:n],
                                           ACT.Copy).then_inc(sem["et_ready"], 1)

                run(act, body)
                copy_heads(LAST)

            @block.vector
            def _(dve):
                def make_keys(b, p, j):
                    dve.tensor_tensor(keys[0:R[j], p, j],
                                      k_all[0:R[j], j, ds(b * N, N)].unsqueeze(1).broadcast_to([R[j], H, N]),
                                      mixing[0:R[j], j, :].unsqueeze(2).broadcast_to([R[j], H, N]),
                                      ALU.mult).then_inc(sem["keys_ready"], 1)

                def copy_values(b, p):
                    dve.wait_ge(sem["v_done"], b + 1)
                    for c, (c0, n) in enumerate(CUT):
                        dve.tensor_tensor(v1[0:n, p, c, :, 0:HEAD], v_ps[0:n, c, :].rearrange("p (h d) -> p h d", h=H),
                                          v_bias[0:n, :].rearrange("p (h d) -> p h d", h=H),
                                          ALU.add).then_inc(sem["v_ready"], 1)

                def normalise(b):
                    dve.wait_ge(sem["av_done"], 4 * b + 4)
                    dve.reciprocal(inv[:], av_ps[:, :, :, HEAD]).then_inc(sem["inv_ready"], 1)
                    dve.wait_ge(sem["inv_ready"], b + 1)
                    dve.tensor_tensor(att[:], av_ps[:, :, :, 0:HEAD],
                                      inv[:].unsqueeze(3).broadcast_to([65, 2, H, HEAD]),
                                      ALU.mult).then_inc(sem["att_ready"], 1)

                def add_output(b):
                    dve.wait_ge(sem["proj_done"], b + 1)
                    for m in range(2):
                        cols_b = h[:, m, ds(b * N, N)]
                        dve.scalar_tensor_tensor(out=cols_b, in0=o_ps[:, m, :], scalar=cols[:, 0, m:m + 1],
                                                 in1=cols_b, op0=ALU.add, op1=ALU.add).then_inc(sem["h_ready"], 1)

                dve.wait_ge(sem["ones_ready"], 2)
                for j in range(2):
                    make_keys(0, 0, j)
                copy_values(0, 0)

                def body(b, p, first, last):
                    for i, (c, g) in enumerate(ROUNDS):
                        r = 4 * b + i
                        n = QCUT[c][1]
                        dve.wait_ge(sem["s_done"], r + 1)
                        s = s_ps[i % 2][0:n, :, 0:3 * N].rearrange("p i (h m) -> p i h m", h=3)
                        t = top[0:n, i % 2].rearrange("p (i h) -> p i h", i=2)
                        dve.tensor_reduce(t, s, AX.X, ALU.max).then_inc(sem["top_ready"], 1)
                        dve.wait_ge(sem["top_ready"], r + 1)
                        if not first or i >= 2:
                            dve.wait_ge(sem["et_done"], r - 1)
                        dve.tensor_tensor(e[0:n, i % 2].rearrange("p (i h) m -> p i h m", i=2), s,
                                          t.unsqueeze(3).broadcast_to([n, 2, 3, N]),
                                          ALU.subtract).then_inc(sem["shifted"], 1)
                        if i == 0 and not first:
                            normalise(b - 1)
                        if i < 2 and not last:
                            make_keys(b + 1, 1 - p, i)
                        if i == 2 and not first:
                            add_output(b - 1)
                        if i == 3 and not last:
                            copy_values(b + 1, 1 - p)

                run(dve, body)
                normalise(LAST)
                add_output(LAST)


def store_output(nc, h, out):
    with Stage(nc, "store") as st:
        stored = st.sem("stored")
        with st.block() as block:
            @block.sync
            def _(sp):
                for j in range(2):
                    sp.dma_start(out[:, j, :], h[:, j, :]).then_inc(stored, 16)
                sp.wait_ge(stored, 32)


STAGES = [embed_tokens, linear_attention, grouped_experts, bidirectional_mamba, quantised_mlp, group_attention, shared_experts,
          collaborative_attention, gelu_experts]


def build(nc, dram, out):
    Stage.used = []
    with nc.sbuf_tensor("h", [HALF, 2, T], F32) as h, nc.sbuf_tensor("xn", [HALF, 2, T], F32) as xn:
        for stage in STAGES:
            stage(nc, dram, h, xn)
        store_output(nc, h, out)


def lay_out(i):
    import numpy as np
    a = {k: np.asarray(v) for k, v in i.items()}

    def halves(w):
        return np.ascontiguousarray(w.reshape((2, HALF) + w.shape[1:]).swapaxes(0, 1))

    def columns(*vs):
        return np.stack([halves(v.reshape(D)) for v in vs], axis=1)

    d = {}
    d["x"] = halves(a["x"][..., 0].transpose(2, 0, 1))
    d["embed_taps"] = halves(a["L0_tok_dw_w"].reshape(D, 7))
    d["embed_point_w"] = halves(a["L0_tok_pw_w"].T)
    d["embed_cols"] = columns(a["L0_tok_pw_b"], a["L0_tok_ln_g"], a["L0_tok_ln_b"], a["cls_tok"])
    d["linattn_qkv"] = halves(a["L0_attn_qkv_w"].T)
    d["linattn_proj"] = halves(a["L0_attn_proj_w"].T)
    d["linattn_cols"] = columns(a["L0_attn_proj_b"])
    head = np.arange(HALF) // 16
    mask = (head[:, None] == head[None, :]).astype(np.float32)
    d["head_mask"] = np.stack([mask, mask], axis=1)
    d["ident"] = np.eye(128, dtype=np.float32)
    sel = np.zeros((SPLIT, 16, 128), np.float32)
    for e in range(16):
        sel[e::32, e] = 1.0
    d["sel"] = sel.astype(mybir.dt.np(BF16))

    def per_expert(w):
        return halves(w.transpose(1, 0, 2).reshape(D, -1))

    d["grouped_router_w"] = halves(a["L0_ffn_gate_w"])
    d["grouped_router_b"] = np.stack([a["L0_ffn_gate_b"], a["L0_ffn_bias"]])
    for mine, theirs in (("up", "Wu"), ("gate", "Wg")):
        d["grouped_" + mine] = halves(np.concatenate([a["L0_ffn_" + theirs], a["L0_ffn_s" + theirs][None]])
                                      .transpose(1, 0, 2))
    d["grouped_down"] = np.concatenate([a["L0_ffn_Wd"], a["L0_ffn_sWd"][None]]).transpose(1, 0, 2)
    d["grouped_bias"] = np.stack([np.concatenate([a["L0_ffn_" + b], a["L0_ffn_s" + b][None]]).T
                                  for b in ("bu", "bg")], axis=1)
    bd = np.zeros((3, 32, D), np.float32)
    bd[:, 0:16] = a["L0_ffn_bd"]
    d["grouped_bd"] = bd.reshape(SPLIT, D)
    d["grouped_cols"] = columns(a["L0_ffn_sbd"])
    d["shared_router_w"] = halves(np.concatenate([a["L2_ffn_router_w"], a["L2_ffn_sg_w"]], axis=1))
    zeros8 = np.zeros(8, np.float32)
    d["shared_router_b"] = np.stack([np.concatenate([zeros8, a["L2_ffn_sg_b"]]), np.zeros(9, np.float32)])
    for mine, theirs in (("up", "gate"), ("gate", "up")):
        d["shared_" + mine] = np.concatenate([per_expert(a["L2_ffn_w_" + theirs]),
                                              halves(a["L2_ffn_ws_" + theirs])], axis=2)
    d["shared_down_r"] = a["L2_ffn_w_down"].reshape(16, HALF, D).transpose(1, 0, 2)
    d["shared_down_s"] = a["L2_ffn_ws_down"].reshape(6, 128, D).transpose(1, 0, 2)
    d["geluexp_router_w"] = halves(a["L3_ffn_router_w"].T)
    d["geluexp_router_b"] = np.zeros((2, 8), np.float32)
    d["geluexp_up"] = per_expert(a["L3_ffn_w1"])
    d["geluexp_down"] = a["L3_ffn_w2"].reshape(48, 128, D).transpose(1, 0, 2)
    def chunks(w):
        return np.ascontiguousarray(w.reshape((IC, 128) + w.shape[1:]).swapaxes(0, 1))

    for which in ("f", "b"):
        m = {k: a[f"L1_attn_{which}_{k}"] for k in ("in_w", "conv_w", "conv_b", "xproj_w", "dt_w", "dt_b",
                                                    "A_log", "D_skip", "out_w")}
        p = f"mamba_{which}_"
        d[p + "in"] = halves(m["in_w"].T)
        xw = np.zeros((INNER, 128), np.float32)
        xw[:, 0:RANK] = m["xproj_w"][0:RANK].T
        for r in (32, 64, 96):
            xw[:, r:r + 2 * STATES] = m["xproj_w"][RANK:].T
        d[p + "x"] = chunks(xw)
        d[p + "dt"] = m["dt_w"].T
        d[p + "out"] = chunks(m["out_w"].T)
        d[p + "cols"] = chunks(np.concatenate([m["conv_w"], m["conv_b"][:, None], m["dt_b"][:, None],
                                               m["D_skip"][:, None]], axis=1))
        d[p + "A_log"] = chunks(m["A_log"])
    d["mamba_norm_cols"] = columns(a["L1_attn_ln_g"], a["L1_attn_ln_b"])
    state_sel = np.zeros((128, 2 * STATES, 128), np.float32)
    for e in range(2 * STATES):
        state_sel[32 + e::32, e] = 1.0
    d["state_sel"] = state_sel.astype(mybir.dt.np(BF16))
    d["quant_w1"] = halves(a["L1_ffn_w1"].T)
    d["quant_w2"] = a["L1_ffn_w2"].T.reshape(6, 128, D).transpose(1, 0, 2)
    d["quant_step_w1"] = a["L1_ffn_alpha_w1"][None]
    d["quant_step_w2"] = a["L1_ffn_alpha_w2"][None]
    d["quant_a1"] = a["L1_ffn_alpha_a1"].reshape(HALF, 2)
    d["quant_a2"] = a["L1_ffn_alpha_a2"].reshape(HALF, 8)
    d["quant_hid"] = np.stack([a["L1_ffn_alpha_w1"].reshape(6, 128).T, a["L1_ffn_b1"].reshape(6, 128).T], axis=1)
    d["quant_out"] = columns(a["L1_ffn_alpha_w2"], a["L1_ffn_b2"])
    d["groupattn_qkv"] = halves(a["L2_attn_W_qkv"])
    d["groupattn_proj"] = halves(a["L2_attn_W_proj"])
    d["groupattn_gp"] = halves(a["L2_attn_W_gp"])
    b_qkv = a["L2_attn_b_qkv"]
    d["groupattn_cols"] = columns(b_qkv[0:D], b_qkv[D:2 * D], a["L2_attn_b_proj"])
    d["groupattn_v_bias"] = b_qkv[None, 2 * D:]
    d["groupattn_alpha"] = a["L2_attn_alpha"][None]
    d["collab_q"] = halves(a["L3_attn_Wq"].T)
    wk = a["L3_attn_Wk"].T
    d["collab_k"] = halves(np.concatenate([wk[:, 0:HALF], a["L3_attn_Wcb"].T, wk[:, HALF:]], axis=1))
    d["collab_v"] = halves(a["L3_attn_Wv"].T)
    d["collab_proj"] = halves(a["L3_attn_Wproj"].T)
    mixing = np.zeros((HALF + 12, 2, 12), np.float32)
    mixing[HALF:, 0] = np.eye(12, dtype=np.float32)
    mixing[0:HALF] = halves(a["L3_attn_Wmix"].T)
    d["collab_mixing"] = mixing
    d["collab_cols"] = columns(a["L3_attn_bproj"])
    d["collab_v_bias"] = a["L3_attn_bv"][None]
    return d


def kernel(**inputs):
    import numpy as np
    import concourse.bacc as bacc
    from concourse.bass_utils import run_bass_kernel_spmd

    nc = bacc.Bacc("TRN2", target_bir_lowering=False, num_devices=1)
    arrays = {f"in_{k}": np.ascontiguousarray(v) for k, v in lay_out(inputs).items()}
    dram = {k[3:]: nc.dram_tensor(k, v.shape, mybir.dt.from_np(v.dtype), kind="ExternalInput").ap()
            for k, v in arrays.items()}
    out = nc.dram_tensor("out_h", (HALF, 2, T), F32, kind="ExternalOutput").ap()
    build(nc, dram, out)
    r = run_bass_kernel_spmd(nc, [arrays], core_ids=[0])
    got = r.results[0]["out_h"]
    return np.ascontiguousarray(got.reshape(HALF, 2, ITEMS, N).transpose(2, 3, 1, 0).reshape(ITEMS, N, D))
```
